# Optimizing a Trainium2 kernel written in Bass

```python
import numpy as np
import jax
import jax.numpy as jnp

def _softmax(x, axis=-1):
    return jax.nn.softmax(x, axis=axis)

def _gelu(x):
    return jax.nn.gelu(x, approximate=True)

def _silu(x):
    return jax.nn.silu(x)

def _sigmoid(x):
    return jax.nn.sigmoid(x)

def _layernorm(x, axis=-1, eps=1e-05):
    m = jnp.mean(x, axis=axis, keepdims=True)
    v = jnp.var(x, axis=axis, keepdims=True)
    return (x - m) / jnp.sqrt(v + eps)

def _scatter_add(tgt, idx, src, axis=0):
    return tgt.at[idx].add(src)

def _segment_sum(src, seg, n):
    return jax.ops.segment_sum(src, seg, n)
kernel_name = 'mk_gnn_resnorm_d4_gnn_r32_e615af'

def setup_inputs(seed: int=0):
    np.random.seed(seed)
    _w = jnp.asarray

    def _rec_inputs():
        import jax
        import jax.numpy as jnp
        _gk = jax.random.key(seed)
        x = -0.000202 + 1 * jax.random.normal(jax.random.fold_in(_gk, 1), (3125, 64), jnp.float32)
        _s = jax.random.randint(jax.random.fold_in(_gk, 2), (25000,), 0, 3125, jnp.int32)
        _d = jax.random.randint(jax.random.fold_in(_gk, 3), (25000,), 0, 3125, jnp.int32)
        _loop = jnp.arange(3125, dtype=jnp.int32)
        src = jnp.concatenate([_s, _d, _loop])
        dst = jnp.concatenate([_d, _s, _loop])
        _o = jnp.argsort(dst, stable=True)
        src = src[_o]
        dst = dst[_o]
        edge_attr_32 = 0.000196303 + 1.00016 * jax.random.normal(jax.random.fold_in(_gk, 12), (53125, 32), jnp.float32)
        edge_type_3 = jax.random.randint(jax.random.fold_in(_gk, 14), (53125,), 0, 3, jnp.int32)
        edge_weight = jax.random.uniform(jax.random.fold_in(_gk, 15), (53125,), jnp.float32, 0.0, 0.999998)
        return (x, src, dst, edge_attr_32, edge_type_3, edge_weight)
    x, src, dst, edge_attr_32, edge_type_3, edge_weight = _rec_inputs()

    def _L0_gnn_setup():
        import jax, jax.numpy as jnp
        import numpy as np
        N_NODES = 3125
        N_EDGES = 50000
        C = 64
        L = 3
        BN_EPS = 1e-05

        def _bn(h, g, b):
            return g * (h * (1.0 / np.sqrt(1.0 + BN_EPS))) + b
        key = jax.random.key(seed)
        ks = jax.random.split(key, 16)
        x = jax.random.normal(ks[0], (N_NODES, C), dtype=jnp.float32)
        edge_index = jax.random.randint(ks[1], (2, N_EDGES), 0, N_NODES, dtype=jnp.int32)
        s = 1.0 / np.sqrt(C)
        W1 = jax.random.normal(ks[2], (L, C, C), dtype=jnp.float32) * s
        b1 = jnp.zeros((L, C), dtype=jnp.float32)
        g1 = jnp.ones((L, C), dtype=jnp.float32)
        be1 = jnp.zeros((L, C), dtype=jnp.float32)
        W2 = jax.random.normal(ks[3], (L, C, C), dtype=jnp.float32) * s
        b2 = jnp.zeros((L, C), dtype=jnp.float32)
        g2 = jnp.ones((L, C), dtype=jnp.float32)
        be2 = jnp.zeros((L, C), dtype=jnp.float32)
        bn_g = jnp.ones((L, C), dtype=jnp.float32)
        bn_be = jnp.zeros((L, C), dtype=jnp.float32)
        eps = jnp.zeros((L,), dtype=jnp.float32)
        return {'x': x, 'edge_index': edge_index, 'eps': eps, 'W1': W1, 'b1': b1, 'g1': g1, 'be1': be1, 'W2': W2, 'b2': b2, 'g2': g2, 'be2': be2, 'bn_g': bn_g, 'bn_be': bn_be}
    _L0_gnn_all = _L0_gnn_setup()
    _L0_gnn_in = {k: v for k, v in _L0_gnn_all.items() if k in ('eps', 'W1', 'b1', 'g1', 'be1', 'W2', 'b2', 'g2', 'be2', 'bn_g', 'bn_be')}
    del _L0_gnn_all

    def _L1_gnn_setup():
        import jax, jax.numpy as jnp
        import numpy as np
        N_NODES = 50000
        N_EDGES = 25000
        F_X = 64
        F_E = 32
        H = 128
        F_OUT = 64

        def scatter_mean(vals, idx, num_segments):
            s = jax.ops.segment_sum(vals, idx, num_segments=num_segments)
            cnt = jax.ops.segment_sum(jnp.ones((vals.shape[0],), dtype=vals.dtype), idx, num_segments=num_segments)
            return s / jnp.maximum(cnt, 1.0)[:, None]
        key = jax.random.key(seed)
        ks = jax.random.split(key, 12)
        x = jax.random.normal(ks[0], (N_NODES, F_X), dtype=jnp.float32)
        edge_index = jax.random.randint(ks[1], (2, N_EDGES), 0, N_NODES)
        edge_attr = jax.random.normal(ks[2], (N_EDGES, F_E), dtype=jnp.float32)

        def lin(k, fan_in, fan_out):
            kw, kb = jax.random.split(k)
            bound = 1.0 / np.sqrt(fan_in)
            W = jax.random.uniform(kw, (fan_in, fan_out), minval=-bound, maxval=bound, dtype=jnp.float32)
            b = jax.random.uniform(kb, (fan_out,), minval=-bound, maxval=bound, dtype=jnp.float32)
            return (W, b)
        W1, b1 = lin(ks[3], F_X + F_E, H)
        W2, b2 = lin(ks[4], H, F_OUT)
        W3, b3 = lin(ks[5], F_X + F_OUT, H)
        W4, b4 = lin(ks[6], H, F_OUT)
        return {'x': x, 'edge_index': edge_index, 'edge_attr': edge_attr, 'W1': W1, 'b1': b1, 'W2': W2, 'b2': b2, 'W3': W3, 'b3': b3, 'W4': W4, 'b4': b4}
    _L1_gnn_all = _L1_gnn_setup()
    _L1_gnn_in = {k: v for k, v in _L1_gnn_all.items() if k in ('W1', 'b1', 'W2', 'b2', 'W3', 'b3', 'W4', 'b4')}
    del _L1_gnn_all

    def _L2_gnn_setup():
        import jax, jax.numpy as jnp
        import numpy as np
        N, E, D_IN, HEAD, HD = (3125, 50000, 64, 4, 16)
        REL = 64
        NEG_SLOPE = 0.01
        key = jax.random.key(seed)
        ks = jax.random.split(key, 8)
        init = lambda k, shape, fan: jax.random.normal(k, shape, jnp.float32) / np.sqrt(fan)
        return {'x': jax.random.normal(ks[0], (N, D_IN), jnp.float32), 'src': jax.random.randint(ks[1], (E,), 0, N), 'dst': jax.random.randint(ks[2], (E,), 0, N), 'Wl': init(ks[3], (D_IN, HEAD * HD), D_IN), 'bl': jnp.zeros((HEAD * HD,), jnp.float32), 'Wa': init(ks[4], (2 * HD, 1), 2 * HD), 'ba': jnp.zeros((1,), jnp.float32), 'Wd': init(ks[5], (D_IN, REL), D_IN), 'bd': jnp.zeros((REL,), jnp.float32), 'Wf': init(ks[6], (3 * REL, 1), 3 * REL), 'bf': jnp.zeros((1,), jnp.float32)}
    _L2_gnn_all = _L2_gnn_setup()
    _L2_gnn_in = {k: v for k, v in _L2_gnn_all.items() if k in ('Wl', 'bl', 'Wa', 'ba', 'Wd', 'bd', 'Wf', 'bf')}
    del _L2_gnn_all

    def _L3_gnn_setup():
        import jax, jax.numpy as jnp
        import numpy as np
        N_NODES = 50000
        N_EDGES = 25000
        D = 64
        N_REL = 3
        BN_EPS = 1e-05
        key = jax.random.key(seed)
        ks = jax.random.split(key, 6)
        h = jax.random.normal(ks[0], (N_NODES, D), dtype=jnp.float32)
        src = jax.random.randint(ks[1], (N_EDGES,), 0, N_NODES, dtype=jnp.int32)
        dst = jax.random.randint(ks[2], (N_EDGES,), 0, N_NODES, dtype=jnp.int32)
        rel_type = jax.random.randint(ks[3], (N_EDGES,), 0, N_REL, dtype=jnp.int32)
        norm = jax.random.uniform(ks[4], (N_EDGES,), dtype=jnp.float32)
        weight = jax.random.normal(ks[5], (N_REL, D, D), dtype=jnp.float32) * (2.0 / D) ** 0.5
        gamma = jnp.ones((D,), dtype=jnp.float32)
        beta = jnp.zeros((D,), dtype=jnp.float32)
        return {'h': h, 'src': src, 'dst': dst, 'rel_type': rel_type, 'norm': norm, 'weight': weight, 'gamma': gamma, 'beta': beta}
    _L3_gnn_all = _L3_gnn_setup()
    _L3_gnn_in = {k: v for k, v in _L3_gnn_all.items() if k in ('weight', 'gamma', 'beta')}
    del _L3_gnn_all
    return {'x': x, 'src': src, 'dst': dst, 'edge_attr_32': edge_attr_32, 'edge_type_3': edge_type_3, 'edge_weight': edge_weight, 'L0_gnn_eps': _L0_gnn_in['eps'], 'L0_gnn_W1': _L0_gnn_in['W1'], 'L0_gnn_b1': _L0_gnn_in['b1'], 'L0_gnn_g1': _L0_gnn_in['g1'], 'L0_gnn_be1': _L0_gnn_in['be1'], 'L0_gnn_W2': _L0_gnn_in['W2'], 'L0_gnn_b2': _L0_gnn_in['b2'], 'L0_gnn_g2': _L0_gnn_in['g2'], 'L0_gnn_be2': _L0_gnn_in['be2'], 'L0_gnn_bn_g': _L0_gnn_in['bn_g'], 'L0_gnn_bn_be': _L0_gnn_in['bn_be'], 'L1_gnn_W1': _L1_gnn_in['W1'], 'L1_gnn_b1': _L1_gnn_in['b1'], 'L1_gnn_W2': _L1_gnn_in['W2'], 'L1_gnn_b2': _L1_gnn_in['b2'], 'L1_gnn_W3': _L1_gnn_in['W3'], 'L1_gnn_b3': _L1_gnn_in['b3'], 'L1_gnn_W4': _L1_gnn_in['W4'], 'L1_gnn_b4': _L1_gnn_in['b4'], 'L2_gnn_Wl': _L2_gnn_in['Wl'], 'L2_gnn_bl': _L2_gnn_in['bl'], 'L2_gnn_Wa': _L2_gnn_in['Wa'], 'L2_gnn_ba': _L2_gnn_in['ba'], 'L2_gnn_Wd': _L2_gnn_in['Wd'], 'L2_gnn_bd': _L2_gnn_in['bd'], 'L2_gnn_Wf': _L2_gnn_in['Wf'], 'L2_gnn_bf': _L2_gnn_in['bf'], 'L3_gnn_weight': _L3_gnn_in['weight'], 'L3_gnn_gamma': _L3_gnn_in['gamma'], 'L3_gnn_beta': _L3_gnn_in['beta']}

def reference(x, src, dst, edge_attr_32, edge_type_3, edge_weight, L0_gnn_eps, L0_gnn_W1, L0_gnn_b1, L0_gnn_g1, L0_gnn_be1, L0_gnn_W2, L0_gnn_b2, L0_gnn_g2, L0_gnn_be2, L0_gnn_bn_g, L0_gnn_bn_be, L1_gnn_W1, L1_gnn_b1, L1_gnn_W2, L1_gnn_b2, L1_gnn_W3, L1_gnn_b3, L1_gnn_W4, L1_gnn_b4, L2_gnn_Wl, L2_gnn_bl, L2_gnn_Wa, L2_gnn_ba, L2_gnn_Wd, L2_gnn_bd, L2_gnn_Wf, L2_gnn_bf, L3_gnn_weight, L3_gnn_gamma, L3_gnn_beta):
    import jax
    import jax.numpy as jnp

    def _L0_gnn_ref(x, edge_index, eps, W1, b1, g1, be1, W2, b2, g2, be2, bn_g, bn_be):
        import jax, jax.numpy as jnp
        import numpy as np
        N_NODES = 3125
        N_EDGES = 50000
        C = 64
        L = 3
        BN_EPS = 1e-05

        def _bn(h, g, b):
            return g * (h * (1.0 / np.sqrt(1.0 + BN_EPS))) + b
        src, dst = (edge_index[0], edge_index[1])
        for i in range(L):
            agg = jax.ops.segment_sum(x[src], dst, num_segments=N_NODES)
            h = (1.0 + eps[i]) * x + agg
            h = jax.nn.relu(_bn(h @ W1[i] + b1[i], g1[i], be1[i]))
            h = jax.nn.relu(_bn(h @ W2[i] + b2[i], g2[i], be2[i]))
            x = _bn(h, bn_g[i], bn_be[i])
            if i < L - 1:
                x = jax.nn.relu(x)
        return x

    def _L1_gnn_ref(x, edge_index, edge_attr, W1, b1, W2, b2, W3, b3, W4, b4):
        import jax, jax.numpy as jnp
        import numpy as np
        N_NODES = 50000
        N_EDGES = 25000
        F_X = 64
        F_E = 32
        H = 128
        F_OUT = 64

        def scatter_mean(vals, idx, num_segments):
            s = jax.ops.segment_sum(vals, idx, num_segments=num_segments)
            cnt = jax.ops.segment_sum(jnp.ones((vals.shape[0],), dtype=vals.dtype), idx, num_segments=num_segments)
            return s / jnp.maximum(cnt, 1.0)[:, None]
        row, col = (edge_index[0], edge_index[1])
        h = jnp.concatenate([x[row], edge_attr], axis=1)
        h = jax.nn.relu(h @ W1 + b1)
        h = h @ W2 + b2
        agg = scatter_mean(h, col, x.shape[0])
        g = jnp.concatenate([x, agg], axis=1)
        g = jax.nn.relu(g @ W3 + b3)
        return g @ W4 + b4

    def _L2_gnn_ref(x, src, dst, Wl, bl, Wa, ba, Wd, bd, Wf, bf):
        import jax, jax.numpy as jnp
        import numpy as np
        N, E, D_IN, HEAD, HD = (3125, 50000, 64, 4, 16)
        REL = 64
        NEG_SLOPE = 0.01
        hx = x @ Wd + bd
        hs, hd_ = (hx[src], hx[dst])
        e = jnp.tanh(jnp.concatenate([hs, hd_, hs - hd_], axis=-1) @ Wf + bf)
        sign = jnp.sign(e)
        h = (x @ Wl + bl).reshape(N, HEAD, HD)
        sf = sign[:, :, None] * h[src]
        z = jnp.concatenate([sf, h[dst]], axis=-1)
        alpha = jax.nn.leaky_relu(jnp.squeeze(z @ Wa + ba, -1), NEG_SLOPE)
        amax = jax.ops.segment_max(alpha, dst, num_segments=N)
        amax = jnp.where(jnp.isfinite(amax), amax, 0.0)
        aexp = jnp.exp(alpha - amax[dst])
        denom = jax.ops.segment_sum(aexp, dst, num_segments=N)
        num = jax.ops.segment_sum(aexp[:, :, None] * sf, dst, num_segments=N)
        out = num / jnp.maximum(denom, 1e-16)[:, :, None]
        return out.reshape(N, HEAD * HD)

    def _L3_gnn_ref(h, src, dst, rel_type, norm, weight, gamma, beta):
        import jax, jax.numpy as jnp
        import numpy as np
        N_NODES = 50000
        N_EDGES = 25000
        D = 64
        N_REL = 3
        BN_EPS = 1e-05
        proj = jnp.einsum('nd,rdo->rno', h, weight)
        msg = proj[rel_type, src] * norm[:, None]
        Swh = jax.ops.segment_sum(msg, dst, num_segments=h.shape[0])
        mean = jnp.mean(h, axis=0)
        var = jnp.mean((h - mean) ** 2, axis=0)
        h_bn = (h - mean) * jax.lax.rsqrt(var + BN_EPS) * gamma + beta
        return jax.nn.relu(h_bn + Swh)
    edge_index = jnp.stack([src, dst])
    x = _layernorm(x + _L0_gnn_ref(x, edge_index, L0_gnn_eps, L0_gnn_W1, L0_gnn_b1, L0_gnn_g1, L0_gnn_be1, L0_gnn_W2, L0_gnn_b2, L0_gnn_g2, L0_gnn_be2, L0_gnn_bn_g, L0_gnn_bn_be), axis=-1)
    x = _layernorm(x + _L1_gnn_ref(x, edge_index, edge_attr_32, L1_gnn_W1, L1_gnn_b1, L1_gnn_W2, L1_gnn_b2, L1_gnn_W3, L1_gnn_b3, L1_gnn_W4, L1_gnn_b4), axis=-1)
    x = _layernorm(x + _L2_gnn_ref(x, src, dst, L2_gnn_Wl, L2_gnn_bl, L2_gnn_Wa, L2_gnn_ba, L2_gnn_Wd, L2_gnn_bd, L2_gnn_Wf, L2_gnn_bf), axis=-1)
    x = _layernorm(x + _L3_gnn_ref(x, src, dst, edge_type_3, edge_weight, L3_gnn_weight, L3_gnn_gamma, L3_gnn_beta), axis=-1)
    return x

_drawn_inputs = setup_inputs


def setup_inputs(seed=0):
    import zlib

    import numpy as np

    out = dict(_drawn_inputs(seed))
    spreads = {'L0_gnn_eps': (0.0, 0.597),
     'L0_gnn_b1': (0.0, 0.1),
     'L0_gnn_g1': (1.0, 0.2),
     'L0_gnn_be1': (0.0, 0.1),
     'L0_gnn_b2': (0.0, 0.1),
     'L0_gnn_g2': (1.0, 0.2),
     'L0_gnn_be2': (0.0, 0.1),
     'L0_gnn_bn_g': (1.0, 0.2),
     'L0_gnn_bn_be': (0.0, 0.1),
     'L2_gnn_bl': (0.0, 0.1),
     'L2_gnn_bd': (0.0, 0.1),
     'L3_gnn_gamma': (1.0, 0.2),
     'L3_gnn_beta': (0.0, 0.539)}
    factors = {'edge_attr_32': 3.594, 'L1_gnn_b1': 6.529, 'L1_gnn_b2': 3.251, 'L2_gnn_Wa': 4.845}
    for name, (base, spread) in spreads.items():
        noise = np.random.default_rng([zlib.crc32(name.encode()), seed]).standard_normal(out[name].shape)
        drawn = base * np.exp(spread * noise) if base else spread * noise
        out[name] = jnp.asarray(drawn.astype(out[name].dtype))
    for name, factor in factors.items():
        out[name] = (out[name] * factor).astype(out[name].dtype)
    return out
```

```python
from contextlib import ExitStack, contextmanager

import concourse.bass as bass
from concourse import mybir
from concourse.alu_op_type import AluOpType as ALU

F32 = mybir.dt.float32
I32 = mybir.dt.int32
BF16 = mybir.dt.bfloat16
ACT = mybir.ActivationFunctionType
AX = mybir.AxisListType.X

N = 3125
C = 64
E_EDGES = 53125
FE = 32
HID = 128
HEADS, HD = 4, 16
RELS = 3
TILE = 128
WIN = 32
NP_, NT = 125, 25
BANK = 512
STEP = BANK - WIN
NB = -(-N // STEP)
HALF = 8
BODY = 2 * HALF
T_GIVEN = -(-E_EDGES // (TILE * BODY)) * BODY
BLOCKS = -(-N // WIN)
T_SORTED = -(-(T_GIVEN + BLOCKS) // BODY) * BODY
CH = 4
NCH = -(-NT // CH)
ROW2 = C + HEADS + 1
FAR = 1 << 20
BIG = 1.0e30
NEG_SLOPE = 0.01
BN_C = 1.0 / (1.0 + 1e-05) ** 0.5
N_LOADS = 15
P_B1, P_G1, P_BE1, P_B2, P_G2, P_BE2, P_BNG, P_BNB, P_EPS = range(0, 27, 3)
P_L1B3, P_L1B4, P_BL, P_BD, P_GAMMA, P_BETA, P_BA, P_BF = range(27, 35)
P_WF, P_A1, P_A2, P_COLS = 35, 38, 42, 46


def cols(c):
    return slice(c * CH * NP_, min((c + 1) * CH, NT) * NP_)


def tiles(c):
    return range(c * CH, min((c + 1) * CH, NT))


class Chain:

    def __init__(self, eng, sem):
        self.eng, self.sem, self.n, self.i = eng, sem, 0, None

    def __call__(self, ins):
        ins.then_inc(self.sem, 1)
        self.n += 1
        if self.i is None:
            self.eng.wait_ge(self.sem, self.n)
        else:
            self.eng.wait_ge(self.sem, self.i * self.per + self.n)

    @contextmanager
    def loop(self, rounds, per):
        before = self.n
        with self.eng.Fori(0, rounds) as i:
            self.i, self.per = i, per
            yield i
            assert self.n == before + per, (self.n - before, per)
        self.i, self.n = None, before + per * rounds


class Edges:

    def __init__(self, t, ch, src, dst, rel, wgt, dst_t, attr):
        self.t, self.ch, self.nc, self.rounds = t, ch, t // ch, t // BODY
        self.src, self.dst, self.rel, self.wgt, self.dst_t, self.attr = src, dst, rel, wgt, dst_t, attr
        assert self.nc * ch == t and ch % 4 == 0 and ch <= 128 and self.nc <= 6

    def landed(self, s, i):
        return i * (16 * HALF) + (s * self.rounds + 1) * (16 * HALF)

    def staged(self, s, i):
        return i + (s * (self.rounds + 1) + 1)


def build(nc, I, out):
    def dram(name, shape, dt=F32):
        return nc.dram_tensor(name, shape, dt, kind="Internal").ap()

    given = Edges(T_GIVEN, T_GIVEN // 4, I["src_e"], I["dst_e"], I["rel_e"], I["wgt_e"], I["dst_t"],
                  I["attr_t"])
    records = dram("records", [(T_SORTED + HALF) * TILE, 4 + FE])
    attr_sorted = dram("attr_sorted", [FE, T_SORTED * TILE])
    ordered = Edges(T_SORTED, T_SORTED // 6, None, None, None, None, None, attr_sorted)
    gin_tab = [dram(f"gin_tab{k}", [N, C]) for k in range(2)]
    edge_tab = dram("edge_tab", [N, HID])
    att_tab = dram("att_tab", [N, ROW2])
    q_tab = dram("q_tab", [N + WIN, 1])
    va_tab = dram("va_tab", [N + WIN, 2 * HEADS])
    rel_tab = dram("rel_tab", [RELS * N, C])
    stash = dram("stash", [T_SORTED // HALF * TILE, HALF, ROW2])

    with ExitStack() as ctx:
        def sb(name, shape, dt=F32):
            return ctx.enter_context(nc.sbuf_tensor(name, shape, dt))
        TM = T_SORTED
        onehot = sb("onehot", [TILE, TM, WIN])
        src_i = sb("src_i", [TILE, TM + BODY], I32)
        dst_i = sb("dst_i", [TILE, TM], I32)
        rel_i = sb("rel_i", [TILE, TM + BODY], I32)
        wgt = sb("wgt", [TILE, TM])
        dst_loc = sb("dst_loc", [TILE, TM])
        base_row = sb("base_row", [1, TM], I32)
        off_row = sb("off_row", [1, TM], I32)
        base_f = sb("base_f", [128, 6])
        base_i = sb("base_i", [128, 6], I32)
        off_f = sb("off_f", [128, 6])
        step6 = sb("step6", [128, 6, 8])
        span = sb("span", [128, 8])
        flag_f = sb("flag_f", [1, 2])
        flag = sb("flag", [1, 1], I32)
        ident = sb("ident", [128, 128])
        iota_f = sb("iota_f", [128, 128])
        pidx_i = sb("pidx_i", [128, 4], I32)
        pidx_f = sb("pidx_f", [128, 4])
        jmask = sb("jmask", [128, WIN])
        kmask = sb("kmask", [128, HEADS])
        m4 = sb("m4", [128, 4])
        ones = sb("ones", [128, 128])
        zeros = sb("zeros", [128, BANK], BF16)
        prm = sb("prm", [128, P_COLS])
        fold = sb("fold", [C, 6, 3])
        wgin = sb("wgin", [C, 6, C])
        w1a, w1b = sb("w1a", [C, HID]), sb("w1b", [FE, HID])
        w2, w4 = sb("w2", [HID, C]), sb("w4", [HID, C])
        w3a, w3b = sb("w3a", [C, HID]), sb("w3b", [C, HID])
        wl, wd = sb("wl", [C, C]), sb("wd", [C, C])
        wrel = sb("wrel", [C, RELS, C])
        brow = sb("brow", [1, HID + C])
        hproj = sb("hproj", [C, C + HEADS])
        fpq = sb("fpq", [C, 2])
        xt = sb("xt", [C, N])
        xn = sb("xn", [NP_, NT, C])
        yn = sb("yn", [NP_, NT, C])
        agg = sb("agg", [128, N])
        y1 = sb("y1", [128, N + WIN])
        row_t = sb("row_t", [1, NB - 1, WIN])
        tabn = sb("tabn", [NP_, 2, CH * RELS * C])
        stat = sb("stat", [NP_, 4, NT])
        bnst = sb("bnst", [C, 8])
        rows = sb("rows", [TILE, 2, HALF, HID])
        stage = sb("stage", [TILE, 2, HALF], I32)
        attr_buf = sb("attr_buf", [128, 2 * HALF * TILE])
        work = sb("work", [TILE, 2, HALF, HID])
        trio = sb("trio", [TILE, 3, 2, HALF, WIN])
        zbuf = sb("zbuf", [TILE, 2, 3, HALF])
        late = sb("late", [128, 3 * HEADS * TM])
        sg = sb("sg", [TILE, TM])
        abuf = sb("abuf", [TILE, 2, 3, HALF, HEADS])
        mxg = sb("mxg", [128, 2, HALF])
        mxe = sb("mxe", [128, 2, HALF, WIN])
        ps = ctx.enter_context(nc.psum_tensor("ps", [128, 8 * BANK], F32))
        attr = attr_buf[0:FE, :].rearrange("p (h n) -> p h n", h=2)
        winv = attr_buf[:, 0:6 * WIN * 2 * HEADS].rearrange("p (c n) -> p c n", c=6)
        winq = attr_buf[:, 6 * WIN * 2 * HEADS:6 * WIN * (2 * HEADS + 1)].rearrange("p (c n) -> p c n", c=6)
        iota_i = attr_buf[:, 0:128].bitcast(I32)
        wexp = trio[:, 1, :, 0:4, :]
        ohs, msk = trio[:, 0], trio[:, 1]
        ohT = trio[:, 2].rearrange("p h a b -> p h (a b)")
        dst_tm = trio[:, :, :, :, :].bitcast(I32).rearrange("p a h k w -> p (a h k w)")[:, 0:6 * TILE]\
            .rearrange("p (c n) -> p c n", n=TILE)
        row2 = late[0:1, 0:2 * N].rearrange("p (a n) -> p a n", a=2)
        su = late[:, 0:HEADS * TM].rearrange("p (t k) -> p t k", k=HEADS)
        wtv = late[:, HEADS * TM:].rearrange("p (t k) -> p t k", k=2 * HEADS)
        wtq = dst_loc
        sq = agg[0:NP_, 0:NT * C].rearrange("p (i f) -> p i f", f=C)
        smax = y1[0:HEADS, :]
        vt = agg[0:HEADS, :]
        diag = work

        pe_regs = dve_regs = None

        def bank(b, n=BANK, off=0):
            return ps[:, b * BANK + off:b * BANK + off + n]

        sems = {}

        def sem(name):
            if name not in sems:
                sems[name] = ctx.enter_context(nc.semaphore(name))
            return sems[name]

        PARTS = ((0, 16), (16, NT))
        V, A, M = nc.vector, nc.scalar.activation, nc.tensor.matmul

        def chunk(c):
            return len(tiles(c))

        def table_parts(k, c):
            return k * ((NCH + 1 - c % 2) // 2) + (RELS if k == 3 else 1) * (c // 2)

        def half_tiles(i, h):
            return bass.ds(i * BODY + h * HALF, HALF)

        def sp_start(sp):
            sp.dma_start(dst_tm[0:given.ch, 0:given.nc, :], I["dst_t"]).then_inc(sem("dst_in"), 16)
            sp_edges(sp, given)
            loads = [(prm[:, :], I["params"]), (xt[:, :], I["x_t"]),
                     (xn[:, :, :], I["x"].rearrange("(i p) c -> p i c", p=NP_)),
                     (wgin[:, 0:3, :], I["L0_gnn_W1"].rearrange("l a b -> a l b")),
                     (wgin[:, 3:6, :], I["L0_gnn_W2"].rearrange("l a b -> a l b")),
                     (w1a[:, :], I["L1_gnn_W1"][0:C, :]), (w1b[:, :], I["L1_gnn_W1"][C:C + FE, :]),
                     (w2[:, :], I["L1_gnn_W2"]), (w3a[:, :], I["L1_gnn_W3"][0:C, :]),
                     (w3b[:, :], I["L1_gnn_W3"][C:2 * C, :]), (w4[:, :], I["L1_gnn_W4"]),
                     (wl[:, :], I["L2_gnn_Wl"]), (wd[:, :], I["L2_gnn_Wd"]),
                     (wrel[:, :, :], I["L3_gnn_weight"].rearrange("r a b -> a r b")),
                     (brow[:, :], I["brow"])]
            assert len(loads) == N_LOADS
            for to, of in loads:
                sp.dma_start(to, of).then_inc(sem("params"), 16)

        def pool_start(pool):
            g = nc.gpsimd
            chain = Chain(pool, sem("pool"))
            g.iota(iota_i[:, :], pattern=[[1, 128]], base=0, channel_multiplier=0).then_inc(sem("consts"), 1)
            g.iota(pidx_i[:, 0:1], pattern=[[0, 1]], base=0, channel_multiplier=1).then_inc(sem("consts"), 1)
            g.memset(ones[:, :], 1.0).then_inc(sem("consts"), 1)
            g.memset(zeros[:, :], 0.0).then_inc(sem("consts"), 1)
            g.memset(src_i[:, T_GIVEN:TM + BODY], 0).then_inc(sem("consts"), 1)
            g.memset(rel_i[:, T_GIVEN:TM + BODY], 0).then_inc(sem("consts"), 1)
            g.memset(rows[:, :, :, C:C + 1], 1.0).then_inc(sem("consts"), 1)
            chain(g.memset(ident[:, :], 0.0))
            g.affine_select(out=ident[:, :], in_=ident[:, :], compare_op=ALU.not_equal, fill=1.0,
                            base=0, pattern=[[-1, 128]], channel_multiplier=1).then_inc(sem("consts"), 1)

        def dve_min_max(dve, chain, E):
            d = dst_tm[0:E.ch, 0:E.nc, :]
            near = work[0:E.ch, 0, 0:E.nc, :]
            V.scalar_tensor_tensor(out=near, in0=d, scalar=float(FAR), in1=d, op0=ALU.is_lt,
                                   op1=ALU.mult).then_inc(sem("dve"), 1)
            chain.n += 1
            chain(V.tensor_reduce(base_f[0:E.ch, 0:E.nc], d, AX, ALU.min))
            chain(V.tensor_reduce(span[0:E.ch, 0:E.nc], near, AX, ALU.max))
            chain(V.tensor_tensor(span[0:E.ch, 0:E.nc], span[0:E.ch, 0:E.nc], base_f[0:E.ch, 0:E.nc],
                                  ALU.subtract))
            chain(V.tensor_scalar(base_f[0:E.ch, 0:E.nc], base_f[0:E.ch, 0:E.nc], float(N - 1), None,
                                  ALU.min))
            V.tensor_reduce(span[0:E.ch, 7:8], span[0:E.ch, 0:E.nc], AX, ALU.max)\
                .then_inc(sem("span_ready"), 1)

        def dve_start(dve, chain):
            dve.wait_ge(sem("dst_in"), 16)
            dve_min_max(dve, chain, given)
            dve.wait_ge(sem("span_row"), 1)
            chain(V.tensor_reduce(flag_f[:, 0:1], bank(0, given.ch)[0:1, :], AX, ALU.max))
            V.tensor_scalar(flag[:, :], flag_f[:, 0:1], float(WIN - 1), None, ALU.is_le)\
                .then_inc(sem("flag"), 1)
            dve.wait_ge(sem("consts"), 8)
            V.tensor_copy(iota_f[:, :], iota_i[:, :]).then_inc(sem("dve"), 1)
            V.tensor_scalar(pidx_i[:, 1:2], pidx_i[:, 0:1], 31, None, ALU.bitwise_and).then_inc(sem("dve"), 1)
            V.tensor_scalar(pidx_i[:, 2:3], pidx_i[:, 0:1], 5, None, ALU.logical_shift_right)\
                .then_inc(sem("dve"), 1)
            chain.n += 3
            chain(V.tensor_scalar(pidx_i[:, 3:4], pidx_i[:, 0:1], 3, None, ALU.bitwise_and))
            chain(V.tensor_copy(pidx_f[:, :], pidx_i[:, :]))
            for mask, n, c in ((jmask, WIN, 1), (kmask, HEADS, 2), (m4, 4, 3)):
                V.tensor_scalar(mask[:, :], iota_f[:, 0:n], pidx_f[:, c:c + 1], None, ALU.is_equal)\
                    .then_inc(sem("masks"), 1)
            dve.wait_ge(sem("params"), 16 * N_LOADS)

            def p(k):
                return prm[0:C, k:k + 3]
            for o, (g, b, be) in ((0, (P_G1, P_B1, P_BE1)), (2, (P_G2, P_B2, P_BE2))):
                chain(V.tensor_scalar(fold[:, o, :], p(g), BN_C, None, ALU.mult))
                chain(V.tensor_tensor(fold[:, o + 1, :], fold[:, o, :], p(b), ALU.mult))
                chain(V.tensor_tensor(fold[:, o + 1, :], fold[:, o + 1, :], p(be), ALU.add))
            chain(V.tensor_scalar(fold[:, 4, :], p(P_BNG), BN_C, None, ALU.mult))
            chain(V.tensor_scalar(fold[:, 5, :], p(P_EPS), 1.0, None, ALU.add))
            chain(V.tensor_tensor(fpq[:, 0:1], prm[0:C, P_WF:P_WF + 1], prm[0:C, P_WF + 2:P_WF + 3], ALU.add))
            chain(V.tensor_tensor(fpq[:, 1:2], prm[0:C, P_WF + 1:P_WF + 2], prm[0:C, P_WF + 2:P_WF + 3],
                                  ALU.subtract))
            chain(V.tensor_copy(hproj[:, 0:C], ident[0:C, 0:C]))
            V.tensor_copy(hproj[:, C:C + HEADS], prm[0:C, P_A1:P_A1 + HEADS]).then_inc(sem("folded"), 1)

        def pe_start(pe):
            pe.wait_ge(sem("consts"), 8)
            pe.wait_ge(sem("span_ready"), 1)
            nc.tensor.transpose(bank(0, given.ch)[0:1, :], span[0:given.ch, 7:8],
                                ident[0:given.ch, 0:given.ch]).then_inc(sem("span_row"), 1)

        def sp_edges(sp, E):
            for to, of in ((src_i[:, 0:E.t], E.src), (dst_i[:, 0:E.t], E.dst), (rel_i[:, 0:E.t], E.rel),
                           (wgt[:, 0:E.t], E.wgt)):
                sp.dma_start(to, of).then_inc(sem("edges_in"), 16)

        def dve_edges(dve, chain, E):
            ch = E.ch
            b = base_f[0:ch, 0:E.nc]
            chain(V.tensor_scalar(step6[0:ch, 0, 0:NB - 1], iota_f[0:ch, 1:NB], float(STEP), None, ALU.mult))
            chain(V.tensor_copy(base_i[0:ch, 0:E.nc], b))
            chain(V.tensor_copy(abuf[0:ch, 0, 0, 0, 0:1], b[:, 0:1]))
            cmp = abuf[0:ch, 1, :, :, :].rearrange("p a b c -> p (a b c)")[:, 0:E.nc * (NB - 1)]\
                .rearrange("p (c m) -> p c m", m=NB - 1)
            chain(V.tensor_tensor(cmp, b.unsqueeze(2).to_broadcast([ch, E.nc, NB - 1]),
                                  step6[0:ch, 0:1, 0:NB - 1].to_broadcast([ch, E.nc, NB - 1]), ALU.is_ge))
            chain(V.tensor_reduce(off_f[0:ch, 0:E.nc], cmp, AX, ALU.add))
            chain(V.scalar_tensor_tensor(out=off_f[0:ch, 0:E.nc], in0=off_f[0:ch, 0:E.nc], scalar=float(WIN),
                                         in1=b, op0=ALU.mult, op1=ALU.add))
            for c in range(E.nc):
                V.tensor_scalar(diag[0:ch, 0, c, 0:ch], ident[0:ch, 0:ch], base_f[0:ch, c:c + 1], None,
                                ALU.mult)
                V.tensor_scalar(diag[0:ch, 1, c, 0:ch], ident[0:ch, 0:ch], off_f[0:ch, c:c + 1], None,
                                ALU.mult).then_inc(sem("diag_ready"), 1)
            dve.wait_ge(sem("edges_in"), 64)
            for c in range(E.nc):
                at = slice(c * ch, (c + 1) * ch)
                dve.wait_ge(sem("base_out"), c + 1)
                V.tensor_copy(base_row[:, at], bank(c, ch)[0:1, :])
                V.tensor_copy(off_row[:, at], bank(c, ch, 256)[0:1, :])
                chain(V.tensor_tensor(dst_loc[:, at], dst_i[:, at], bank(c, ch), ALU.subtract))
            for c in range(E.nc):
                at = slice(c * ch, (c + 1) * ch)
                V.tensor_tensor(onehot[:, at, :], dst_loc[:, at].unsqueeze(2).to_broadcast([TILE, ch, WIN]),
                                iota_f[:, 0:WIN].unsqueeze(1).to_broadcast([TILE, ch, WIN]), ALU.is_equal)\
                    .then_inc(sem("onehot_ready"), 1)
            V.scalar_tensor_tensor(out=rel_i[:, 0:E.t], in0=rel_i[:, 0:E.t], scalar=float(N),
                                   in1=src_i[:, 0:E.t], op0=ALU.mult, op1=ALU.add).then_inc(sem("rel_ready"), 1)

        def pe_edges(pe, E):
            for c in range(E.nc):
                pe.wait_ge(sem("diag_ready"), c + 1)
                M(bank(c, E.ch), ones[0:E.ch, :], diag[0:E.ch, 0, c, 0:E.ch], start=True, stop=True)
                M(bank(c, E.ch, 256)[0:1, :], ones[0:E.ch, 0:1], diag[0:E.ch, 1, c, 0:E.ch],
                  start=True, stop=True, skip_group_check=True).then_inc(sem("base_out"), 1)

        def pool_gather(pool, E, s, table, width):
            with pool.Fori(0, E.rounds) as i:
                for h in range(2):
                    pool.wait_ge(sem(f"staged{h}"), E.staged(s, i))
                    pool.sem_inc(sem("gather_started"), 1)
                    for k in range(HALF):
                        nc.gpsimd.indirect_dma_start(
                            out=rows[:, h, k, 0:width], out_offset=None, in_=table,
                            in_offset=bass.IndirectOffsetOnAxis(ap=stage[:, h, k:k + 1], axis=0))\
                            .then_inc(sem(f"landed{h}"), 16)

        def stage_first(act, E, s, idx):
            for h in range(2):
                A(stage[:, h, :], idx[:, h * HALF:(h + 1) * HALF], ACT.Copy).then_inc(sem(f"staged{h}"), 1)

        def stage_next(s, idx, i, h):
            A(stage[:, h, :], idx[:, bass.ds(i * BODY + BODY + h * HALF, HALF)], ACT.Copy)\
                .then_inc(sem(f"staged{h}"), 1)

        def pe_clear(m):
            for b in range(NB):
                M(bank(b)[0:m, :], zeros[:, 0:m], zeros[:, :], start=True, stop=False, skip_group_check=True)

        def pe_windows(pe, i, h):
            pe.reg_load(pe_regs, off_row[:, half_tiles(i, h)])
            return [pe.snap(r, min_val=0, max_val=NB * BANK - WIN) for r in pe_regs]

        def pe_scatter(col, m, lhsT, rhs):
            return M(ps[0:m, bass.ds(col, WIN)], lhsT, rhs, start=False, stop=False, skip_group_check=True)

        def onehot_tile(i, h, k):
            return onehot[:, bass.ds(i * BODY + h * HALF + k, 1), :].rearrange("p a b -> p (a b)")

        def dve_sums(dve, chain, s, m):
            dve.wait_ge(sem("summed"), s + 1)
            for b in range(NB):
                n = min(STEP, N - b * STEP)
                ins = V.tensor_copy(agg[0:m, b * STEP:b * STEP + n], bank(b, n)[0:m, :])
                if b:
                    chain(ins)
                    at = agg[0:m, b * STEP:b * STEP + WIN]
                    ins = V.tensor_tensor(at, at, bank(b - 1, WIN, STEP)[0:m, :], ALU.add)
                ins.then_inc(sem("sums_ready"), 1)

        def dve_norm(dve, chain, q, after=None):
            for part, (a, b) in enumerate(PARTS):
                if after is not None:
                    dve.wait_ge(*after(part))
                n = b - a
                y, s = yn[:, a:b, :], sq[:, a:b, :]
                wide = [NP_, n, C]
                chain(V.tensor_reduce(stat[:, 0, a:b], y, AX, ALU.add))
                chain(V.tensor_scalar(stat[:, 0, a:b], stat[:, 0, a:b], -1.0 / C, None, ALU.mult))
                chain(V.tensor_tensor(y, y, stat[:, 0, a:b].unsqueeze(2).to_broadcast(wide), ALU.add))
                chain(V.tensor_tensor(s, y, y, ALU.mult))
                chain(V.tensor_reduce(stat[:, 1, a:b], s, AX, ALU.add))
                V.tensor_scalar(stat[:, 1, a:b], stat[:, 1, a:b], 1.0 / C, 1e-05, ALU.mult, ALU.add)\
                    .then_inc(sem("ln_var"), 1)
            for part, (a, b) in enumerate(PARTS):
                wide = [NP_, b - a, C]
                dve.wait_ge(sem("ln_sd"), 2 * q + part + 1)
                chain(V.reciprocal(stat[:, 3, a:b], stat[:, 2, a:b]))
                V.tensor_tensor(xn[:, a:b, :], yn[:, a:b, :], stat[:, 3, a:b].unsqueeze(2).to_broadcast(wide),
                                ALU.mult).then_inc(sem("xn_ready"), 1)

        def act_norm(act, q):
            for part, (a, b) in enumerate(PARTS):
                act.wait_ge(sem("ln_var"), 2 * q + part + 1)
                A(stat[:, 2, a:b], stat[:, 1, a:b], ACT.Sqrt).then_inc(sem("ln_sd"), 1)

        def pe_back(pe, q, c):
            pe.wait_ge(sem("xn_ready"), 2 * q + (1 if tiles(c)[-1] < PARTS[0][1] else 2))
            if c >= 2:
                pe.wait_ge(sem("back_ev"), q * NCH + c - 1)
            for j, t in enumerate(tiles(c)):
                ins = nc.tensor.transpose(bank(c % 2, NP_, j * NP_)[0:C, :], xn[:, t, :], ident[0:NP_, 0:NP_])
            ins.then_inc(sem("back"), 1)

        def act_back(act, q, c):
            act.wait_ge(sem("back"), q * NCH + c + 1)
            A(xt[:, cols(c)], bank(c % 2, chunk(c) * NP_)[0:C, :], ACT.Copy).then_inc(sem("back_ev"), 1)

        def pool_gin(pool, E):
            pool.wait_ge(sem("consts"), 8)
            for l in range(3):
                if l:
                    pool.wait_ge(sem("gin_out"), 16 * NCH * l)
                pool_gather(pool, E, l, I["x"] if l == 0 else gin_tab[l - 1], C)

        def pe_gin(pe, E):
            pe.wait_ge(sem("onehot_ready"), E.nc)
            for l in range(3):
                m = C + (l == 0)
                if l:
                    pe.wait_ge(sem("ev"), NCH * l)
                pe_clear(m)
                with pe.Fori(0, E.rounds) as i:
                    for h in range(2):
                        at = pe_windows(pe, i, h)
                        pe.wait_ge(sem(f"landed{h}"), E.landed(l, i))
                        for k in range(HALF):
                            ins = pe_scatter(at[k], m, rows[:, h, k, 0:m], onehot_tile(i, h, k))
                        ins.then_inc(sem(f"taken{l}{h}"), 1)
                M(bank(7, 8)[0:1, :], zeros[:, 0:1], zeros[:, 0:8], start=True, stop=True)\
                    .then_inc(sem("summed"), 1)
                if l == 0:
                    pe.wait_ge(sem("count_out"), 1)
                for step in range(NCH + 2):
                    if step < NCH:
                        c = step
                        n = chunk(c) * NP_
                        pe.wait_ge(sem("sums_ready"), l * NB + min(c + 2, NB))
                        if c >= 2:
                            pe.wait_ge(sem("a1"), l * NCH + c - 1)
                        M(bank((7, 0)[c % 2], n)[0:C, :], wgin[:, l, :], agg[0:C, cols(c)],
                          start=True, stop=True).then_inc(sem("mm1"), 1)
                    if 1 <= step <= NCH:
                        c = step - 1
                        n = chunk(c) * NP_
                        pe.wait_ge(sem("a1"), l * NCH + c + 1)
                        pe.wait_ge(sem("sums_ready"), l * NB + min(c + 4, NB))
                        if c >= 2:
                            pe.wait_ge(sem("a2"), l * NCH + c - 1)
                        M(bank(1 + c % 2, n)[0:C, :], wgin[:, 3 + l, :], y1[0:C, cols(c)],
                          start=True, stop=True).then_inc(sem("mm2"), 1)
                    if step >= 2:
                        c = step - 2
                        pe.wait_ge(sem("x_new"), l * NCH + c + 1)
                        pe.wait_ge(sem("sums_ready"), l * NB + min(c + 6, NB))
                        if c >= 2:
                            pe.wait_ge(sem("ev"), l * NCH + c - 1)
                        for j, t in enumerate(tiles(c)):
                            ins = nc.tensor.transpose(bank(3 + c % 2, C, j * C)[0:NP_, :],
                                                      xt[:, t * NP_:(t + 1) * NP_], ident[0:C, 0:C])
                        ins.then_inc(sem("tr"), 1)

        def act_gin(act, E):
            act.wait_ge(sem("consts"), 8)
            act.wait_ge(sem("edges_in"), 64)
            for l in range(3):
                stage_first(act, E, l, src_i)
                with act.Fori(0, E.rounds) as i:
                    for h in range(2):
                        act.wait_ge(sem(f"taken{l}{h}"), i + 1)
                        stage_next(l, src_i, i, h)
                if l == 0:
                    act.wait_ge(sem("folded"), 1)
                    act.wait_ge(sem("summed"), 1)
                    banks = ps[C:C + 1, 0:(NB - 1) * BANK].rearrange("p (b n) -> p b n", n=BANK)
                    A(row2[:, 0, 0:(NB - 1) * STEP].rearrange("p (b n) -> p b n", n=STEP),
                      banks[:, :, 0:STEP], ACT.Copy)
                    A(row2[:, 0, (NB - 1) * STEP:N], bank(NB - 1, N - (NB - 1) * STEP)[C:C + 1, :], ACT.Copy)
                    A(row_t[:, :, :], banks[:, :, STEP:BANK], ACT.Copy).then_inc(sem("count_out"), 1)
                for step in range(NCH + 2):
                    if step < NCH:
                        c = step
                        act.wait_ge(sem("mm1"), l * NCH + c + 1)
                        A(y1[0:C, cols(c)], bank((7, 0)[c % 2], chunk(c) * NP_)[0:C, :], ACT.Relu,
                          bias=fold[:, 1, l:l + 1], scale=fold[:, 0, l:l + 1]).then_inc(sem("a1"), 1)
                    if 1 <= step <= NCH:
                        c = step - 1
                        act.wait_ge(sem("mm2"), l * NCH + c + 1)
                        A(y1[0:C, cols(c)], bank(1 + c % 2, chunk(c) * NP_)[0:C, :], ACT.Relu,
                          bias=fold[:, 3, l:l + 1], scale=fold[:, 2, l:l + 1]).then_inc(sem("a2"), 1)
                    if step >= 2 and l < 2:
                        c = step - 2
                        act.wait_ge(sem("tr"), l * NCH + c + 1)
                        A(yn[:, c * CH:c * CH + chunk(c), :].rearrange("p a b -> p (a b)"),
                          bank(3 + c % 2, chunk(c) * C)[0:NP_, :], ACT.Copy).then_inc(sem("ev"), 1)

        def dve_gin(dve, chain, E):
            for l in range(3):
                dve.wait_ge(sem("summed"), l + 1)
                for b in range(NB):
                    n = min(STEP, N - b * STEP)
                    at = slice(b * STEP, b * STEP + n)
                    ins = V.scalar_tensor_tensor(out=agg[0:C, at], in0=xt[:, at], scalar=fold[:, 5, l:l + 1],
                                                 in1=bank(b, n)[0:C, :], op0=ALU.mult, op1=ALU.add)
                    if b:
                        chain(ins)
                        at = agg[0:C, b * STEP:b * STEP + WIN]
                        ins = V.tensor_tensor(at, at, bank(b - 1, WIN, STEP)[0:C, :], ALU.add)
                    ins.then_inc(sem("sums_ready"), 1)
                for step in range(NCH + 1):
                    if step < NCH:
                        c = step
                        dve.wait_ge(sem("a2"), l * NCH + c + 1)
                        ins = V.tensor_scalar(xt[:, cols(c)], y1[0:C, cols(c)], fold[:, 4, l:l + 1],
                                              prm[0:C, P_BNB + l:P_BNB + l + 1], ALU.mult, ALU.add)
                        if l < 2:
                            chain(ins)
                            ins = V.tensor_scalar(xt[:, cols(c)], xt[:, cols(c)], 0.0, None, ALU.max)
                        ins.then_inc(sem("x_new"), 1)
                    if step >= 1 and l == 2:
                        c = step - 1
                        dve.wait_ge(sem("tr"), l * NCH + c + 1)
                        at = slice(c * CH, c * CH + chunk(c))
                        V.tensor_tensor(yn[:, at, :], bank(3 + c % 2, chunk(c) * C)[0:NP_, :]
                                        .rearrange("p (a b) -> p a b", b=C), xn[:, at, :], ALU.add)\
                            .then_inc(sem("ev"), 1)
                if l == 0:
                    dve.wait_ge(sem("count_out"), 1)
                    at = row2[:, 0, STEP:NB * STEP - STEP + WIN]
                    for b in range(1, NB):
                        at = row2[:, 0, b * STEP:b * STEP + WIN]
                        ins = V.tensor_tensor(at, at, row_t[:, b - 1, :], ALU.add)
                    chain(ins)
                    chain(V.tensor_scalar(row2[:, 1, :], row2[:, 0, :], 1.0, None, ALU.max))
                    V.reciprocal(row2[:, 1, :], row2[:, 1, :]).then_inc(sem("count_ready"), 1)
            dve.wait_ge(sem("ev"), 3 * NCH)
            dve_norm(dve, chain, 0)

        def sp_gin(sp, E):
            for l in range(2):
                for c in range(NCH):
                    sp.wait_ge(sem("ev"), l * NCH + c + 1)
                    sp.dma_start(gin_tab[l][cols(c), :].rearrange("(i p) f -> p i f", p=NP_),
                                 yn[:, c * CH:c * CH + chunk(c), :]).then_inc(sem("gin_out"), 16)

        def pe_edge(pe, E):
            for step in range(NCH + 1):
                if step < NCH:
                    pe_back(pe, 0, step)
                if step >= 1:
                    c = step - 1
                    pe.wait_ge(sem("back_ev"), c + 1)
                    if c >= 2:
                        pe.wait_ge(sem("e_ev"), c - 1)
                    for j, t in enumerate(tiles(c)):
                        to = bank(2 + c % 2, HID, j * HID)[0:NP_, :]
                        M(to, xt[:, t * NP_:(t + 1) * NP_], w1a[:, :], start=True, stop=False,
                          skip_group_check=True)
                        ins = M(to, ones[0:1, 0:NP_], brow[:, 0:HID], start=False, stop=True,
                                skip_group_check=True)
                    ins.then_inc(sem("e_mm"), 1)
            pe.wait_ge(sem("e_ev"), NCH)
            pe_clear(HID)
            pe.sem_inc(sem("scattered30"), 1)
            pe.sem_inc(sem("scattered31"), 1)
            pe.sem_inc(sem("px_added"), 1)
            with pe.Fori(0, E.rounds) as i:
                for h in range(2):
                    at = pe_windows(pe, i, h)
                    pe.wait_ge(sem(f"attr_in{h}"), i * 16 + 16)

                    def project(p):
                        pe.wait_ge(sem("px_added"), i * 4 + (2 * h + p + 1))
                        for k in range(4 * p, 4 * p + 4):
                            ins = M(bank(7, HID, (k % 4) * HID),
                                    attr[:, h, k * TILE:(k + 1) * TILE], w1b[:, :], start=True, stop=True,
                                    skip_group_check=True)
                        ins.then_inc(sem("px_full"), 1)

                    def scatter(p):
                        pe.wait_ge(sem("relued"), i * 4 + (2 * h + p + 1))
                        for k in range(4 * p, 4 * p + 4):
                            ins = pe_scatter(at[k], HID, work[:, h, k, :], onehot_tile(i, h, k))
                        return ins

                    project(0)
                    project(1)
                    scatter(0)
                    scatter(1).then_inc(sem(f"scattered3{h}"), 1)
            M(bank(7, 8)[0:1, :], zeros[:, 0:1], zeros[:, 0:8], start=True, stop=True)\
                .then_inc(sem("summed"), 1)
            pe.wait_ge(sem("sums_ready"), 4 * NB)
            for step in range(NCH + 3):
                if step < NCH:
                    c = step
                    n = chunk(c) * NP_
                    if c >= 2:
                        pe.wait_ge(sem("m_mean"), c - 1)
                    if c >= 4:
                        pe.wait_ge(sem("m_ev"), c - 3)
                    to = bank(c % 2, n)[0:C, :]
                    M(to, w2[:, :], agg[:, cols(c)], start=True, stop=False)
                    M(to, brow[:, HID:HID + C], row2[:, 0, cols(c)], start=False, stop=True)
                    M(bank(2 + c % 2, n)[0:C, :], ones[0:1, 0:C], row2[:, 1, cols(c)], start=True, stop=True)\
                        .then_inc(sem("m_sum"), 1)
                if 1 <= step <= NCH:
                    c = step - 1
                    n = chunk(c) * NP_
                    pe.wait_ge(sem("m_mean"), c + 1)
                    if c >= 2:
                        pe.wait_ge(sem("m_relu"), c - 1)
                    M(bank(4 + c % 2, n), w3a[:, :], xt[:, cols(c)], start=True, stop=False)
                    M(bank(4 + c % 2, n), w3b[:, :], y1[0:C, cols(c)], start=False, stop=True)\
                        .then_inc(sem("m_hid"), 1)
                if 2 <= step <= NCH + 1:
                    c = step - 2
                    n = chunk(c) * NP_
                    pe.wait_ge(sem("m_relu"), c + 1)
                    if c >= 2:
                        pe.wait_ge(sem("m_y"), c - 1)
                    M(bank(6 + c % 2, n)[0:C, :], w4[:, :], y1[:, cols(c)], start=True, stop=True)\
                        .then_inc(sem("m_out"), 1)
                if step >= 3:
                    c = step - 3
                    pe.wait_ge(sem("m_y"), c + 1)
                    if c >= 2:
                        pe.wait_ge(sem("m_ev"), c - 1)
                    for j, t in enumerate(tiles(c)):
                        ins = nc.tensor.transpose(bank(2 + c % 2, C, j * C)[0:NP_, :],
                                                  y1[0:C, t * NP_:(t + 1) * NP_], ident[0:C, 0:C])
                    ins.then_inc(sem("m_tr"), 1)

        def dve_edge(dve, chain, E):
            with dve.Fori(0, E.rounds) as i:
                for h in range(2):
                    dve.wait_ge(sem(f"landed{h}"), E.landed(3, i))
                    dve.wait_ge(sem(f"scattered3{h}"), i + 1)
                    for p in range(2):
                        dve.wait_ge(sem("px_full"), i * 4 + (2 * h + p + 1))
                        V.tensor_tensor(work[:, h, 4 * p:4 * p + 4, :], rows[:, h, 4 * p:4 * p + 4, :],
                                        bank(7).rearrange("p (a b) -> p a b", b=HID),
                                        ALU.add).then_inc(sem("px_added"), 1)
            dve_sums(dve, chain, 3, HID)
            for step in range(NCH + 2):
                if step < NCH:
                    c = step
                    dve.wait_ge(sem("m_rb"), c + 1)
                    V.tensor_tensor(y1[0:C, cols(c)], bank(c % 2, chunk(c) * NP_)[0:C, :],
                                    work[0:C, c % 2, :, :].rearrange("p a b -> p (a b)")[:, 0:chunk(c) * NP_],
                                    ALU.mult).then_inc(sem("m_mean"), 1)
                if step >= 2:
                    c = step - 2
                    dve.wait_ge(sem("m_out"), c + 1)
                    V.scalar_tensor_tensor(out=y1[0:C, cols(c)], in0=bank(6 + c % 2, chunk(c) * NP_)[0:C, :],
                                           scalar=prm[0:C, P_L1B4:P_L1B4 + 1], in1=xt[:, cols(c)],
                                           op0=ALU.add, op1=ALU.add).then_inc(sem("m_y"), 1)
            dve_norm(dve, chain, 1, lambda part: (sem("m_ev"), (4, NCH)[part]))

        def act_edge(act, E):
            act_norm(act, 0)
            for step in range(NCH + 1):
                if step < NCH:
                    act_back(act, 0, step)
                if step >= 1:
                    c = step - 1
                    act.wait_ge(sem("e_mm"), c + 1)
                    if c >= 2:
                        act.wait_ge(sem(f"table_out{c % 2}"), 16 * table_parts(0, c))
                    A(tabn[:, c % 2, 0:chunk(c) * HID], bank(2 + c % 2, chunk(c) * HID)[0:NP_, :], ACT.Copy)\
                        .then_inc(sem("e_ev"), 1)
            stage_first(act, E, 3, src_i)
            with act.Fori(0, E.rounds) as i:
                for h in range(2):
                    for p in range(2):
                        act.wait_ge(sem("px_added"), i * 4 + (2 * h + p + 2))
                        four = work[:, h, 4 * p:4 * p + 4, :]
                        A(four, four, ACT.Relu).then_inc(sem("relued"), 1)
                    stage_next(3, src_i, i, h)
            for step in range(NCH + 3):
                if step < NCH:
                    c = step
                    act.wait_ge(sem("m_sum"), c + 1)
                    if c >= 2:
                        act.wait_ge(sem("m_mean"), c - 1)
                    A(work[0:C, c % 2, :, :].rearrange("p a b -> p (a b)")[:, 0:chunk(c) * NP_],
                      bank(2 + c % 2, chunk(c) * NP_)[0:C, :], ACT.Copy).then_inc(sem("m_rb"), 1)
                if 1 <= step <= NCH:
                    c = step - 1
                    act.wait_ge(sem("m_hid"), c + 1)
                    A(y1[:, cols(c)], bank(4 + c % 2, chunk(c) * NP_), ACT.Relu,
                      bias=prm[:, P_L1B3:P_L1B3 + 1]).then_inc(sem("m_relu"), 1)
                if step >= 3:
                    c = step - 3
                    act.wait_ge(sem("m_tr"), c + 1)
                    A(yn[:, c * CH:c * CH + chunk(c), :].rearrange("p a b -> p (a b)"),
                      bank(2 + c % 2, chunk(c) * C)[0:NP_, :], ACT.Copy).then_inc(sem("m_ev"), 1)
            act_norm(act, 1)

        def sp_edge(sp, E):
            for c in range(NCH):
                sp.wait_ge(sem("e_ev"), c + 1)
                sp.dma_start(edge_tab[cols(c), :].rearrange("(i p) f -> p i f", p=NP_),
                             tabn[:, c % 2, 0:chunk(c) * HID].rearrange("p (a b) -> p a b", b=HID))\
                    .then_inc(sem(f"table_out{c % 2}"), 16)
            with sp.Fori(0, E.rounds) as i:
                for h in range(2):
                    sp.wait_ge(sem(f"scattered3{h}"), i + 1)
                    sp.dma_start(attr[:, h, :],
                                 E.attr[:, bass.ds(i * (BODY * TILE) + h * HALF * TILE, HALF * TILE)])\
                        .then_inc(sem(f"attr_in{h}"), 16)

        def pool_edge(pool, E):
            pool.wait_ge(sem("table_out0"), 16 * table_parts(0, NCH + NCH % 2))
            pool.wait_ge(sem("table_out1"), 16 * table_parts(0, NCH + 1 - NCH % 2))
            pool_gather(pool, E, 3, edge_tab, HID)

        def pe_att_tables(pe, E):
            for step in range(NCH + 2):
                if step < NCH:
                    pe_back(pe, 1, step)
                if 1 <= step <= NCH:
                    c = step - 1
                    n = chunk(c) * NP_
                    pe.wait_ge(sem("back_ev"), NCH + c + 1)
                    if c:
                        pe.wait_ge(sem("proj_ev"), 2 * c)
                    M(bank(2, n)[0:C, :], wl[:, :], xt[:, cols(c)], start=True, stop=True)\
                        .then_inc(sem("proj"), 1)
                    M(bank(3, n)[0:C, :], wd[:, :], xt[:, cols(c)], start=True, stop=True)\
                        .then_inc(sem("proj"), 1)
                if step >= 2:
                    c = step - 2
                    n = chunk(c) * NP_
                    pe.wait_ge(sem("proj_ev"), 2 * c + 2)
                    if c >= 2:
                        pe.wait_ge(sem("hup_ev"), c - 1)
                    if c:
                        pe.wait_ge(sem("vq_ev"), 2 * c)
                    for j, t in enumerate(tiles(c)):
                        at = slice(t * NP_, (t + 1) * NP_)
                        M(bank(4 + c % 2, C + HEADS, j * 72)[0:NP_, :], agg[0:C, at], hproj[:, :],
                          start=True, stop=True, skip_group_check=True)
                        ins = M(bank(4 + c % 2, 1, j * 72 + C + HEADS)[0:NP_, :], y1[0:C, at], fpq[:, 0:1],
                                start=True, stop=True, skip_group_check=True)
                    ins.then_inc(sem("hup"), 1)
                    M(bank(6, n)[0:HEADS, :], prm[0:C, P_A2:P_A2 + HEADS], agg[0:C, cols(c)],
                      start=True, stop=True)
                    M(bank(7, n)[0:1, :], fpq[:, 1:2], y1[0:C, cols(c)], start=True, stop=True)\
                        .then_inc(sem("vq"), 1)
            for c in range(E.nc):
                pe.wait_ge(sem("wq_spread"), c + 1)
                if c >= 2:
                    pe.wait_ge(sem("wq_ev"), c - 1)
                nc.tensor.transpose(bank(c % 2, E.ch), wexp[0:E.ch, c % 2].rearrange("p a b -> p (a b)"),
                                    ident[0:E.ch, 0:E.ch]).then_inc(sem("wq_tr"), 1)

        def act_att_tables(act, E):
            for step in range(NCH + 2):
                if step < NCH:
                    act_back(act, 1, step)
                if 1 <= step <= NCH:
                    c = step - 1
                    n = chunk(c) * NP_
                    for k, (to, b) in enumerate(((agg, P_BL), (y1, P_BD))):
                        act.wait_ge(sem("proj"), 2 * c + k + 1)
                        A(to[0:C, cols(c)], bank(2 + k, n)[0:C, :], ACT.Identity, bias=prm[0:C, b:b + 1])\
                            .then_inc(sem("proj_ev"), 1)
                if step >= 2:
                    c = step - 2
                    act.wait_ge(sem("hup"), c + 1)
                    if c >= 2:
                        act.wait_ge(sem(f"table_out{c % 2}"), 16 * table_parts(1, c))
                    A(tabn[:, c % 2, 0:chunk(c) * ROW2].rearrange("p (a b) -> p a b", b=ROW2),
                      bank(4 + c % 2, chunk(c) * 72)[0:NP_, :].rearrange("p (a b) -> p a b", b=72)[:, :, 0:ROW2],
                      ACT.Copy).then_inc(sem("hup_ev"), 1)
            stage_first(act, E, 4, src_i)

        def dve_att_tables(dve, chain, E):
            for c in range(NCH):
                n = chunk(c) * NP_
                dve.wait_ge(sem("vq"), c + 1)
                V.tensor_scalar(vt[:, cols(c)], bank(6, n)[0:HEADS, :], prm[0:HEADS, P_BA:P_BA + 1], None,
                                ALU.add).then_inc(sem("vq_ev"), 1)
                V.tensor_scalar(row2[:, 0, cols(c)], bank(7, n)[0:1, :], prm[0:1, P_BF:P_BF + 1], None,
                                ALU.add).then_inc(sem("vq_ev"), 1)
            chain(V.memset(smax[:, :], -BIG))
            for c in range(E.nc + 1):
                if c < E.nc:
                    dve.wait_ge(sem("wq_in"), 16 * E.nc)
                    if c >= 2:
                        dve.wait_ge(sem("wq_tr"), c - 1)
                    wide = [E.ch, 4, WIN]
                    V.tensor_tensor(wexp[0:E.ch, c % 2], winq[0:E.ch, c, :].unsqueeze(1).to_broadcast(wide),
                                    m4[0:E.ch, :].unsqueeze(2).to_broadcast(wide), ALU.mult)\
                        .then_inc(sem("wq_spread"), 1)
                if c >= 1:
                    dve.wait_ge(sem("wq_tr"), c)
                    V.tensor_copy(wtq[:, (c - 1) * E.ch:c * E.ch], bank((c - 1) % 2, E.ch))\
                        .then_inc(sem("wq_ev"), 1)

        def sp_att_tables(sp, E):
            for c in range(NCH):
                sp.wait_ge(sem("hup_ev"), c + 1)
                sp.dma_start(att_tab[cols(c), :].rearrange("(i p) f -> p i f", p=NP_),
                             tabn[:, c % 2, 0:chunk(c) * ROW2].rearrange("p (a b) -> p a b", b=ROW2))\
                    .then_inc(sem(f"table_out{c % 2}"), 16)
            sp.wait_ge(sem("vq_ev"), 2 * NCH)
            sp.dma_start(q_tab[0:N, :].rearrange("n a -> a n"), row2[:, 0, :]).then_inc(sem("q_out"), 16)
            sp.dma_start(q_tab[N:N + WIN, :].rearrange("n a -> a n"), I["nought"][0:1, :])\
                .then_inc(sem("q_out"), 16)
            sp.dma_start(va_tab[N:N + WIN, :], I["nought"][:, 0:2 * HEADS]).then_inc(sem("q_out"), 16)

        def pool_att_tables(pool, E):
            pool.wait_ge(sem("q_out"), 48)
            for c in range(E.nc):
                nc.gpsimd.indirect_dma_start(
                    out=winq[0:E.ch, c, :], out_offset=None, in_=q_tab,
                    in_offset=bass.IndirectOffsetOnAxis(ap=base_i[0:E.ch, c:c + 1], axis=0))\
                    .then_inc(sem("wq_in"), 16)
            pool.wait_ge(sem("table_out0"), 16 * table_parts(1, NCH + NCH % 2))
            pool.wait_ge(sem("table_out1"), 16 * table_parts(1, NCH + 1 - NCH % 2))

        def act_signs(act, chain, E):
            act.wait_ge(sem("wq_ev"), E.nc)
            with chain.loop(E.rounds, 2) as i:
                for h in range(2):
                    act.wait_ge(sem(f"l_ready{h}"), i + 1)
                    A(ohs[:, h], onehot[:, half_tiles(i, h), :], ACT.Copy).then_inc(sem("oh_copy"), 1)
                    act.wait_ge(sem("oh_copy"), i * 2 + (h + 1))
                    A(msk[:, h], ohs[:, h], ACT.Copy, bias=-BIG, scale=BIG).then_inc(sem("mask"), 1)
                    act.wait_ge(sem("oh_tr"), i * 2 + (h + 1))
                    A(ohT[:, h, :], bank(h, HALF * WIN), ACT.Copy).then_inc(sem("oh_tr_ev"), 1)
                for h in range(2):
                    act.wait_ge(sem("z_ready"), i * 2 + (h + 1))
                    chain(A(zbuf[:, h, 1, :], zbuf[:, h, 0, :], ACT.Tanh))
                    A(sg[:, half_tiles(i, h)], zbuf[:, h, 1, :], ACT.Sign).then_inc(sem("sg_ready"), 1)
                    act.wait_ge(sem(f"su_ready{h}"), i + 1)
                    act.wait_ge(sem(f"stashed{h}"), i * 16 + 16)
                    stage_next(4, src_i, i, h)

        def pe_signs(pe, E):
            pe.wait_ge(sem("vq_ev"), 2 * NCH)
            pe.wait_ge(sem("wq_ev"), E.nc)
            pe.wait_ge(sem("hup_ev"), NCH)
            for h in range(2):
                pe.sem_inc(sem(f"l_ready{h}"), 1)
            pe.sem_inc(sem("l_max"), 1)
            with pe.Fori(0, E.rounds) as i:
                for h in range(2):
                    pe.wait_ge(sem("oh_copy"), i * 2 + (h + 1))
                    for q in range(2):
                        ins = nc.tensor.transpose(bank(h, TILE, q * TILE),
                                                  ohs[:, h, 4 * q:4 * q + 4, :].rearrange("p a b -> p (a b)"),
                                                  ident[:, :])
                    ins.then_inc(sem("oh_tr"), 1)
                for h in range(2):
                    pe.wait_ge(sem("oh_tr_ev"), i * 2 + (h + 1))
                    for q in range(2):
                        ins = M(bank(2 + h, 4, 4 * q), ohT[:, h, q * TILE:(q + 1) * TILE],
                                wtq[:, bass.ds(i * BODY + (h * HALF + 4 * q), 4)], start=True, stop=True,
                                skip_group_check=True)
                    ins.then_inc(sem("q_edge"), 1)
                for h in range(2):
                    pe.wait_ge(sem(f"l_ready{h}"), i + 2)
                    pe.wait_ge(sem("l_max"), i * 2 + (h + 1))
                    for k in range(HALF):
                        ins = nc.tensor.transpose(bank(4 + k // 4, TILE, (k % 4) * TILE), work[:, h, k, :],
                                                  ident[:, :])
                    ins.then_inc(sem("l_tr"), 1)
                    pe.wait_ge(sem("max_spread"), i * 2 + (h + 1))
                    M(bank(6 + h, HALF * WIN)[0:HEADS, :], kmask[:, :],
                      mxe[:, h].rearrange("p a b -> p (a b)"), start=True, stop=True)\
                        .then_inc(sem("max_row"), 1)

        def dve_signs(dve, chain, E):
            with chain.loop(E.rounds, 2 * HALF) as i:
                for h in range(2):
                    dve.wait_ge(sem(f"landed{h}"), E.landed(4, i))
                    dve.wait_ge(sem("q_edge"), i * 2 + (h + 1))
                    V.tensor_tensor(zbuf[:, h, 0, :], bank(2 + h, HALF), rows[:, h, :, C + HEADS], ALU.add)\
                        .then_inc(sem("z_ready"), 1)
                    dve.wait_ge(sem("sg_ready"), i * 2 + (h + 1))
                    at = su[:, half_tiles(i, h), :]
                    V.tensor_tensor(at, rows[:, h, :, C:C + HEADS],
                                    sg[:, half_tiles(i, h)].unsqueeze(2).to_broadcast([TILE, HALF, HEADS]),
                                    ALU.mult).then_inc(sem(f"su_ready{h}"), 1)
                    dve.wait_ge(sem(f"su_ready{h}"), i + 1)
                    dve.wait_ge(sem("mask"), i * 2 + (h + 1))
                    wide = [TILE, HALF, HEADS, WIN]
                    V.tensor_tensor(work[:, h].rearrange("p a (k j) -> p a k j", j=WIN),
                                    at.unsqueeze(3).to_broadcast(wide),
                                    msk[:, h].unsqueeze(2).to_broadcast(wide), ALU.add)\
                        .then_inc(sem(f"l_ready{h}"), 1)
                for h in range(2):
                    dve.wait_ge(sem("l_tr"), i * 2 + (h + 1))
                    V.tensor_reduce(mxg[:, h, :], ps[:, 4 * BANK:6 * BANK].rearrange("p (a b) -> p a b", b=TILE),
                                    AX, ALU.max).then_inc(sem("l_max"), 1)
                    dve.wait_ge(sem("l_max"), i * 2 + (h + 2))
                    wide = [128, HALF, WIN]
                    V.tensor_tensor(mxe[:, h], mxg[:, h, :].unsqueeze(2).to_broadcast(wide),
                                    jmask[:, :].unsqueeze(1).to_broadcast(wide), ALU.mult)\
                        .then_inc(sem("max_spread"), 1)
                for h in range(2):
                    dve.reg_load(dve_regs, base_row[:, half_tiles(i, h)])
                    base = [dve.snap(r, min_val=0, max_val=N) for r in dve_regs]
                    dve.wait_ge(sem("max_row"), i * 2 + (h + 1))
                    for k in range(HALF):
                        at = smax[:, bass.ds(base[k], WIN)]
                        chain(V.tensor_tensor(at, at, bank(6 + h, WIN, k * WIN)[0:HEADS, :], ALU.max))
            for c in range(NCH):
                at = smax[:, cols(c)]
                chain(V.tensor_tensor(at, at, vt[:, cols(c)], ALU.add))
                V.scalar_tensor_tensor(out=at, in0=at, scalar=NEG_SLOPE, in1=at, op0=ALU.mult, op1=ALU.max)\
                    .then_inc(sem("am_ready"), 1)

        def sp_signs(sp, E):
            with sp.Fori(0, E.rounds) as i:
                for h in range(2):
                    sp.wait_ge(sem(f"landed{h}"), E.landed(4, i))
                    sp.dma_start(stash[bass.ds(i * (2 * TILE) + h * TILE, TILE), :, :], rows[:, h, :, 0:ROW2])\
                        .then_inc(sem(f"stashed{h}"), 16)

        def pe_va(pe, E):
            for c in range(NCH):
                pe.wait_ge(sem("am_ready"), c + 1)
                if c >= 2:
                    pe.wait_ge(sem("va_ev"), c - 1)
                for j, t in enumerate(tiles(c)):
                    for k, of in enumerate((vt, smax)):
                        ins = nc.tensor.transpose(bank(c % 2, HEADS, (2 * j + k) * HEADS)[0:NP_, :],
                                                  of[:, t * NP_:(t + 1) * NP_], ident[0:HEADS, 0:HEADS])
                ins.then_inc(sem("va_tr"), 1)
            for c in range(E.nc):
                pe.wait_ge(sem("wv_spread"), c + 1)
                if c >= 2:
                    pe.wait_ge(sem("wv_ev"), 2 * (c - 1))
                for f in range(2 * HEADS):
                    ins = nc.tensor.transpose(bank(2 + 2 * (c % 2) + f // 4, E.ch, (f % 4) * E.ch),
                                              work[0:E.ch, c % 2, f, :], ident[0:E.ch, 0:E.ch])
                    if f % 4 == 3:
                        ins.then_inc(sem("wv_tr"), 1)

        def act_va(act, E):
            act.wait_ge(sem("table_out0"), 16 * table_parts(1, NCH + NCH % 2))
            act.wait_ge(sem("table_out1"), 16 * table_parts(1, NCH + 1 - NCH % 2))
            for c in range(NCH):
                act.wait_ge(sem("va_tr"), c + 1)
                if c >= 2:
                    act.wait_ge(sem(f"table_out{c % 2}"), 16 * table_parts(2, c))
                A(tabn[:, c % 2, 0:chunk(c) * 2 * HEADS], bank(c % 2, chunk(c) * 2 * HEADS)[0:NP_, :], ACT.Copy)\
                    .then_inc(sem("va_ev"), 1)
            for c in range(E.nc):
                for g in range(2):
                    act.wait_ge(sem("wv_tr"), 2 * c + g + 1)
                    A(wtv[:, c * E.ch:(c + 1) * E.ch, 4 * g:4 * g + 4].rearrange("p t f -> p f t"),
                      bank(2 + 2 * (c % 2) + g, 4 * E.ch).rearrange("p (f t) -> p f t", f=4), ACT.Copy)\
                        .then_inc(sem("wv_ev"), 1)

        def dve_va(dve, chain, E):
            dve.wait_ge(sem("wv_in"), 16 * E.nc)
            for c in range(E.nc):
                if c >= 2:
                    dve.wait_ge(sem("wv_tr"), 2 * (c - 1))
                wide = [E.ch, 4, WIN]
                for f in range(2 * HEADS):
                    ins = V.tensor_tensor(
                        work[0:E.ch, c % 2, f, :].rearrange("p (a b) -> p a b", b=WIN),
                        winv[0:E.ch, c, :].rearrange("p (j f) -> p f j", f=2 * HEADS)[:, f:f + 1, :].to_broadcast(wide),
                        m4[0:E.ch, :].unsqueeze(2).to_broadcast(wide), ALU.mult)
                ins.then_inc(sem("wv_spread"), 1)

        def sp_va(sp, E):
            for c in range(NCH):
                sp.wait_ge(sem("va_ev"), c + 1)
                sp.dma_start(va_tab[cols(c), :].rearrange("(i p) f -> p i f", p=NP_),
                             tabn[:, c % 2, 0:chunk(c) * 2 * HEADS].rearrange("p (a b) -> p a b", b=2 * HEADS))\
                    .then_inc(sem(f"table_out{c % 2}"), 16)

        def pool_va(pool, E):
            pool.wait_ge(sem("table_out0"), 16 * table_parts(2, NCH + NCH % 2))
            pool.wait_ge(sem("table_out1"), 16 * table_parts(2, NCH + 1 - NCH % 2))
            for c in range(E.nc):
                nc.gpsimd.indirect_dma_start(
                    out=winv[0:E.ch, c, :], out_offset=None, in_=va_tab,
                    in_offset=bass.IndirectOffsetOnAxis(ap=base_i[0:E.ch, c:c + 1], axis=0))\
                    .then_inc(sem("wv_in"), 16)

        def sp_soft(sp, E):
            for h in range(2):
                sp.wait_ge(sem(f"stashed{h}"), 16 * E.rounds)
            with sp.Fori(0, E.rounds) as i:
                for h in range(2):
                    sp.wait_ge(sem(f"msg_ready{h}"), i + 1)
                    sp.dma_start(rows[:, h, :, 0:ROW2], stash[bass.ds(i * (2 * TILE) + h * TILE, TILE), :, :])\
                        .then_inc(sem(f"fetched{h}"), 16)

        def pe_soft(pe, E):
            pe.wait_ge(sem("wv_ev"), 2 * E.nc)
            pe_clear(C + HEADS)
            for h in range(2):
                pe.sem_inc(sem(f"msg_ready{h}"), 1)
                pe.sem_inc(sem(f"scattered6{h}"), 1)
            pe.sem_inc(sem("va_taken"), 1)
            with pe.Fori(0, E.rounds) as i:
                for h in range(2):
                    pe.wait_ge(sem("oh2_copy"), i * 2 + (h + 1))
                    pe.wait_ge(sem("va_taken"), i * 2 + (h + 1))
                    for q in range(2):
                        ins = nc.tensor.transpose(bank(7, TILE, q * TILE),
                                                  ohs[:, h, 4 * q:4 * q + 4, :].rearrange("p a b -> p (a b)"),
                                                  ident[:, :])
                    ins.then_inc(sem("oh2_tr"), 1)
                    pe.wait_ge(sem("oh2_tr_ev"), i * 2 + (h + 1))
                    for q in range(2):
                        ins = M(bank(7, 32, 32 * q), ohT[:, h, q * TILE:(q + 1) * TILE],
                                wtv[:, bass.ds(i * BODY + (h * HALF + 4 * q), 4), :].rearrange("p a b -> p (a b)"),
                                start=True, stop=True, skip_group_check=True)
                    ins.then_inc(sem("va_edge"), 1)
                for h in range(2):
                    at = pe_windows(pe, i, h)
                    pe.wait_ge(sem(f"msg_ready{h}"), i + 2)
                    for k in range(HALF):
                        ins = pe_scatter(at[k], C + HEADS, work[:, h, k, 0:C + HEADS], onehot_tile(i, h, k))
                    ins.then_inc(sem(f"scattered6{h}"), 1)
            M(bank(7, 8)[0:1, :], zeros[:, 0:1], zeros[:, 0:8], start=True, stop=True)\
                .then_inc(sem("summed"), 1)
            pe.wait_ge(sem("sums_ready"), 5 * NB)
            for c in range(NCH):
                if c >= 2:
                    pe.wait_ge(sem("o_ev"), c - 1)
                for j, t in enumerate(tiles(c)):
                    ins = nc.tensor.transpose(bank(c % 2, C + HEADS, j * (C + HEADS))[0:NP_, :],
                                              agg[0:C + HEADS, t * NP_:(t + 1) * NP_],
                                              ident[0:C + HEADS, 0:C + HEADS])
                ins.then_inc(sem("o_tr"), 1)

        def act_soft(act, E):
            with act.Fori(0, E.rounds) as i:
                for h in range(2):
                    A(ohs[:, h], onehot[:, half_tiles(i, h), :], ACT.Copy).then_inc(sem("oh2_copy"), 1)
                    act.wait_ge(sem("oh2_tr"), i * 2 + (h + 1))
                    A(ohT[:, h, :], bank(7, HALF * WIN), ACT.Copy).then_inc(sem("oh2_tr_ev"), 1)
                for h in range(2):
                    act.wait_ge(sem("d_ready"), i * 2 + (h + 1))
                    act.wait_ge(sem(f"scattered6{h}"), i + 1)
                    A(work[:, h, :, C:C + HEADS], abuf[:, h, 2], ACT.Exp).then_inc(sem("w_ready"), 1)

        def dve_soft(dve, chain, E):
            with chain.loop(E.rounds, 2 * 3) as i:
                for h in range(2):
                    dve.wait_ge(sem("va_edge"), i * 2 + (h + 1))
                    va = bank(7, HALF * 2 * HEADS).rearrange("p (t f) -> p t f", f=2 * HEADS)
                    V.tensor_copy(abuf[:, h, 1], va[:, :, HEADS:2 * HEADS])
                    V.tensor_tensor(abuf[:, h, 0], va[:, :, 0:HEADS], su[:, half_tiles(i, h), :], ALU.add)\
                        .then_inc(sem("va_taken"), 1)
                    dve.wait_ge(sem("va_taken"), i * 2 + (h + 2))
                    chain(V.scalar_tensor_tensor(out=abuf[:, h, 2], in0=abuf[:, h, 0], scalar=NEG_SLOPE,
                                                 in1=abuf[:, h, 0], op0=ALU.mult, op1=ALU.max))
                    chain(V.tensor_tensor(abuf[:, h, 2], abuf[:, h, 2], abuf[:, h, 1], ALU.subtract))
                    V.tensor_scalar(abuf[:, h, 2], abuf[:, h, 2], 0.0, None, ALU.min)\
                        .then_inc(sem("d_ready"), 1)
                for h in range(2):
                    dve.wait_ge(sem("w_ready"), i * 2 + (h + 1))
                    chain(V.tensor_tensor(abuf[:, h, 0], work[:, h, :, C:C + HEADS],
                                          sg[:, half_tiles(i, h)].unsqueeze(2).to_broadcast([TILE, HALF, HEADS]),
                                          ALU.mult))
                    dve.wait_ge(sem(f"fetched{h}"), i * 16 + 16)
                    wide = [TILE, HALF, HEADS, HD]
                    V.tensor_tensor(work[:, h, :, 0:C].rearrange("p a (k d) -> p a k d", d=HD),
                                    rows[:, h, :, 0:C].rearrange("p a (k d) -> p a k d", d=HD),
                                    abuf[:, h, 0].unsqueeze(3).to_broadcast(wide), ALU.mult)\
                        .then_inc(sem(f"msg_ready{h}"), 1)
            dve_sums(dve, chain, 4, C + HEADS)
            for c in range(NCH):
                n = chunk(c)
                dve.wait_ge(sem("o_tr"), c + 1)
                got = bank(c % 2, n * (C + HEADS))[0:NP_, :].rearrange("p (a b) -> p a b", b=C + HEADS)
                den = tabn[:, 0, 0:n * HEADS].rearrange("p (a b) -> p a b", b=HEADS)
                y = yn[:, c * CH:c * CH + n, :]
                chain(V.tensor_scalar(den, got[:, :, C:C + HEADS], 1e-16, None, ALU.max))
                chain(V.reciprocal(den, den))
                V.tensor_tensor(y.rearrange("p a (k d) -> p a k d", d=HD),
                                got[:, :, 0:C].rearrange("p a (k d) -> p a k d", d=HD),
                                den.unsqueeze(3).to_broadcast([NP_, n, HEADS, HD]), ALU.mult)\
                    .then_inc(sem("o_ev"), 1)
                dve.wait_ge(sem("o_ev"), c + 1)
                chain(V.tensor_tensor(y, y, xn[:, c * CH:c * CH + n, :], ALU.add))
            dve_norm(dve, chain, 2)

        PAIRS = [(c, j) for c in range(NCH) for j in range(0, chunk(c), 2)]

        def pe_rel(pe, E):
            for step in range(NCH + 1):
                if step < NCH:
                    pe_back(pe, 2, step)
                if step >= 1:
                    c = step - 1
                    pe.wait_ge(sem("back_ev"), 2 * NCH + c + 1)
                    for n, (cc, j) in enumerate(PAIRS):
                        if cc != c:
                            continue
                        if n >= 4:
                            pe.wait_ge(sem("rel_ev"), n - 3)
                        for k in range(min(2, chunk(c) - j)):
                            t = c * CH + j + k
                            ins = M(bank(2 + n % 4, RELS * C, k * RELS * C)[0:NP_, :],
                                    xt[:, t * NP_:(t + 1) * NP_], wrel[:, :, :].rearrange("p r c -> p (r c)"),
                                    start=True, stop=True, skip_group_check=True)
                        ins.then_inc(sem("rel_mm"), 1)
            pe.wait_ge(sem("rel_ev"), len(PAIRS))
            pe_clear(C)
            for h in range(2):
                pe.sem_inc(sem(f"scattered5{h}"), 1)
            with pe.Fori(0, E.rounds) as i:
                for h in range(2):
                    at = pe_windows(pe, i, h)
                    pe.wait_ge(sem("weighted"), i * 2 + (h + 1))
                    pe.wait_ge(sem(f"landed{h}"), E.landed(5, i))
                    for k in range(HALF):
                        ins = pe_scatter(at[k], C, rows[:, h, k, 0:C], msk[:, h, k, :])
                    ins.then_inc(sem(f"scattered5{h}"), 1)
            M(bank(7, 8)[0:1, :], zeros[:, 0:1], zeros[:, 0:8], start=True, stop=True)\
                .then_inc(sem("summed"), 1)
            pe.wait_ge(sem("sums_ready"), 6 * NB)
            for c in range(NCH):
                pe.wait_ge(sem("y_ready"), c + 1)
                if c >= 2:
                    pe.wait_ge(sem("y_ev"), c - 1)
                for j, t in enumerate(tiles(c)):
                    ins = nc.tensor.transpose(bank(c % 2, C, j * C)[0:NP_, :], y1[0:C, t * NP_:(t + 1) * NP_],
                                              ident[0:C, 0:C])
                ins.then_inc(sem("y_tr"), 1)

        def act_rel(act, E):
            act_norm(act, 2)
            for step in range(NCH + 1):
                if step < NCH:
                    act_back(act, 2, step)
                if step >= 1:
                    c = step - 1
                    if c >= 2:
                        act.wait_ge(sem(f"table_out{c % 2}"), 16 * table_parts(3, c))
                    for n, (cc, j) in enumerate(PAIRS):
                        if cc == c:
                            m = min(2, chunk(c) - j) * RELS * C
                            act.wait_ge(sem("rel_mm"), n + 1)
                            A(tabn[:, c % 2, j * RELS * C:j * RELS * C + m], bank(2 + n % 4, m)[0:NP_, :],
                              ACT.Copy).then_inc(sem("rel_ev"), 1)
            stage_first(act, E, 5, rel_i)
            act.wait_ge(sem("bn_mean"), 1)
            A(y1[0:C, 0:N], xt[:, :], ACT.Square, bias=bnst[:, 1:2], accum_out=bnst[:, 2:3])\
                .then_inc(sem("bn_square"), 1)
            act.wait_ge(sem("bn_var"), 1)
            A(bnst[:, 4:5], bnst[:, 3:4], ACT.Sqrt).then_inc(sem("bn_sd"), 1)
            with act.Fori(0, E.rounds) as i:
                for h in range(2):
                    act.wait_ge(sem(f"scattered5{h}"), i + 2)
                    stage_next(5, rel_i, i, h)
            for step in range(NCH + 2):
                if step < NCH:
                    c = step
                    act.wait_ge(sem("hbn"), c + 1)
                    A(y1[0:C, cols(c)], y1[0:C, cols(c)], ACT.Relu, bias=bnst[:, 7:8])\
                        .then_inc(sem("relu_out"), 1)
                if step >= 2:
                    c = step - 2
                    act.wait_ge(sem("y_tr"), c + 1)
                    A(yn[:, c * CH:c * CH + chunk(c), :].rearrange("p a b -> p (a b)"),
                      bank(c % 2, chunk(c) * C)[0:NP_, :], ACT.Copy).then_inc(sem("y_ev"), 1)
            act_norm(act, 3)

        def dve_rel(dve, chain, E):
            dve.wait_ge(sem("back_ev"), 3 * NCH)
            chain(V.tensor_reduce(bnst[:, 0:1], xt[:, :], AX, ALU.add))
            V.tensor_scalar(bnst[:, 1:2], bnst[:, 0:1], -1.0 / N, None, ALU.mult).then_inc(sem("bn_mean"), 1)
            dve.wait_ge(sem("bn_square"), 1)
            V.tensor_scalar(bnst[:, 3:4], bnst[:, 2:3], 1.0 / N, 1e-05, ALU.mult, ALU.add)\
                .then_inc(sem("bn_var"), 1)
            dve.wait_ge(sem("bn_sd"), 1)
            chain(V.reciprocal(bnst[:, 5:6], bnst[:, 4:5]))
            chain(V.tensor_tensor(bnst[:, 6:7], bnst[:, 5:6], prm[0:C, P_GAMMA:P_GAMMA + 1], ALU.mult))
            V.scalar_tensor_tensor(out=bnst[:, 7:8], in0=bnst[:, 1:2], scalar=bnst[:, 6:7],
                                   in1=prm[0:C, P_BETA:P_BETA + 1], op0=ALU.mult, op1=ALU.add)\
                .then_inc(sem("bn_ready"), 1)
            with dve.Fori(0, E.rounds) as i:
                for h in range(2):
                    dve.wait_ge(sem(f"scattered5{h}"), i + 1)
                    V.tensor_tensor(msk[:, h], onehot[:, half_tiles(i, h), :],
                                    wgt[:, half_tiles(i, h)].unsqueeze(2).to_broadcast([TILE, HALF, WIN]),
                                    ALU.mult).then_inc(sem("weighted"), 1)
            dve_sums(dve, chain, 5, C)
            dve.wait_ge(sem("bn_ready"), 1)
            dve.wait_ge(sem("sums_ready"), 6 * NB)
            for step in range(NCH + 1):
                if step < NCH:
                    c = step
                    V.scalar_tensor_tensor(out=y1[0:C, cols(c)], in0=xt[:, cols(c)], scalar=bnst[:, 6:7],
                                           in1=agg[0:C, cols(c)], op0=ALU.mult, op1=ALU.add)\
                        .then_inc(sem("hbn"), 1)
                if step >= 1:
                    c = step - 1
                    dve.wait_ge(sem("relu_out"), c + 1)
                    V.tensor_tensor(y1[0:C, cols(c)], y1[0:C, cols(c)], xt[:, cols(c)], ALU.add)\
                        .then_inc(sem("y_ready"), 1)
            dve_norm(dve, chain, 3, lambda part: (sem("y_ev"), (4, NCH)[part]))

        def sp_rel(sp, E):
            for c in range(NCH):
                sp.wait_ge(sem("rel_ev"), sum(1 for cc, _ in PAIRS if cc <= c))
                for r in range(RELS):
                    sp.dma_start(
                        rel_tab[r * N + cols(c).start:r * N + cols(c).stop, :].rearrange("(i p) f -> p i f", p=NP_),
                        tabn[:, c % 2, 0:chunk(c) * RELS * C].rearrange("p (a b) -> p a b", b=RELS * C)
                        [:, :, r * C:(r + 1) * C]).then_inc(sem(f"table_out{c % 2}"), 16)

        def pool_rel(pool, E):
            pool.wait_ge(sem("table_out0"), 16 * table_parts(3, NCH + NCH % 2))
            pool.wait_ge(sem("table_out1"), 16 * table_parts(3, NCH + 1 - NCH % 2))
            pool_gather(pool, E, 5, rel_tab, C)

        def sp_out(sp):
            for part, (a, b) in enumerate(PARTS):
                sp.wait_ge(sem("xn_ready"), 7 + part)
                sp.dma_start(out[a * NP_:b * NP_, :].rearrange("(i p) f -> p i f", p=NP_), xn[:, a:b, :])\
                    .then_inc(sem("out_done"), 16)
            sp.wait_ge(sem("out_done"), 32)

        scratch = onehot[:, :, :].rearrange("p t j -> p (t j)")
        TG = T_GIVEN
        blk, member, rank, place = (scratch[:, k * TG:(k + 1) * TG] for k in range(4))
        blk_i = scratch[:, 4 * TG:5 * TG].bitcast(I32)
        place_i = scratch[:, 5 * TG:6 * TG].bitcast(I32)
        rest = scratch[:, 6 * TG:]
        RECORD = 4 + FE
        rec = rest[:, 0:HALF * RECORD].rearrange("p (k f) -> p k f", f=RECORD)
        rec_i = rest[:, 0:HALF * RECORD].bitcast(I32).rearrange("p (k f) -> p k f", f=RECORD)
        empty = rest[:, 320:320 + HALF * RECORD].rearrange("p (k f) -> p k f", f=RECORD)
        empty_i = rest[:, 320:320 + HALF * RECORD].bitcast(I32).rearrange("p (k f) -> p k f", f=RECORD)
        place_st = rest[:, 640:640 + HALF].bitcast(I32)
        lower = rest[:, 704:704 + 128]
        at_blk, first, held, before, full = (rest[:, 840 + k:841 + k] for k in range(5))
        full_i = rest[:, 848:849].bitcast(I32)
        spare = rest[:, 849:850]
        attr_s = rest[0:FE, 1024:1024 + HALF * TILE]
        dst_f = rest[:, 2048:2048 + T_SORTED]

        def dve_sort(dve, chain):
            dve.wait_ge(sem("edges_in"), 64)
            chain(V.memset(empty, 0.0))
            V.memset(empty_i[:, :, 1:2], FAR).then_inc(sem("empty_ready"), 1)
            chain(V.tensor_scalar(lower, iota_f[:, :], pidx_f[:, 0:1], None, ALU.is_gt))
            chain(V.tensor_scalar(blk_i, dst_i[:, 0:TG], WIN.bit_length() - 1, None, ALU.logical_shift_right))
            chain(V.tensor_copy(blk, blk_i))
            chain(V.memset(place, 0.0))
            chain(V.memset(rest[:, 840:850], 0.0))
            with chain.loop(BLOCKS, 13) as i:
                chain(V.tensor_scalar(member, blk, at_blk, None, ALU.is_equal))
                chain(V.tensor_tensor_scan(rank, member, member, 0.0, ALU.add, ALU.bypass))
                V.tensor_copy(held, rank[:, TG - 1:TG]).then_inc(sem("held"), 1)
                dve.wait_ge(sem("held_sums"), i + 1)
                chain(V.tensor_scalar(before, bank(0, 1), first, -1.0, ALU.add, ALU.add))
                chain(V.tensor_scalar(full, bank(0, 1, 1), float(TILE - 1), None, ALU.add))
                chain(V.tensor_scalar(rank, rank, before, None, ALU.add))
                chain(V.tensor_tensor(rank, rank, member, ALU.mult))
                chain(V.tensor_tensor(place, place, rank, ALU.add))
                chain(V.tensor_copy(full_i, full))
                chain(V.tensor_scalar(full_i, full_i, 7, None, ALU.logical_shift_right))
                chain(V.tensor_scalar(full_i, full_i, 7, None, ALU.logical_shift_left))
                chain(V.tensor_copy(full, full_i))
                chain(V.tensor_tensor(first, first, full, ALU.add))
                chain(V.tensor_scalar(at_blk, at_blk, 1.0, None, ALU.add))
            chain(V.tensor_scalar(spare, pidx_f[:, 0:1], float(T_SORTED * TILE), None, ALU.add))
            chain(V.tensor_scalar(member, blk, float(FAR // WIN), spare, ALU.is_equal, ALU.mult))
            chain(V.tensor_tensor(place, place, member, ALU.add))
            V.tensor_copy(place_i, place).then_inc(sem("places"), 1)
            E = ordered
            for c in range(E.nc):
                dve.wait_ge(sem("dst_tr"), c + 1)
                V.tensor_copy(dst_tm[0:E.ch, c, :], bank(3 + c % 2, TILE)[0:E.ch, :])\
                    .then_inc(sem("dst_tr_ev"), 1)
            dve.wait_ge(sem("dst_tr_ev"), E.nc)
            dve_min_max(dve, chain, E)

        def pe_sort(pe):
            pe.wait_ge(sem("empty_ready"), 1)
            with pe.Fori(0, BLOCKS) as i:
                pe.wait_ge(sem("held"), i + 1)
                M(bank(0, 1), lower, held, start=True, stop=True, skip_group_check=True)
                M(bank(0, 1, 1), ones[:, :], held, start=True, stop=True, skip_group_check=True)\
                    .then_inc(sem("held_sums"), 1)
            with pe.Fori(0, T_SORTED // HALF) as i:
                pe.wait_ge(sem("rec_back"), i * 16 + 16)
                for k in range(HALF):
                    ins = nc.tensor.transpose(bank(1 + k // 4, TILE, (k % 4) * TILE)[0:FE, :],
                                              rec[:, k, 4:RECORD], ident[:, :])
                ins.then_inc(sem("attr_tr"), 1)
            for c in range(ordered.nc):
                pe.wait_ge(sem("dst_back"), 1)
                if c >= 2:
                    pe.wait_ge(sem("dst_tr_ev"), c - 1)
                nc.tensor.transpose(bank(3 + c % 2, TILE)[0:ordered.ch, :],
                                    dst_f[:, c * ordered.ch:(c + 1) * ordered.ch], ident[:, :])\
                    .then_inc(sem("dst_tr"), 1)

        def act_sort(act):
            act.wait_ge(sem("consts"), 8)
            act.wait_ge(sem("edges_in"), 64)
            act.wait_ge(sem("places"), 1)
            act.sem_inc(sem("rec_free"), 1)
            with act.Fori(0, T_GIVEN // HALF) as i:
                act.wait_ge(sem("rec_free"), i + 1)
                eight = bass.ds(i * HALF, HALF)
                A(place_st, place_i[:, eight], ACT.Copy).then_inc(sem("rec_cols"), 1)
                for f, of in enumerate((src_i, dst_i, rel_i)):
                    A(rec_i[:, :, f], of[:, eight], ACT.Copy).then_inc(sem("rec_cols"), 1)
                A(rec[:, :, 3], wgt[:, eight], ACT.Copy).then_inc(sem("rec_cols"), 1)
            with act.Fori(0, T_SORTED // HALF) as i:
                act.wait_ge(sem("rec_back"), i * 16 + 16)
                eight = bass.ds(i * HALF, HALF)
                for f, to in enumerate((src_i, dst_i, rel_i)):
                    A(to[:, eight], rec_i[:, :, f], ACT.Copy)
                A(dst_f[:, eight], rec_i[:, :, 1], ACT.Copy)
                A(wgt[:, eight], rec[:, :, 3], ACT.Copy)
                act.wait_ge(sem("attr_tr"), i + 1)
                act.wait_ge(sem("attr_stored"), i * 16 + 16)
                A(attr_s, ps[0:FE, BANK:3 * BANK], ACT.Copy).then_inc(sem("attr_back"), 1)
            act.wait_ge(sem("attr_back"), T_SORTED // HALF + 1)
            act.wait_ge(sem("attr_stored"), 16 * (T_SORTED // HALF + 1))
            act.sem_inc(sem("dst_back"), 1)

        def sp_sort(sp):
            sp.wait_ge(sem("empty_ready"), 1)
            with sp.Fori(0, T_SORTED // HALF + 1) as i:
                sp.dma_start(records[bass.ds(i * (HALF * TILE), HALF * TILE), :]
                             .rearrange("(k p) f -> p k f", p=TILE), empty).then_inc(sem("emptied"), 16)
            with sp.Fori(0, T_GIVEN // HALF) as i:
                sp.wait_ge(sem("rec_free"), i + 1)
                sp.dma_start(rec[:, :, 4:RECORD], I["attr_r"][bass.ds(i * (HALF * TILE), HALF * TILE), :]
                             .rearrange("(k p) f -> p k f", p=TILE)).then_inc(sem("rec_attr"), 16)
            sp.wait_ge(sem("rec_free"), T_GIVEN // HALF + 1)
            sp.sem_inc(sem("attr_back"), 1)
            sp.sem_inc(sem("attr_stored"), 16)
            with sp.Fori(0, T_SORTED // HALF) as i:
                at = sp.snap(i * (HALF * TILE), min_val=0, max_val=(T_SORTED - HALF) * TILE)
                sp.wait_ge(sem("attr_back"), i + 1)
                sp.dma_start(rec, records[bass.ds(at, HALF * TILE), :]
                             .rearrange("(k p) f -> p k f", p=TILE)).then_inc(sem("rec_back"), 16)
                sp.wait_ge(sem("attr_back"), i + 2)
                sp.sem_inc(sem("store_started"), 1)
                sp.dma_start(attr_sorted[:, bass.ds(at, HALF * TILE)], attr_s)\
                    .then_inc(sem("attr_stored"), 16)
            sp.wait_ge(sem("attr_stored"), 16 * (T_SORTED // HALF + 1))

        def pool_sort(pool):
            pool.wait_ge(sem("emptied"), 16 * (T_SORTED // HALF + 1))
            with pool.Fori(0, T_GIVEN // HALF) as i:
                pool.wait_ge(sem("rec_attr"), i * 16 + 16)
                pool.wait_ge(sem("rec_cols"), i * 5 + 5)
                pool.sem_inc(sem("gather_started"), 1)
                for k in range(HALF):
                    nc.gpsimd.indirect_dma_start(
                        out=records, out_offset=bass.IndirectOffsetOnAxis(ap=place_st[:, k:k + 1], axis=0),
                        in_=rec[:, k, :], in_offset=None).then_inc(sem("scattered_rec"), 16)
                pool.wait_ge(sem("scattered_rec"), i * (16 * HALF) + 16 * HALF)
                pool.sem_inc(sem("rec_free"), 1)

        def fits(eng):
            eng.wait_ge(sem("flag"), 1)
            return eng.value_load(flag[0:1, 0:1], min_val=0, max_val=1)

        def sp_passes(sp, E):
            sp_gin(sp, E)
            sp_edge(sp, E)
            sp_att_tables(sp, E)
            sp_signs(sp, E)
            sp_va(sp, E)
            sp_soft(sp, E)
            sp_rel(sp, E)
            sp_out(sp)

        def pool_passes(pool, E):
            pool_gin(pool, E)
            pool_edge(pool, E)
            pool_att_tables(pool, E)
            pool_gather(pool, E, 4, att_tab, ROW2)
            pool_va(pool, E)
            pool_rel(pool, E)

        def act_passes(act, E):
            act_gin(act, E)
            act_edge(act, E)
            act_att_tables(act, E)
            act_signs(act, Chain(act, sem("act")), E)
            act_va(act, E)
            act_soft(act, E)
            act_rel(act, E)

        def dve_passes(dve, chain, E):
            dve_edges(dve, chain, E)
            dve_gin(dve, chain, E)
            dve_edge(dve, chain, E)
            dve_att_tables(dve, chain, E)
            dve_signs(dve, chain, E)
            dve_va(dve, chain, E)
            dve_soft(dve, chain, E)
            dve_rel(dve, chain, E)

        def pe_passes(pe, E):
            pe_edges(pe, E)
            pe_gin(pe, E)
            pe_edge(pe, E)
            pe_att_tables(pe, E)
            pe_signs(pe, E)
            pe_va(pe, E)
            pe_soft(pe, E)
            pe_rel(pe, E)

        block = ctx.enter_context(nc.Block())

        @block.sync
        def _(sp):
            sp_start(sp)
            with sp.If(fits(sp)):
                sp_passes(sp, given)
            with sp.Else():
                sp_sort(sp)
                sp_passes(sp, ordered)

        @block.gpsimd
        def _(pool):
            pool_start(pool)
            with pool.If(fits(pool)):
                pool_passes(pool, given)
            with pool.Else():
                pool_sort(pool)
                pool_passes(pool, ordered)

        @block.scalar
        def _(act):
            with act.If(fits(act)):
                act_passes(act, given)
            with act.Else():
                act_sort(act)
                act_passes(act, ordered)

        @block.vector
        def _(dve):
            nonlocal dve_regs
            dve_regs = [dve.alloc_register(f"base{k}") for k in range(HALF)]
            chain = Chain(dve, sem("dve"))
            dve_start(dve, chain)
            steps = chain.n
            with dve.If(fits(dve)):
                dve_passes(dve, chain, given)
            with dve.Else():
                chain.n = steps
                dve_sort(dve, chain)
                dve_passes(dve, chain, ordered)

        @block.tensor
        def _(pe):
            nonlocal pe_regs
            pe_regs = [pe.alloc_register(f"window{k}") for k in range(HALF)]
            pe_start(pe)
            with pe.If(fits(pe)):
                pe_passes(pe, given)
            with pe.Else():
                pe_sort(pe)
                pe_passes(pe, ordered)


def lay_out(inputs):
    import numpy as np

    a = {k: np.asarray(v) for k, v in inputs.items()}
    pad = T_GIVEN * TILE - E_EDGES

    def tiled(v, fill):
        return np.ascontiguousarray(np.pad(v, (0, pad), constant_values=fill).reshape(T_GIVEN, TILE).T)

    dst = np.pad(a["dst"], (0, pad), constant_values=FAR).reshape(4, T_GIVEN // 4, TILE)
    prm = np.zeros((128, P_COLS), np.float32)
    for at, name in ((P_B1, "L0_gnn_b1"), (P_G1, "L0_gnn_g1"), (P_BE1, "L0_gnn_be1"), (P_B2, "L0_gnn_b2"),
                     (P_G2, "L0_gnn_g2"), (P_BE2, "L0_gnn_be2"), (P_BNG, "L0_gnn_bn_g"),
                     (P_BNB, "L0_gnn_bn_be")):
        prm[0:C, at:at + 3] = a[name].T
    prm[0:C, P_EPS:P_EPS + 3] = a["L0_gnn_eps"][None, :]
    prm[:, P_L1B3] = a["L1_gnn_b3"]
    for at, name in ((P_L1B4, "L1_gnn_b4"), (P_BL, "L2_gnn_bl"), (P_BD, "L2_gnn_bd"),
                     (P_GAMMA, "L3_gnn_gamma"), (P_BETA, "L3_gnn_beta")):
        prm[0:C, at] = a[name]
    prm[:, P_BA], prm[:, P_BF] = a["L2_gnn_ba"][0], a["L2_gnn_bf"][0]
    prm[0:C, P_WF:P_WF + 3] = a["L2_gnn_Wf"].reshape(3, C).T
    for k in range(HEADS):
        prm[k * HD:(k + 1) * HD, P_A1 + k] = a["L2_gnn_Wa"][0:HD, 0]
        prm[k * HD:(k + 1) * HD, P_A2 + k] = a["L2_gnn_Wa"][HD:2 * HD, 0]
    got = {
        "x": a["x"], "x_t": np.ascontiguousarray(a["x"].T), "params": prm,
        "src_e": tiled(a["src"], 0), "dst_e": tiled(a["dst"], FAR), "rel_e": tiled(a["edge_type_3"], 0),
        "wgt_e": tiled(a["edge_weight"], 0), "dst_t": np.ascontiguousarray(dst.transpose(1, 0, 2)),
        "attr_r": np.pad(a["edge_attr_32"], ((0, pad), (0, 0))),
        "attr_t": np.ascontiguousarray(np.pad(a["edge_attr_32"], ((0, pad), (0, 0))).T),
        "brow": np.concatenate([a["L1_gnn_b1"], a["L1_gnn_b2"]])[None, :],
        "nought": np.zeros((WIN, WIN), np.float32),
    }
    for name in ("L0_gnn_W1", "L0_gnn_W2", "L1_gnn_W1", "L1_gnn_W2", "L1_gnn_W3", "L1_gnn_W4",
                 "L2_gnn_Wl", "L2_gnn_Wd", "L3_gnn_weight"):
        got[name] = a[name]
    return got


def kernel(**inputs):
    import numpy as np
    import concourse.bacc as bacc
    from concourse.bass_utils import run_bass_kernel_spmd

    arrays = {f"in_{k}": v for k, v in lay_out(inputs).items()}
    nc = bacc.Bacc("TRN2", target_bir_lowering=False, num_devices=1)
    args = {k[3:]: nc.dram_tensor(k, v.shape, mybir.dt.from_np(v.dtype), kind="ExternalInput").ap()
            for k, v in arrays.items()}
    out = nc.dram_tensor("out", [N, C], F32, kind="ExternalOutput").ap()
    build(nc, args, out)
    got = run_bass_kernel_spmd(nc, [arrays], core_ids=[0])
    return np.asarray(got.results[0]["out"])
```

```python
from contextlib import ExitStack, contextmanager

import concourse.bass as bass
from concourse import mybir
from concourse.alu_op_type import AluOpType as ALU

F32 = mybir.dt.float32
I32 = mybir.dt.int32
BF16 = mybir.dt.bfloat16
ACT = mybir.ActivationFunctionType
AX = mybir.AxisListType.X

N = 3125
C = 64
E_EDGES = 53125
FE = 32
HID = 128
HEADS, HD = 4, 16
RELS = 3
TILE = 128
WIN = 32
NP_, NT = 125, 25
BANK = 512
STEP = BANK - WIN
NB = -(-N // STEP)
HALF = 8
BODY = 2 * HALF
T_GIVEN = -(-E_EDGES // (TILE * BODY)) * BODY
BLOCKS = -(-N // WIN)
T_SORTED = -(-(T_GIVEN + BLOCKS) // BODY) * BODY
CH = 4
NCH = -(-NT // CH)
ROW2 = C + 2 * HEADS + 2
FAR = 1 << 20
BIG = 1.0e30
NEG_SLOPE = 0.01
BN_C = 1.0 / (1.0 + 1e-05) ** 0.5
N_LOADS = 16
P_B1, P_G1, P_BE1, P_B2, P_G2, P_BE2, P_BNG, P_BNB, P_EPS = range(0, 27, 3)
P_L1B3, P_UNUSED, P_BL, P_BD, P_GAMMA, P_BETA, P_BA, P_BF = range(27, 35)
P_WF, P_A1, P_A2, P_COLS = 35, 38, 42, 46


def cols(c):
    return slice(c * CH * NP_, min((c + 1) * CH, NT) * NP_)


def tiles(c):
    return range(c * CH, min((c + 1) * CH, NT))


class Chain:

    def __init__(self, eng, sem):
        self.eng, self.sem, self.n, self.i = eng, sem, 0, None

    def __call__(self, ins):
        ins.then_inc(self.sem, 1)
        self.n += 1
        if self.i is None:
            self.eng.wait_ge(self.sem, self.n)
        else:
            self.eng.wait_ge(self.sem, self.i * self.per + self.n)

    @contextmanager
    def loop(self, rounds, per):
        before = self.n
        with self.eng.Fori(0, rounds) as i:
            self.i, self.per = i, per
            yield i
            assert self.n == before + per, (self.n - before, per)
        self.i, self.n = None, before + per * rounds


class Edges:

    def __init__(self, t, ch, src, dst, rel, wgt, dst_t, attr):
        self.t, self.ch, self.nc, self.rounds = t, ch, t // ch, t // BODY
        self.src, self.dst, self.rel, self.wgt, self.dst_t, self.attr = src, dst, rel, wgt, dst_t, attr
        assert self.nc * ch == t and ch % 4 == 0 and ch <= 128 and self.nc <= 6

    def landed(self, s, i):
        return i * (16 * HALF) + (s * self.rounds + 1) * (16 * HALF)

    def staged(self, s, i):
        return i + (s * (self.rounds + 1) + 1)


def build(nc, I, out):
    def dram(name, shape, dt=F32):
        return nc.dram_tensor(name, shape, dt, kind="Internal").ap()

    given = Edges(T_GIVEN, T_GIVEN // 4, I["src_e"], I["dst_e"], I["rel_e"], I["wgt_e"], I["dst_t"],
                  I["attr_t"])
    records = dram("records", [(T_SORTED + HALF) * TILE, 4 + FE])
    attr_sorted = dram("attr_sorted", [FE, T_SORTED * TILE])
    ordered = Edges(T_SORTED, T_SORTED // 6, None, None, None, None, None, attr_sorted)
    gin_tab = [dram(f"gin_tab{k}", [N, C]) for k in range(2)]
    edge_tab = dram("edge_tab", [N, HID])
    att_tab = dram("att_tab", [N, ROW2])
    va_tab = dram("va_tab", [N + WIN, 2 * HEADS])
    rel_tab = dram("rel_tab", [RELS * N, C])
    stash = dram("stash", [T_SORTED // HALF * TILE, HALF, C])

    with ExitStack() as ctx:
        def sb(name, shape, dt=F32):
            return ctx.enter_context(nc.sbuf_tensor(name, shape, dt))
        TM = T_SORTED
        onehot = sb("onehot", [TILE, TM, WIN])
        src_i = sb("src_i", [TILE, TM + BODY], I32)
        dst_i = sb("dst_i", [TILE, TM], I32)
        rel_i = sb("rel_i", [TILE, TM + BODY], I32)
        wgt = sb("wgt", [TILE, TM])
        dst_loc = sb("dst_loc", [TILE, TM])
        late_row = sb("late_row", [1, TM + 2 * BODY], I32)
        off_row = sb("off_row", [1, TM], I32)
        base_f = sb("base_f", [128, 6])
        base_i = sb("base_i", [128, 6], I32)
        off_f = sb("off_f", [128, 6])
        step6 = sb("step6", [128, 6, 8])
        span = sb("span", [128, 8])
        flag_f = sb("flag_f", [1, 2])
        flag = sb("flag", [1, 1], I32)
        ident = sb("ident", [128, 128])
        iota_f = sb("iota_f", [128, 128])
        pidx_i = sb("pidx_i", [128, 4], I32)
        pidx_f = sb("pidx_f", [128, 4])
        jmask = sb("jmask", [128, WIN])
        kmask = sb("kmask", [128, HEADS])
        m4 = sb("m4", [128, 4])
        ones = sb("ones", [128, 128])
        zeros = sb("zeros", [128, BANK], BF16)
        prm = sb("prm", [128, P_COLS])
        fold = sb("fold", [C, 6, 3])
        wgin = sb("wgin", [C, 6, C])
        w1a, w1b = sb("w1a", [C, HID]), sb("w1b", [FE + 1, HID])
        w2, w4 = sb("w2", [HID, C]), sb("w4", [HID, C])
        w3a, w23 = sb("w3a", [C, HID]), sb("w23", [HID, HID])
        wl, wd = sb("wl", [C, C]), sb("wd", [C, C])
        wrel = sb("wrel", [C, RELS, C])
        brow = sb("brow", [1, 2 * C])
        b23 = sb("b23", [1, HID])
        hproj = sb("hproj", [C, C + 2 * HEADS])
        watt, batt = sb("watt", [C, ROW2]), sb("batt", [1, ROW2])
        bv = sb("bv", [HEADS, 1])
        fpq = sb("fpq", [C, 2])
        xt = sb("xt", [C, N])
        xn = sb("xn", [NP_, NT, C])
        yn = sb("yn", [NP_, NT, C])
        agg = sb("agg", [128, N])
        y1 = sb("y1", [128, N + WIN])
        row_t = sb("row_t", [1, NB - 1, WIN])
        tabn = sb("tabn", [NP_, 2, CH * RELS * C])
        stat = sb("stat", [NP_, 4, NT])
        bnst = sb("bnst", [C, 8])
        rows = sb("rows", [TILE, 2, HALF, HID])
        stage = sb("stage", [TILE, 2, HALF], I32)
        attr_buf = sb("attr_buf", [128, 2 * HALF * TILE])
        work = sb("work", [TILE, 2, HALF, HID])
        trio = sb("trio", [TILE, 3, 2, HALF, WIN])
        zbuf = sb("zbuf", [TILE, 2, 3, HALF])
        late = sb("late", [128, 3 * HEADS * TM])
        sg = sb("sg", [TILE, TM])
        abuf = sb("abuf", [TILE, 2, 3, HALF, HEADS])
        mxg = sb("mxg", [128, 2, HALF])
        mxe = sb("mxe", [128, 2, HALF, WIN])
        ps = ctx.enter_context(nc.psum_tensor("ps", [128, 8 * BANK], F32))
        attr = attr_buf[0:FE + 1, :].rearrange("p (h n) -> p h n", h=2)
        winv = attr_buf[:, 0:6 * WIN * 2 * HEADS].rearrange("p (c n) -> p c n", c=6)
        iota_i = attr_buf[:, 0:128].bitcast(I32)
        wexp = trio[:, 1, :, 0:4, :]
        ohs, msk = trio[:, 0], trio[:, 1]
        ohT = trio[:, 2].rearrange("p h a b -> p h (a b)")
        dst_tm = trio[:, :, :, :, :].bitcast(I32).rearrange("p a h k w -> p (a h k w)")[:, 0:6 * TILE]\
            .rearrange("p (c n) -> p c n", n=TILE)
        row2 = late[0:1, 0:2 * N].rearrange("p (a n) -> p a n", a=2)
        su = late[:, 0:HEADS * TM].rearrange("p (t k) -> p t k", k=HEADS)
        wtv = late[:, HEADS * TM:].rearrange("p (t k) -> p t k", k=2 * HEADS)
        q_row = late[0:1, HEADS * TM:HEADS * TM + N + WIN]
        w2_t, b2_col = late[0:C, 2 * C:2 * C + HID], late[0:C, 256:257]
        w3b, b4b = w23[0:C, :], w2[0:NP_, :]
        rcp_all = late[:, N:2 * N]
        attw_t = late[0:C, 0:2 * C].rearrange("p (a n) -> p a n", a=2)
        sq = agg[0:NP_, 0:NT * C].rearrange("p (i f) -> p i f", f=C)
        packed = rows[:, :, :, :].rearrange("p h a b -> p (h a b)")\
            .rearrange("p (s k f) -> p s k f", s=4, f=C)
        ohs4 = [trio[:, s // 2, s % 2] for s in range(4)]
        ohT4 = attr_buf[:, 0:4 * HALF * WIN].rearrange("p (s n) -> p s n", s=4)
        smax = y1[0:HEADS, :]
        vt = agg[0:HEADS, :]
        diag = work

        pe_regs = dve_regs = None

        def bank(b, n=BANK, off=0):
            return ps[:, b * BANK + off:b * BANK + off + n]

        sems = {}

        def sem(name):
            if name not in sems:
                sems[name] = ctx.enter_context(nc.semaphore(name))
            return sems[name]

        PARTS = ((0, 16), (16, NT))
        V, A, M = nc.vector, nc.scalar.activation, nc.tensor.matmul

        def chunk(c):
            return len(tiles(c))

        def table_parts(k, c):
            return k * ((NCH + 1 - c % 2) // 2) + (RELS if k == 3 else 1) * (c // 2)

        def half_tiles(i, h):
            return bass.ds(i * BODY + h * HALF, HALF)

        def sp_start(sp):
            sp.dma_start(dst_tm[0:given.ch, 0:given.nc, :], I["dst_t"]).then_inc(sem("dst_in"), 16)
            sp_edges(sp, given)
            loads = [(prm[:, :], I["params"]), (xt[:, :], I["x_t"]),
                     (xn[:, :, :], I["x"].rearrange("(i p) c -> p i c", p=NP_)),
                     (wgin[:, 0:3, :], I["L0_gnn_W1"].rearrange("l a b -> a l b")),
                     (wgin[:, 3:6, :], I["L0_gnn_W2"].rearrange("l a b -> a l b")),
                     (w1a[:, :], I["L1_gnn_W1"][0:C, :]), (w1b[0:FE, :], I["L1_gnn_W1"][C:C + FE, :]),
                     (w1b[FE:FE + 1, :], I["b1_row"]),
                     (w2[:, :], I["L1_gnn_W2"]), (w3a[:, :], I["L1_gnn_W3"][0:C, :]),
                     (w3b[:, :], I["L1_gnn_W3"][C:2 * C, :]), (w4[:, :], I["L1_gnn_W4"]),
                     (wl[:, :], I["L2_gnn_Wl"]), (wd[:, :], I["L2_gnn_Wd"]),
                     (wrel[:, :, :], I["L3_gnn_weight"].rearrange("r a b -> a r b")),
                     (brow[:, :], I["brow"])]
            assert len(loads) == N_LOADS
            for to, of in loads:
                sp.dma_start(to, of).then_inc(sem("params"), 16)

        def pool_start(pool):
            g = nc.gpsimd
            chain = Chain(pool, sem("pool"))
            g.iota(iota_i[:, :], pattern=[[1, 128]], base=0, channel_multiplier=0).then_inc(sem("consts"), 1)
            g.iota(pidx_i[:, 0:1], pattern=[[0, 1]], base=0, channel_multiplier=1).then_inc(sem("consts"), 1)
            g.memset(ones[:, :], 1.0).then_inc(sem("consts"), 1)
            g.memset(zeros[:, :], 0.0).then_inc(sem("consts"), 1)
            g.memset(src_i[:, T_GIVEN:TM + BODY], 0).then_inc(sem("consts"), 1)
            g.memset(rel_i[:, T_GIVEN:TM + BODY], 0).then_inc(sem("consts"), 1)
            g.memset(rows[:, :, :, C:C + 1], 1.0).then_inc(sem("consts"), 1)
            chain(g.memset(ident[:, :], 0.0))
            g.affine_select(out=ident[:, :], in_=ident[:, :], compare_op=ALU.not_equal, fill=1.0,
                            base=0, pattern=[[-1, 128]], channel_multiplier=1).then_inc(sem("consts"), 1)

        def dve_min_max(dve, chain, E):
            d = dst_tm[0:E.ch, 0:E.nc, :]
            near = work[0:E.ch, 0, 0:E.nc, :]
            V.scalar_tensor_tensor(out=near, in0=d, scalar=float(FAR), in1=d, op0=ALU.is_lt,
                                   op1=ALU.mult).then_inc(sem("dve"), 1)
            chain.n += 1
            chain(V.tensor_reduce(base_f[0:E.ch, 0:E.nc], d, AX, ALU.min))
            chain(V.tensor_reduce(span[0:E.ch, 0:E.nc], near, AX, ALU.max))
            chain(V.tensor_tensor(span[0:E.ch, 0:E.nc], span[0:E.ch, 0:E.nc], base_f[0:E.ch, 0:E.nc],
                                  ALU.subtract))
            chain(V.tensor_scalar(base_f[0:E.ch, 0:E.nc], base_f[0:E.ch, 0:E.nc], float(N - 1), None,
                                  ALU.min))
            V.tensor_reduce(span[0:E.ch, 7:8], span[0:E.ch, 0:E.nc], AX, ALU.max)\
                .then_inc(sem("span_ready"), 1)

        def dve_start(dve, chain):
            dve.wait_ge(sem("dst_in"), 16)
            dve_min_max(dve, chain, given)
            dve.wait_ge(sem("span_row"), 1)
            chain(V.tensor_reduce(flag_f[:, 0:1], bank(0, given.ch)[0:1, :], AX, ALU.max))
            V.tensor_scalar(flag[:, :], flag_f[:, 0:1], float(WIN - 1), None, ALU.is_le)\
                .then_inc(sem("flag"), 1)
            dve.wait_ge(sem("consts"), 8)
            V.tensor_copy(iota_f[:, :], iota_i[:, :]).then_inc(sem("dve"), 1)
            V.tensor_scalar(pidx_i[:, 1:2], pidx_i[:, 0:1], 31, None, ALU.bitwise_and).then_inc(sem("dve"), 1)
            V.tensor_scalar(pidx_i[:, 2:3], pidx_i[:, 0:1], 5, None, ALU.logical_shift_right)\
                .then_inc(sem("dve"), 1)
            chain.n += 3
            chain(V.tensor_scalar(pidx_i[:, 3:4], pidx_i[:, 0:1], 3, None, ALU.bitwise_and))
            chain(V.tensor_copy(pidx_f[:, :], pidx_i[:, :]))
            for mask, n, c in ((jmask, WIN, 1), (kmask, HEADS, 2), (m4, 4, 3)):
                V.tensor_scalar(mask[:, :], iota_f[:, 0:n], pidx_f[:, c:c + 1], None, ALU.is_equal)\
                    .then_inc(sem("masks"), 1)
            dve.wait_ge(sem("params"), 16 * N_LOADS)

            def p(k):
                return prm[0:C, k:k + 3]
            for o, (g, b, be) in ((0, (P_G1, P_B1, P_BE1)), (2, (P_G2, P_B2, P_BE2))):
                chain(V.tensor_scalar(fold[:, o, :], p(g), BN_C, None, ALU.mult))
                chain(V.tensor_tensor(fold[:, o + 1, :], fold[:, o, :], p(b), ALU.mult))
                chain(V.tensor_tensor(fold[:, o + 1, :], fold[:, o + 1, :], p(be), ALU.add))
            chain(V.tensor_scalar(fold[:, 4, :], p(P_BNG), BN_C, None, ALU.mult))
            chain(V.tensor_scalar(fold[:, 5, :], p(P_EPS), 1.0, None, ALU.add))
            chain(V.tensor_tensor(fpq[:, 0:1], prm[0:C, P_WF:P_WF + 1], prm[0:C, P_WF + 2:P_WF + 3], ALU.add))
            chain(V.tensor_tensor(fpq[:, 1:2], prm[0:C, P_WF + 1:P_WF + 2], prm[0:C, P_WF + 2:P_WF + 3],
                                  ALU.subtract))
            chain(V.tensor_copy(hproj[:, 0:C], ident[0:C, 0:C]))
            V.tensor_copy(hproj[:, C:C + 2 * HEADS], prm[0:C, P_A1:P_A1 + 2 * HEADS]).then_inc(sem("folded"), 1)

        def pe_start(pe):
            pe.wait_ge(sem("consts"), 8)
            pe.wait_ge(sem("span_ready"), 1)
            nc.tensor.transpose(bank(0, given.ch)[0:1, :], span[0:given.ch, 7:8],
                                ident[0:given.ch, 0:given.ch]).then_inc(sem("span_row"), 1)

        def sp_edges(sp, E):
            for to, of in ((src_i[:, 0:E.t], E.src), (dst_i[:, 0:E.t], E.dst), (rel_i[:, 0:E.t], E.rel),
                           (wgt[:, 0:E.t], E.wgt)):
                sp.dma_start(to, of).then_inc(sem("edges_in"), 16)

        def dve_edges(dve, chain, E):
            ch = E.ch
            b = base_f[0:ch, 0:E.nc]
            chain(V.tensor_scalar(step6[0:ch, 0, 0:NB - 1], iota_f[0:ch, 1:NB], float(STEP), None, ALU.mult))
            chain(V.tensor_copy(base_i[0:ch, 0:E.nc], b))
            chain(V.memset(late_row[:, :], 0))
            chain(V.tensor_copy(abuf[0:ch, 0, 0, 0, 0:1], b[:, 0:1]))
            cmp = abuf[0:ch, 1, :, :, :].rearrange("p a b c -> p (a b c)")[:, 0:E.nc * (NB - 1)]\
                .rearrange("p (c m) -> p c m", m=NB - 1)
            chain(V.tensor_tensor(cmp, b.unsqueeze(2).to_broadcast([ch, E.nc, NB - 1]),
                                  step6[0:ch, 0:1, 0:NB - 1].to_broadcast([ch, E.nc, NB - 1]), ALU.is_ge))
            chain(V.tensor_reduce(off_f[0:ch, 0:E.nc], cmp, AX, ALU.add))
            chain(V.scalar_tensor_tensor(out=off_f[0:ch, 0:E.nc], in0=off_f[0:ch, 0:E.nc], scalar=float(WIN),
                                         in1=b, op0=ALU.mult, op1=ALU.add))
            for c in range(E.nc):
                V.tensor_scalar(diag[0:ch, 0, c, 0:ch], ident[0:ch, 0:ch], base_f[0:ch, c:c + 1], None,
                                ALU.mult)
                V.tensor_scalar(diag[0:ch, 1, c, 0:ch], ident[0:ch, 0:ch], off_f[0:ch, c:c + 1], None,
                                ALU.mult).then_inc(sem("diag_ready"), 1)
            dve.wait_ge(sem("edges_in"), 64)
            for c in range(E.nc):
                at = slice(c * ch, (c + 1) * ch)
                dve.wait_ge(sem("base_out"), c + 1)
                V.tensor_copy(late_row[:, HALF + c * ch:HALF + (c + 1) * ch], bank(c, ch)[0:1, :])
                V.tensor_copy(off_row[:, at], bank(c, ch, 256)[0:1, :])
                chain(V.tensor_tensor(dst_loc[:, at], dst_i[:, at], bank(c, ch), ALU.subtract))
            for c in range(E.nc):
                at = slice(c * ch, (c + 1) * ch)
                V.tensor_tensor(onehot[:, at, :], dst_loc[:, at].unsqueeze(2).to_broadcast([TILE, ch, WIN]),
                                iota_f[:, 0:WIN].unsqueeze(1).to_broadcast([TILE, ch, WIN]), ALU.is_equal)\
                    .then_inc(sem("onehot_ready"), 1)
            V.scalar_tensor_tensor(out=rel_i[:, 0:E.t], in0=rel_i[:, 0:E.t], scalar=float(N),
                                   in1=src_i[:, 0:E.t], op0=ALU.mult, op1=ALU.add).then_inc(sem("rel_ready"), 1)

        def pe_edges(pe, E):
            for c in range(E.nc):
                pe.wait_ge(sem("diag_ready"), c + 1)
                M(bank(c, E.ch), ones[0:E.ch, :], diag[0:E.ch, 0, c, 0:E.ch], start=True, stop=True)
                M(bank(c, E.ch, 256)[0:1, :], ones[0:E.ch, 0:1], diag[0:E.ch, 1, c, 0:E.ch],
                  start=True, stop=True, skip_group_check=True).then_inc(sem("base_out"), 1)

        def pool_gather(pool, E, s, table, width):
            with pool.Fori(0, E.rounds) as i:
                for h in range(2):
                    pool.wait_ge(sem(f"staged{h}"), E.staged(s, i))
                    pool.sem_inc(sem("gather_started"), 1)
                    for k in range(HALF):
                        nc.gpsimd.indirect_dma_start(
                            out=rows[:, h, k, 0:width], out_offset=None, in_=table,
                            in_offset=bass.IndirectOffsetOnAxis(ap=stage[:, h, k:k + 1], axis=0))\
                            .then_inc(sem(f"landed{h}"), 16)

        def stage_first(act, E, s, idx):
            for h in range(2):
                A(stage[:, h, :], idx[:, h * HALF:(h + 1) * HALF], ACT.Copy).then_inc(sem(f"staged{h}"), 1)

        def stage_next(s, idx, i, h):
            A(stage[:, h, :], idx[:, bass.ds(i * BODY + BODY + h * HALF, HALF)], ACT.Copy)\
                .then_inc(sem(f"staged{h}"), 1)

        def pe_clear(m):
            for b in range(NB):
                M(bank(b)[0:m, :], zeros[:, 0:m], zeros[:, :], start=True, stop=False, skip_group_check=True)

        def pe_windows(pe, i, h):
            pe.reg_load(pe_regs, off_row[:, half_tiles(i, h)])
            return [pe.snap(r, min_val=0, max_val=NB * BANK - WIN) for r in pe_regs]

        def pe_scatter(col, m, lhsT, rhs):
            return M(ps[0:m, bass.ds(col, WIN)], lhsT, rhs, start=False, stop=False, skip_group_check=True)

        def onehot_tile(i, h, k):
            return onehot[:, bass.ds(i * BODY + h * HALF + k, 1), :].rearrange("p a b -> p (a b)")

        def dve_sums(dve, chain, s, m):
            dve.wait_ge(sem("summed"), s + 1)
            for b in range(NB):
                n = min(STEP, N - b * STEP)
                ins = V.tensor_copy(agg[0:m, b * STEP:b * STEP + n], bank(b, n)[0:m, :])
                if b:
                    chain(ins)
                    at = agg[0:m, b * STEP:b * STEP + WIN]
                    ins = V.tensor_tensor(at, at, bank(b - 1, WIN, STEP)[0:m, :], ALU.add)
                ins.then_inc(sem("sums_ready"), 1)

        def dve_norm(dve, chain, q, after=None):
            for part, (a, b) in enumerate(PARTS):
                if after is not None:
                    dve.wait_ge(*after(part))
                n = b - a
                y, s = yn[:, a:b, :], sq[:, a:b, :]
                wide = [NP_, n, C]
                chain(V.tensor_reduce(stat[:, 0, a:b], y, AX, ALU.add))
                chain(V.tensor_scalar(stat[:, 0, a:b], stat[:, 0, a:b], -1.0 / C, None, ALU.mult))
                chain(V.tensor_tensor(y, y, stat[:, 0, a:b].unsqueeze(2).to_broadcast(wide), ALU.add))
                chain(V.tensor_tensor(s, y, y, ALU.mult))
                chain(V.tensor_reduce(stat[:, 1, a:b], s, AX, ALU.add))
                V.tensor_scalar(stat[:, 1, a:b], stat[:, 1, a:b], 1.0 / C, 1e-05, ALU.mult, ALU.add)\
                    .then_inc(sem("ln_var"), 1)
            for part, (a, b) in enumerate(PARTS):
                wide = [NP_, b - a, C]
                dve.wait_ge(sem("ln_sd"), 2 * q + part + 1)
                chain(V.reciprocal(stat[:, 3, a:b], stat[:, 2, a:b]))
                V.tensor_tensor(xn[:, a:b, :], yn[:, a:b, :], stat[:, 3, a:b].unsqueeze(2).to_broadcast(wide),
                                ALU.mult).then_inc(sem("xn_ready"), 1)

        def act_norm(act, q):
            for part, (a, b) in enumerate(PARTS):
                act.wait_ge(sem("ln_var"), 2 * q + part + 1)
                A(stat[:, 2, a:b], stat[:, 1, a:b], ACT.Sqrt).then_inc(sem("ln_sd"), 1)

        def pe_back(pe, q, c):
            pe.wait_ge(sem("xn_ready"), 2 * q + (1 if tiles(c)[-1] < PARTS[0][1] else 2))
            if c >= 2:
                pe.wait_ge(sem("back_ev"), q * NCH + c - 1)
            for j, t in enumerate(tiles(c)):
                ins = nc.tensor.transpose(bank(c % 2, NP_, j * NP_)[0:C, :], xn[:, t, :], ident[0:NP_, 0:NP_])
            ins.then_inc(sem("back"), 1)

        def act_back(act, q, c):
            act.wait_ge(sem("back"), q * NCH + c + 1)
            A(xt[:, cols(c)], bank(c % 2, chunk(c) * NP_)[0:C, :], ACT.Copy).then_inc(sem("back_ev"), 1)

        def pool_gin(pool, E):
            pool.wait_ge(sem("consts"), 8)
            for l in range(3):
                if l:
                    pool.wait_ge(sem("gin_out"), 16 * NCH * l)
                pool_gather(pool, E, l, I["x"] if l == 0 else gin_tab[l - 1], C)

        def pe_gin(pe, E):
            pe_att_weights(pe)
            pe.wait_ge(sem("w_att"), 5)
            pe.wait_ge(sem("onehot_ready"), E.nc)
            for l in range(3):
                m = C + (l == 0)
                if l:
                    pe.wait_ge(sem("ev"), NCH * l)
                pe_clear(m)
                with pe.Fori(0, E.rounds) as i:
                    for h in range(2):
                        at = pe_windows(pe, i, h)
                        pe.wait_ge(sem(f"landed{h}"), E.landed(l, i))
                        for k in range(HALF):
                            ins = pe_scatter(at[k], m, rows[:, h, k, 0:m], onehot_tile(i, h, k))
                        ins.then_inc(sem(f"taken{l}{h}"), 1)
                M(bank(7, 8)[0:1, :], zeros[:, 0:1], zeros[:, 0:8], start=True, stop=True)\
                    .then_inc(sem("summed"), 1)
                if l == 0:
                    pe.wait_ge(sem("count_out"), 1)
                for step in range(NCH + 2):
                    if step < NCH:
                        c = step
                        n = chunk(c) * NP_
                        pe.wait_ge(sem("sums_ready"), l * NB + min(c + 2, NB))
                        if c >= 2:
                            pe.wait_ge(sem("a1"), l * NCH + c - 1)
                        M(bank((7, 0)[c % 2], n)[0:C, :], wgin[:, l, :], agg[0:C, cols(c)],
                          start=True, stop=True).then_inc(sem("mm1"), 1)
                    if 1 <= step <= NCH:
                        c = step - 1
                        n = chunk(c) * NP_
                        pe.wait_ge(sem("a1"), l * NCH + c + 1)
                        pe.wait_ge(sem("sums_ready"), l * NB + min(c + 4, NB))
                        if c >= 2:
                            pe.wait_ge(sem("a2"), l * NCH + c - 1)
                        M(bank(1 + c % 2, n)[0:C, :], wgin[:, 3 + l, :], y1[0:C, cols(c)],
                          start=True, stop=True).then_inc(sem("mm2"), 1)
                    if step >= 2:
                        c = step - 2
                        pe.wait_ge(sem("x_new"), l * NCH + c + 1)
                        pe.wait_ge(sem("sums_ready"), l * NB + min(c + 6, NB))
                        if c >= 2:
                            pe.wait_ge(sem("ev"), l * NCH + c - 1)
                        for j, t in enumerate(tiles(c)):
                            ins = nc.tensor.transpose(bank(3 + c % 2, C, j * C)[0:NP_, :],
                                                      xt[:, t * NP_:(t + 1) * NP_], ident[0:C, 0:C])
                        ins.then_inc(sem("tr"), 1)

        def act_gin(act, E):
            act.wait_ge(sem("consts"), 8)
            act.wait_ge(sem("edges_in"), 64)
            for l in range(3):
                stage_first(act, E, l, src_i)
                if l == 0:
                    act_att_weights(act)
                with act.Fori(0, E.rounds) as i:
                    for h in range(2):
                        act.wait_ge(sem(f"taken{l}{h}"), i + 1)
                        stage_next(l, src_i, i, h)
                if l == 0:
                    act.wait_ge(sem("folded"), 1)
                    act.wait_ge(sem("summed"), 1)
                    banks = ps[C:C + 1, 0:(NB - 1) * BANK].rearrange("p (b n) -> p b n", n=BANK)
                    A(row2[:, 0, 0:(NB - 1) * STEP].rearrange("p (b n) -> p b n", n=STEP),
                      banks[:, :, 0:STEP], ACT.Copy)
                    A(row2[:, 0, (NB - 1) * STEP:N], bank(NB - 1, N - (NB - 1) * STEP)[C:C + 1, :], ACT.Copy)
                    A(row_t[:, :, :], banks[:, :, STEP:BANK], ACT.Copy).then_inc(sem("count_out"), 1)
                for step in range(NCH + 2):
                    if step < NCH:
                        c = step
                        act.wait_ge(sem("mm1"), l * NCH + c + 1)
                        A(y1[0:C, cols(c)], bank((7, 0)[c % 2], chunk(c) * NP_)[0:C, :], ACT.Relu,
                          bias=fold[:, 1, l:l + 1], scale=fold[:, 0, l:l + 1]).then_inc(sem("a1"), 1)
                    if 1 <= step <= NCH:
                        c = step - 1
                        act.wait_ge(sem("mm2"), l * NCH + c + 1)
                        A(y1[0:C, cols(c)], bank(1 + c % 2, chunk(c) * NP_)[0:C, :], ACT.Relu,
                          bias=fold[:, 3, l:l + 1], scale=fold[:, 2, l:l + 1]).then_inc(sem("a2"), 1)
                    if step >= 2 and l < 2:
                        c = step - 2
                        act.wait_ge(sem("tr"), l * NCH + c + 1)
                        A(yn[:, c * CH:c * CH + chunk(c), :].rearrange("p a b -> p (a b)"),
                          bank(3 + c % 2, chunk(c) * C)[0:NP_, :], ACT.Copy).then_inc(sem("ev"), 1)

        def dve_gin(dve, chain, E):
            for l in range(3):
                dve.wait_ge(sem("summed"), l + 1)
                for b in range(NB):
                    n = min(STEP, N - b * STEP)
                    at = slice(b * STEP, b * STEP + n)
                    ins = V.scalar_tensor_tensor(out=agg[0:C, at], in0=xt[:, at], scalar=fold[:, 5, l:l + 1],
                                                 in1=bank(b, n)[0:C, :], op0=ALU.mult, op1=ALU.add)
                    if b:
                        chain(ins)
                        at = agg[0:C, b * STEP:b * STEP + WIN]
                        ins = V.tensor_tensor(at, at, bank(b - 1, WIN, STEP)[0:C, :], ALU.add)
                    ins.then_inc(sem("sums_ready"), 1)
                for step in range(NCH + 1):
                    if step < NCH:
                        c = step
                        dve.wait_ge(sem("a2"), l * NCH + c + 1)
                        ins = V.tensor_scalar(xt[:, cols(c)], y1[0:C, cols(c)], fold[:, 4, l:l + 1],
                                              prm[0:C, P_BNB + l:P_BNB + l + 1], ALU.mult, ALU.add)
                        if l < 2:
                            chain(ins)
                            ins = V.tensor_scalar(xt[:, cols(c)], xt[:, cols(c)], 0.0, None, ALU.max)
                        ins.then_inc(sem("x_new"), 1)
                    if step >= 1 and l == 2:
                        c = step - 1
                        dve.wait_ge(sem("tr"), l * NCH + c + 1)
                        at = slice(c * CH, c * CH + chunk(c))
                        V.tensor_tensor(yn[:, at, :], bank(3 + c % 2, chunk(c) * C)[0:NP_, :]
                                        .rearrange("p (a b) -> p a b", b=C), xn[:, at, :], ALU.add)\
                            .then_inc(sem("ev"), 1)
                if l == 0:
                    dve.wait_ge(sem("count_out"), 1)
                    at = row2[:, 0, STEP:NB * STEP - STEP + WIN]
                    for b in range(1, NB):
                        at = row2[:, 0, b * STEP:b * STEP + WIN]
                        ins = V.tensor_tensor(at, at, row_t[:, b - 1, :], ALU.add)
                    chain(ins)
                    chain(V.tensor_scalar(row2[:, 1, :], row2[:, 0, :], 1.0, None, ALU.max))
                    chain(V.reciprocal(row2[:, 1, :], row2[:, 1, :]))
                    chain(V.tensor_tensor(row2[:, 0, :], row2[:, 0, :], row2[:, 1, :], ALU.mult))
            dve.wait_ge(sem("ev"), 3 * NCH)
            dve_norm(dve, chain, 0)

        def sp_gin(sp, E):
            for l in range(2):
                for c in range(NCH):
                    sp.wait_ge(sem("ev"), l * NCH + c + 1)
                    sp.dma_start(gin_tab[l][cols(c), :].rearrange("(i p) f -> p i f", p=NP_),
                                 yn[:, c * CH:c * CH + chunk(c), :]).then_inc(sem("gin_out"), 16)

        def pe_edge(pe, E):
            for step in range(NCH + 1):
                if step < NCH:
                    pe_back(pe, 0, step)
                if step >= 1:
                    c = step - 1
                    pe.wait_ge(sem("back_ev"), c + 1)
                    if c >= 2:
                        pe.wait_ge(sem("e_ev"), c - 1)
                    for j, t in enumerate(tiles(c)):
                        ins = M(bank(2 + c % 2, HID, j * HID)[0:NP_, :], xt[:, t * NP_:(t + 1) * NP_], w1a[:, :],
                                start=True, stop=True, skip_group_check=True)
                    ins.then_inc(sem("e_mm"), 1)
            for c in range(NCH):
                if c >= 2:
                    pe.wait_ge(sem("mean_ev"), c - 1)
                M(bank(4 + c % 2, chunk(c) * NP_), ones[0:1, :], row2[:, 1, cols(c)], start=True, stop=True)\
                    .then_inc(sem("mean_mm"), 1)
            pe.wait_ge(sem("e_ev"), NCH)
            pe.wait_ge(sem("mean_ev"), NCH)
            pe_clear(HID)
            pe.sem_inc(sem("scattered30"), 1)
            pe.sem_inc(sem("scattered31"), 1)
            pe.sem_inc(sem("px_added"), 1)
            pe.wait_ge(sem("ones_row"), 1)
            with pe.Fori(0, E.rounds) as i:
                for h in range(2):
                    at = pe_windows(pe, i, h)
                    pe.wait_ge(sem(f"attr_in{h}"), i * 16 + 16)

                    def project(p):
                        pe.wait_ge(sem("px_added"), i * 4 + (2 * h + p + 1))
                        for k in range(4 * p, 4 * p + 4):
                            ins = M(bank(7, HID, (k % 4) * HID),
                                    attr[:, h, k * TILE:(k + 1) * TILE], w1b[:, :], start=True, stop=True,
                                    skip_group_check=True)
                        ins.then_inc(sem("px_full"), 1)

                    def scatter(p):
                        pe.wait_ge(sem("relued"), i * 4 + (2 * h + p + 1))
                        for k in range(4 * p, 4 * p + 4):
                            ins = pe_scatter(at[k], HID, work[:, h, k, :], onehot_tile(i, h, k))
                        return ins

                    project(0)
                    project(1)
                    scatter(0)
                    scatter(1).then_inc(sem(f"scattered3{h}"), 1)
            M(bank(7, 8)[0:1, :], zeros[:, 0:1], zeros[:, 0:8], start=True, stop=True)\
                .then_inc(sem("summed"), 1)
            for step in range(NCH + 1):
                if step < NCH:
                    c = step
                    to = bank((7, 0)[c % 2], chunk(c) * NP_)
                    pe.wait_ge(sem("sums_ready"), 3 * NB + min(c + 2, NB))
                    if c >= 2:
                        pe.wait_ge(sem("m_relu"), c - 1)
                    M(to, w3a[:, :], xt[:, cols(c)], start=True, stop=False)
                    M(to, b23[:, :], row2[:, 0, cols(c)], start=False, stop=False)
                    M(to, w23[:, :], agg[:, cols(c)], start=False, stop=True).then_inc(sem("m_hid"), 1)
                if step >= 1:
                    c = step - 1
                    pe.wait_ge(sem("m_relu"), c + 1)
                    pe.wait_ge(sem("sums_ready"), 3 * NB + min(c + 4, NB))
                    if c >= 2:
                        pe.wait_ge(sem("m_ev"), c - 1)
                    for j, t in enumerate(tiles(c)):
                        ins = M(bank(1 + c % 2, C, j * C)[0:NP_, :], y1[:, t * NP_:(t + 1) * NP_], w4[:, :],
                                start=True, stop=True, skip_group_check=True)
                    ins.then_inc(sem("m_out"), 1)

        def dve_edge(dve, chain, E):
            V.memset(attr[FE:FE + 1, :, :], 1.0).then_inc(sem("ones_row"), 1)
            dve.wait_ge(sem("back_ev"), NCH)
            V.tensor_tensor(xn[:, :, :], xn[:, :, :], b4b[:, :].unsqueeze(1).to_broadcast([NP_, NT, C]), ALU.add)\
                .then_inc(sem("x_b4"), 1)
            for c in range(NCH):
                dve.wait_ge(sem("mean_mm"), c + 1)
                V.tensor_copy(rcp_all[:, cols(c)], bank(4 + c % 2, chunk(c) * NP_)).then_inc(sem("mean_ev"), 1)
            with dve.Fori(0, E.rounds) as i:
                for h in range(2):
                    dve.wait_ge(sem(f"landed{h}"), E.landed(3, i))
                    dve.wait_ge(sem(f"scattered3{h}"), i + 1)
                    for p in range(2):
                        dve.wait_ge(sem("px_full"), i * 4 + (2 * h + p + 1))
                        V.tensor_tensor(work[:, h, 4 * p:4 * p + 4, :], rows[:, h, 4 * p:4 * p + 4, :],
                                        bank(7).rearrange("p (a b) -> p a b", b=HID),
                                        ALU.add).then_inc(sem("px_added"), 1)
            dve.wait_ge(sem("summed"), 4)
            for b in range(NB):
                n = min(STEP, N - b * STEP)
                at = slice(b * STEP, b * STEP + n)
                ins = V.tensor_tensor(agg[:, at], bank(b, n), rcp_all[:, at], ALU.mult)
                if b:
                    over = slice(b * STEP, b * STEP + WIN)
                    chain(V.tensor_tensor(work[:, 0, b, 0:WIN], bank(b - 1, WIN, STEP), rcp_all[:, over], ALU.mult))
                    ins = V.tensor_tensor(agg[:, over], agg[:, over], work[:, 0, b, 0:WIN], ALU.add)
                ins.then_inc(sem("sums_ready"), 1)
            dve.wait_ge(sem("x_b4"), 1)
            for c in range(NCH):
                dve.wait_ge(sem("m_out"), c + 1)
                at = slice(c * CH, c * CH + chunk(c))
                V.tensor_tensor(yn[:, at, :], bank(1 + c % 2, chunk(c) * C)[0:NP_, :]
                                .rearrange("p (a b) -> p a b", b=C), xn[:, at, :], ALU.add).then_inc(sem("m_ev"), 1)
            dve_norm(dve, chain, 1, lambda part: (sem("m_ev"), (4, NCH)[part]))

        def act_edge(act, E):
            act_norm(act, 0)
            for step in range(NCH + 1):
                if step < NCH:
                    act_back(act, 0, step)
                if step >= 1:
                    c = step - 1
                    act.wait_ge(sem("e_mm"), c + 1)
                    if c >= 2:
                        act.wait_ge(sem(f"table_out{c % 2}"), 16 * table_parts(0, c))
                    A(tabn[:, c % 2, 0:chunk(c) * HID], bank(2 + c % 2, chunk(c) * HID)[0:NP_, :], ACT.Copy)\
                        .then_inc(sem("e_ev"), 1)
            stage_first(act, E, 3, src_i)
            with act.Fori(0, E.rounds) as i:
                for h in range(2):
                    for p in range(2):
                        act.wait_ge(sem("px_added"), i * 4 + (2 * h + p + 2))
                        four = work[:, h, 4 * p:4 * p + 4, :]
                        A(four, four, ACT.Relu).then_inc(sem("relued"), 1)
                    stage_next(3, src_i, i, h)
            for c in range(NCH):
                act.wait_ge(sem("m_hid"), c + 1)
                A(y1[:, cols(c)], bank((7, 0)[c % 2], chunk(c) * NP_), ACT.Relu,
                  bias=prm[:, P_L1B3:P_L1B3 + 1]).then_inc(sem("m_relu"), 1)
            act_norm(act, 1)

        def sp_edge(sp, E):
            for c in range(NCH):
                sp.wait_ge(sem("e_ev"), c + 1)
                sp.dma_start(edge_tab[cols(c), :].rearrange("(i p) f -> p i f", p=NP_),
                             tabn[:, c % 2, 0:chunk(c) * HID].rearrange("p (a b) -> p a b", b=HID))\
                    .then_inc(sem(f"table_out{c % 2}"), 16)
            with sp.Fori(0, E.rounds) as i:
                for h in range(2):
                    sp.wait_ge(sem(f"scattered3{h}"), i + 1)
                    sp.dma_start(attr[0:FE, h, :],
                                 E.attr[:, bass.ds(i * (BODY * TILE) + h * HALF * TILE, HALF * TILE)])\
                        .then_inc(sem(f"attr_in{h}"), 16)

        def pool_edge(pool, E):
            pool.wait_ge(sem("table_out0"), 16 * table_parts(0, NCH + NCH % 2))
            pool.wait_ge(sem("table_out1"), 16 * table_parts(0, NCH + 1 - NCH % 2))
            pool_gather(pool, E, 3, edge_tab, HID)

        def pe_att_weights(pe):
            pe.wait_ge(sem("folded"), 1)
            nc.tensor.transpose(bank(7, C)[0:C, :], wl[:, :], ident[0:C, 0:C])
            nc.tensor.transpose(bank(7, C, C)[0:C, :], wd[:, :], ident[0:C, 0:C])
            nc.tensor.transpose(bank(7, HID, 2 * C)[0:C, :], w2[:, :], ident[:, :])
            M(bank(7, 1, 256)[0:C, :], brow[:, 0:C], ones[0:1, 0:1], start=True, stop=True,
              skip_group_check=True).then_inc(sem("w_att"), 1)
            pe.wait_ge(sem("w_att"), 2)
            for lhsT, rows_, at in ((attw_t[:, 0, :], C, 128), (prm[0:C, P_BL:P_BL + 1], 1, 256)):
                M(bank(7, 2 * HEADS, at + C)[0:rows_, :], lhsT, hproj[:, C:C + 2 * HEADS],
                  start=True, stop=True, skip_group_check=True)
            for lhsT, rows_, at in ((attw_t[:, 1, :], C, 128), (prm[0:C, P_BD:P_BD + 1], 1, 256)):
                M(bank(7, 2, at + C + 2 * HEADS)[0:rows_, :], lhsT, fpq[:, :],
                  start=True, stop=True, skip_group_check=True)
            M(bank(7, C, 256)[0:1, :], prm[0:C, P_BL:P_BL + 1], ident[0:C, 0:C],
              start=True, stop=True, skip_group_check=True)
            M(bank(7, 1, 384)[0:HEADS, :], hproj[:, C + HEADS:C + 2 * HEADS], prm[0:C, P_BL:P_BL + 1],
              start=True, stop=True, skip_group_check=True)
            M(bank(6, HID), w2_t, w3b[:, :], start=True, stop=True, skip_group_check=True)
            M(bank(6, HID, HID)[0:1, :], b2_col, w3b[:, :], start=True, stop=True, skip_group_check=True)
            M(bank(6, C, 2 * HID)[0:NP_, :], ones[0:1, 0:NP_], brow[:, C:2 * C], start=True, stop=True,
              skip_group_check=True).then_inc(sem("w_att"), 1)

        def act_att_weights(act):
            act.wait_ge(sem("w_att"), 1)
            A(late[0:C, 0:257], bank(7, 257)[0:C, :], ACT.Copy)\
                .then_inc(sem("w_att"), 1)
            A(watt[:, 0:C], wl[:, :], ACT.Copy)
            act.wait_ge(sem("w_att"), 3)
            A(watt[:, C:ROW2], bank(7, ROW2 - C, 128 + C)[0:C, :], ACT.Copy)
            A(w23[:, :], bank(6, HID), ACT.Copy)
            A(b23[:, :], bank(6, HID, HID)[0:1, :], ACT.Copy)
            A(b4b[:, :], bank(6, C, 2 * HID)[0:NP_, :], ACT.Copy)
            A(batt[:, :], bank(7, ROW2, 256)[0:1, :], ACT.Copy).then_inc(sem("w_att"), 1)
            act.wait_ge(sem("w_att"), 4)
            A(batt[:, C + HEADS:C + 2 * HEADS], batt[:, C + HEADS:C + 2 * HEADS], ACT.Identity,
              bias=prm[0:1, P_BA:P_BA + 1])
            A(batt[:, ROW2 - 1:ROW2], batt[:, ROW2 - 1:ROW2], ACT.Identity, bias=prm[0:1, P_BF:P_BF + 1])
            A(bv[:, :], bank(7, 1, 384)[0:HEADS, :], ACT.Identity, bias=prm[0:HEADS, P_BA:P_BA + 1])\
                .then_inc(sem("w_att"), 1)

        def pe_att_tables(pe, E):
            for step in range(NCH + 1):
                if step < NCH:
                    pe_back(pe, 1, step)
                if step >= 1:
                    c = step - 1
                    pe.wait_ge(sem("back_ev"), NCH + c + 1)
                    if c >= 2:
                        pe.wait_ge(sem("hup_ev"), c - 1)
                    for j, t in enumerate(tiles(c)):
                        to = bank(2 + c % 2, ROW2, j * ROW2)[0:NP_, :]
                        M(to, xt[:, t * NP_:(t + 1) * NP_], watt[:, :], start=True, stop=False,
                          skip_group_check=True)
                        ins = M(to, ones[0:1, 0:NP_], batt[:, :], start=False, stop=True,
                                skip_group_check=True)
                    ins.then_inc(sem("hup"), 1)
            for c in range(NCH):
                n = chunk(c) * NP_
                if c >= 2:
                    pe.wait_ge(sem("vq_ev"), 2 * (c - 1))
                M(bank(4 + 2 * (c % 2), n)[0:1, :], watt[:, ROW2 - 1:ROW2], xt[:, cols(c)], start=True, stop=True)
                M(bank(5 + 2 * (c % 2), n)[0:HEADS, :], watt[:, C + HEADS:C + 2 * HEADS], xt[:, cols(c)],
                  start=True, stop=True).then_inc(sem("vq"), 1)

        def act_att_tables(act, E):
            for step in range(NCH + 1):
                if step < NCH:
                    act_back(act, 1, step)
                if step >= 1:
                    c = step - 1
                    act.wait_ge(sem("hup"), c + 1)
                    if c >= 2:
                        act.wait_ge(sem(f"table_out{c % 2}"), 16 * table_parts(1, c))
                    A(tabn[:, c % 2, 0:chunk(c) * ROW2], bank(2 + c % 2, chunk(c) * ROW2)[0:NP_, :],
                      ACT.Copy).then_inc(sem("hup_ev"), 1)
            stage_first(act, E, 4, src_i)

        def dve_att_tables(dve, chain, E):
            for c in range(NCH):
                n = chunk(c) * NP_
                dve.wait_ge(sem("vq"), c + 1)
                V.tensor_scalar(q_row[:, cols(c)], bank(4 + 2 * (c % 2), n)[0:1, :], batt[:, ROW2 - 1:ROW2], None,
                                ALU.add).then_inc(sem("vq_ev"), 1)
                V.tensor_scalar(vt[:, cols(c)], bank(5 + 2 * (c % 2), n)[0:HEADS, :], bv[:, :], None,
                                ALU.add).then_inc(sem("vq_ev"), 1)
            chain(V.memset(smax[:, :], -BIG))

        def sp_att_tables(sp, E):
            for c in range(NCH):
                sp.wait_ge(sem("hup_ev"), c + 1)
                sp.dma_start(att_tab[cols(c), :].rearrange("(i p) f -> p i f", p=NP_),
                             tabn[:, c % 2, 0:chunk(c) * ROW2].rearrange("p (a b) -> p a b", b=ROW2))\
                    .then_inc(sem(f"table_out{c % 2}"), 16)
            sp.dma_start(va_tab[N:N + WIN, :], I["nought"][:, 0:2 * HEADS]).then_inc(sem("va_tail"), 16)

        def pool_att_tables(pool, E):
            pool.wait_ge(sem("table_out0"), 16 * table_parts(1, NCH + NCH % 2))
            pool.wait_ge(sem("table_out1"), 16 * table_parts(1, NCH + 1 - NCH % 2))

        def act_signs(act, chain, E):
            with chain.loop(E.rounds, 2) as i:
                for h in range(2):
                    act.wait_ge(sem(f"l_ready{h}"), i + 1)
                    A(msk[:, h], onehot[:, half_tiles(i, h), :], ACT.Copy, bias=-BIG, scale=BIG)\
                        .then_inc(sem("mask"), 1)
                for h in range(2):
                    act.wait_ge(sem("z_ready"), i * 2 + (h + 1))
                    chain(A(zbuf[:, h, 1, :], zbuf[:, h, 0, :], ACT.Tanh))
                    A(sg[:, half_tiles(i, h)], zbuf[:, h, 1, :], ACT.Sign).then_inc(sem("sg_ready"), 1)
                    act.wait_ge(sem(f"su_ready{h}"), i + 1)
                    act.wait_ge(sem(f"stashed{h}"), i * 16 + 16)
                    stage_next(4, src_i, i, h)

        def pe_signs(pe, E):
            pe.wait_ge(sem("vq_ev"), 2 * NCH)
            pe.wait_ge(sem("hup_ev"), NCH)
            for h in range(2):
                pe.sem_inc(sem(f"l_ready{h}"), 1)
            pe.sem_inc(sem("l_max"), 1)
            pe.sem_inc(sem("q_taken"), 2)

            def windows_of_q(at, h, before):
                pe.reg_load(pe_regs, late_row[:, at])
                base = [pe.snap(r, min_val=0, max_val=N) for r in pe_regs]
                pe.wait_ge(sem("q_taken"), before)
                for k in range(HALF):
                    ins = M(bank(h, WIN, k * WIN), ones[0:1, :], q_row[:, bass.ds(base[k], WIN)],
                            start=True, stop=True, skip_group_check=True)
                ins.then_inc(sem("q_edge"), 1)

            windows_of_q(slice(HALF, 2 * HALF), 0, 1)
            pe.wait_ge(sem("no_max"), 1)
            M(bank(7, HALF * WIN)[0:HEADS, :], kmask[:, :], mxe[:, 1].rearrange("p a b -> p (a b)"),
              start=True, stop=True).then_inc(sem("max_row"), 1)
            with pe.Fori(0, E.rounds) as i:
                for h in range(2):
                    windows_of_q(bass.ds(i * BODY + (h + 2) * HALF, HALF), 1 - h, i * 2 + (h + 2))
                    pe.wait_ge(sem("l_max"), i * 2 + (h + 1))
                    pe.wait_ge(sem("l_half"), i * 2 + (h + 1))
                    for k in range(HALF):
                        if k == HALF // 2:
                            pe.wait_ge(sem(f"l_ready{h}"), i + 2)
                        ins = nc.tensor.transpose(bank(4 + k // 4, TILE, (k % 4) * TILE), work[:, h, k, :],
                                                  ident[:, :])
                    ins.then_inc(sem("l_tr"), 1)
                    pe.wait_ge(sem("max_spread"), i * 2 + (h + 1))
                    M(bank(6 + h, HALF * WIN)[0:HEADS, :], kmask[:, :],
                      mxe[:, h].rearrange("p a b -> p (a b)"), start=True, stop=True)\
                        .then_inc(sem("max_row"), 1)

        def dve_signs(dve, chain, E):
            def update(at, h, after):
                dve.reg_load(dve_regs, late_row[:, at])
                base = [dve.snap(r, min_val=0, max_val=N) for r in dve_regs]
                dve.wait_ge(sem("max_row"), after)
                for k in range(HALF):
                    if k == HALF // 2:
                        yield
                    to = smax[:, bass.ds(base[k], WIN)]
                    chain(V.tensor_tensor(to, to, bank(6 + h, WIN, k * WIN)[0:HEADS, :], ALU.max))

            V.memset(mxe[:, 1], -BIG).then_inc(sem("no_max"), 1)
            with chain.loop(E.rounds, 2 * HALF + 2) as i:
                for h in range(2):
                    dve.wait_ge(sem("q_edge"), i * 2 + (h + 1))
                    V.tensor_tensor(ohs[:, h], onehot[:, half_tiles(i, h), :],
                                    bank(h, HALF * WIN).rearrange("p (t j) -> p t j", j=WIN), ALU.mult)\
                        .then_inc(sem("q_taken"), 1)
                    dve.wait_ge(sem("q_taken"), i * 2 + (h + 3))
                    chain(V.tensor_reduce(zbuf[:, h, 2, :], ohs[:, h], AX, ALU.add))
                    dve.wait_ge(sem(f"landed{h}"), E.landed(4, i))
                    V.tensor_tensor(zbuf[:, h, 0, :], zbuf[:, h, 2, :], rows[:, h, :, C + 2 * HEADS], ALU.add)\
                        .then_inc(sem("z_ready"), 1)
                    updates = update(half_tiles(i, h), 1 - h, i * 2 + (h + 1))
                    next(updates)
                    dve.wait_ge(sem("sg_ready"), i * 2 + (h + 1))
                    at = su[:, half_tiles(i, h), :]
                    V.tensor_tensor(at, rows[:, h, :, C:C + HEADS],
                                    sg[:, half_tiles(i, h)].unsqueeze(2).to_broadcast([TILE, HALF, HEADS]),
                                    ALU.mult).then_inc(sem(f"su_ready{h}"), 1)
                    dve.wait_ge(sem(f"su_ready{h}"), i + 1)
                    dve.wait_ge(sem("mask"), i * 2 + (h + 1))
                    wide = [TILE, HALF // 2, HEADS, WIN]
                    for p, done in enumerate(("l_half", f"l_ready{h}")):
                        four = slice(4 * p, 4 * p + 4)
                        four_su = su[:, bass.ds(i * BODY + (h * HALF + 4 * p), 4), :]
                        V.tensor_tensor(work[:, h, four].rearrange("p a (k j) -> p a k j", j=WIN),
                                        four_su.unsqueeze(3).to_broadcast(wide),
                                        msk[:, h, four].unsqueeze(2).to_broadcast(wide), ALU.add)\
                            .then_inc(sem(done), 1)
                    next(updates, None)
                    dve.wait_ge(sem("l_tr"), i * 2 + (h + 1))
                    V.tensor_reduce(mxg[:, h, :], ps[:, 4 * BANK:6 * BANK].rearrange("p (a b) -> p a b", b=TILE),
                                    AX, ALU.max).then_inc(sem("l_max"), 1)
                    dve.wait_ge(sem("l_max"), i * 2 + (h + 2))
                    wide = [128, HALF, WIN]
                    V.tensor_tensor(mxe[:, h], mxg[:, h, :].unsqueeze(2).to_broadcast(wide),
                                    jmask[:, :].unsqueeze(1).to_broadcast(wide), ALU.mult)\
                        .then_inc(sem("max_spread"), 1)
            for _ in update(slice(E.t, E.t + HALF), 1, 2 * E.rounds + 1):
                pass
            for c in range(NCH):
                at = smax[:, cols(c)]
                chain(V.tensor_tensor(at, at, vt[:, cols(c)], ALU.add))
                V.scalar_tensor_tensor(out=at, in0=at, scalar=NEG_SLOPE, in1=at, op0=ALU.mult, op1=ALU.max)\
                    .then_inc(sem("am_ready"), 1)

        def sp_signs(sp, E):
            with sp.Fori(0, E.rounds) as i:
                for h in range(2):
                    sp.wait_ge(sem(f"landed{h}"), E.landed(4, i))
                    sp.dma_start(stash[bass.ds(i * (2 * TILE) + h * TILE, TILE), :, :], rows[:, h, :, 0:C])\
                        .then_inc(sem(f"stashed{h}"), 16)

        def pe_va(pe, E):
            for c in range(NCH):
                pe.wait_ge(sem("am_ready"), c + 1)
                if c >= 2:
                    pe.wait_ge(sem("va_ev"), c - 1)
                for j, t in enumerate(tiles(c)):
                    for k, of in enumerate((vt, smax)):
                        ins = nc.tensor.transpose(bank(c % 2, HEADS, (2 * j + k) * HEADS)[0:NP_, :],
                                                  of[:, t * NP_:(t + 1) * NP_], ident[0:HEADS, 0:HEADS])
                ins.then_inc(sem("va_tr"), 1)
            for c in range(E.nc):
                pe.wait_ge(sem("wv_spread"), c + 1)
                if c >= 2:
                    pe.wait_ge(sem("wv_ev"), 2 * (c - 1))
                for f in range(2 * HEADS):
                    ins = nc.tensor.transpose(bank(2 + 2 * (c % 2) + f // 4, E.ch, (f % 4) * E.ch),
                                              work[0:E.ch, c % 2, f, :], ident[0:E.ch, 0:E.ch])
                    if f % 4 == 3:
                        ins.then_inc(sem("wv_tr"), 1)

        def act_va(act, E):
            act.wait_ge(sem("table_out0"), 16 * table_parts(1, NCH + NCH % 2))
            act.wait_ge(sem("table_out1"), 16 * table_parts(1, NCH + 1 - NCH % 2))
            for c in range(NCH):
                act.wait_ge(sem("va_tr"), c + 1)
                if c >= 2:
                    act.wait_ge(sem(f"table_out{c % 2}"), 16 * table_parts(2, c))
                A(tabn[:, c % 2, 0:chunk(c) * 2 * HEADS], bank(c % 2, chunk(c) * 2 * HEADS)[0:NP_, :], ACT.Copy)\
                    .then_inc(sem("va_ev"), 1)
            for c in range(E.nc):
                for g in range(2):
                    act.wait_ge(sem("wv_tr"), 2 * c + g + 1)
                    A(wtv[:, c * E.ch:(c + 1) * E.ch, 4 * g:4 * g + 4].rearrange("p t f -> p f t"),
                      bank(2 + 2 * (c % 2) + g, 4 * E.ch).rearrange("p (f t) -> p f t", f=4), ACT.Copy)\
                        .then_inc(sem("wv_ev"), 1)

        def dve_va(dve, chain, E):
            dve.wait_ge(sem("wv_in"), 16 * E.nc)
            for c in range(E.nc):
                if c >= 2:
                    dve.wait_ge(sem("wv_tr"), 2 * (c - 1))
                wide = [E.ch, 4, WIN]
                for f in range(2 * HEADS):
                    ins = V.tensor_tensor(
                        work[0:E.ch, c % 2, f, :].rearrange("p (a b) -> p a b", b=WIN),
                        winv[0:E.ch, c, :].rearrange("p (j f) -> p f j", f=2 * HEADS)[:, f:f + 1, :].to_broadcast(wide),
                        m4[0:E.ch, :].unsqueeze(2).to_broadcast(wide), ALU.mult)
                ins.then_inc(sem("wv_spread"), 1)

        def sp_va(sp, E):
            for c in range(NCH):
                sp.wait_ge(sem("va_ev"), c + 1)
                sp.dma_start(va_tab[cols(c), :].rearrange("(i p) f -> p i f", p=NP_),
                             tabn[:, c % 2, 0:chunk(c) * 2 * HEADS].rearrange("p (a b) -> p a b", b=2 * HEADS))\
                    .then_inc(sem(f"table_out{c % 2}"), 16)

        def pool_va(pool, E):
            pool.wait_ge(sem("table_out0"), 16 * table_parts(2, NCH + NCH % 2))
            pool.wait_ge(sem("table_out1"), 16 * table_parts(2, NCH + 1 - NCH % 2))
            pool.wait_ge(sem("va_tail"), 16)
            for c in range(E.nc):
                nc.gpsimd.indirect_dma_start(
                    out=winv[0:E.ch, c, :], out_offset=None, in_=va_tab,
                    in_offset=bass.IndirectOffsetOnAxis(ap=base_i[0:E.ch, c:c + 1], axis=0))\
                    .then_inc(sem("wv_in"), 16)

        def ring_loop(eng, E, body):
            with eng.Fori(0, E.rounds // 2) as j:
                body(j, range(4))
            if E.rounds % 2:
                body(E.rounds // 2, range(2))

        def ring_tiles(j, s, k=0, n=HALF):
            return bass.ds(j * (4 * HALF) + (s * HALF + k), n)

        def sp_soft(sp, E):
            for h in range(2):
                sp.wait_ge(sem(f"stashed{h}"), 16 * E.rounds)

            def fetch(j, places):
                for s in places:
                    sp.wait_ge(sem(f"msg_ready{s}"), j + 1)
                    sp.dma_start(packed[:, s], stash[bass.ds(j * (4 * TILE) + s * TILE, TILE), :, :])\
                        .then_inc(sem(f"fetched{s}"), 16)
            ring_loop(sp, E, fetch)

        def pe_soft(pe, E):
            pe.wait_ge(sem("wv_ev"), 2 * E.nc)
            pe.wait_ge(sem("va_ev"), NCH)
            for s in range(4):
                pe.sem_inc(sem(f"msg_ready{s}"), 1)

            def destinations(j, places):
                def turn(s):
                    pe.wait_ge(sem("oh2_copy"), j * 4 + (s + 1))
                    for q in range(2):
                        ins = nc.tensor.transpose(bank(s, TILE, q * TILE),
                                                  ohs4[s][:, 4 * q:4 * q + 4, :].rearrange("p a b -> p (a b)"),
                                                  ident[:, :])
                    ins.then_inc(sem("oh2_tr"), 1)

                def look_up(s):
                    pe.wait_ge(sem("oh2_tr_ev"), j * 4 + (s + 1))
                    for q in range(2):
                        ins = M(bank(4 + s, 32, 32 * q), ohT4[:, s, q * TILE:(q + 1) * TILE],
                                wtv[:, ring_tiles(j, s, 4 * q, 4), :].rearrange("p a b -> p (a b)"),
                                start=True, stop=True, skip_group_check=True)
                    ins.then_inc(sem("va_edge"), 1)
                for s in places:
                    turn(s)
                    if s:
                        look_up(s - 1)
                look_up(places[-1])
            ring_loop(pe, E, destinations)
            pe.wait_ge(sem("va_taken"), 2 * E.rounds)
            pe_clear(C + HEADS)
            pe.sem_inc(sem("scattered6"), 2)

            def scatter(j, places):
                for s in places:
                    pe.reg_load(pe_regs, off_row[:, ring_tiles(j, s)])
                    at = [pe.snap(r, min_val=0, max_val=NB * BANK - WIN) for r in pe_regs]
                    pe.wait_ge(sem(f"msg_ready{s}"), j + 2)
                    pe.wait_ge(sem("w_copied"), j * 4 + (s + 1))
                    for k in range(HALF):
                        rhs = onehot[:, ring_tiles(j, s, k, 1), :].rearrange("p a b -> p (a b)")
                        ins = pe_scatter(at[k], C + HEADS, work[:, s % 2, k, 0:C + HEADS], rhs)
                    ins.then_inc(sem("scattered6"), 1)
            ring_loop(pe, E, scatter)
            M(bank(7, 8)[0:1, :], zeros[:, 0:1], zeros[:, 0:8], start=True, stop=True)\
                .then_inc(sem("summed"), 1)
            pe.wait_ge(sem("sums_ready"), 5 * NB)
            for c in range(NCH):
                if c >= 2:
                    pe.wait_ge(sem("o_ev"), c - 1)
                for j, t in enumerate(tiles(c)):
                    ins = nc.tensor.transpose(bank(c % 2, C + HEADS, j * (C + HEADS))[0:NP_, :],
                                              agg[0:C + HEADS, t * NP_:(t + 1) * NP_],
                                              ident[0:C + HEADS, 0:C + HEADS])
                ins.then_inc(sem("o_tr"), 1)

        def act_soft(act, E):
            act.sem_inc(sem("oh2_tr_ev0"), 4)

            def copy_onehots(j, places):
                for s in places:
                    act.wait_ge(sem("oh2_tr_ev0"), j * 4 + (s + 1))
                    A(ohs4[s], onehot[:, ring_tiles(j, s), :], ACT.Copy).then_inc(sem("oh2_copy"), 1)
            ring_loop(act, E, copy_onehots)
            for n, at in soft_parts(E):
                act.wait_ge(sem("d_ready"), n + 1)
                A(wtv[:, at, 0:HEADS], su[:, at, :], ACT.Exp).then_inc(sem("w_ready"), 1)
            act.wait_ge(sem("w_ready"), 2)

            def copy_weights(j, places):
                for s in places:
                    act.wait_ge(sem("scattered6"), j * 4 + (s + 1))
                    A(work[:, s % 2, :, C:C + HEADS], wtv[:, ring_tiles(j, s), 0:HEADS], ACT.Copy)\
                        .then_inc(sem("w_copied"), 1)
            ring_loop(act, E, copy_weights)

        def soft_parts(E):
            return ((0, slice(0, E.t // 2)), (1, slice(E.t // 2, E.t)))

        def dve_soft(dve, chain, E):
            def take(j, places):
                for s in places:
                    dve.wait_ge(sem("oh2_tr"), j * 4 + (s + 1))
                    V.tensor_copy(ohT4[:, s, :], bank(s, HALF * WIN)).then_inc(sem("oh2_tr_ev"), 1)
                    dve.wait_ge(sem("oh2_tr_ev"), j * 4 + (s + 1))
                    dve.sem_inc(sem("oh2_tr_ev0"), 1)
                    if s:
                        take_values(j, s - 1)
                take_values(j, places[-1])

            def take_values(j, s):
                dve.wait_ge(sem("va_edge"), j * 4 + (s + 1))
                V.tensor_copy(wtv[:, ring_tiles(j, s), :],
                              bank(4 + s, HALF * 2 * HEADS).rearrange("p (t f) -> p t f", f=2 * HEADS))\
                    .then_inc(sem("va_taken"), 1)
            ring_loop(dve, E, take)
            dve.wait_ge(sem("va_taken"), 2 * E.rounds)
            for n, at in soft_parts(E):
                s = su[:, at, :]
                chain(V.tensor_tensor(s, s, wtv[:, at, 0:HEADS], ALU.add))
                chain(V.scalar_tensor_tensor(out=s, in0=s, scalar=NEG_SLOPE, in1=s, op0=ALU.mult, op1=ALU.max))
                chain(V.tensor_tensor(s, s, wtv[:, at, HEADS:2 * HEADS], ALU.subtract))
                V.tensor_scalar(s, s, 0.0, None, ALU.min).then_inc(sem("d_ready"), 1)
            for n, at in soft_parts(E):
                dve.wait_ge(sem("w_ready"), n + 1)
                n_at = at.stop - at.start
                chain(V.tensor_tensor(su[:, at, :], wtv[:, at, 0:HEADS],
                                      sg[:, at].unsqueeze(2).to_broadcast([TILE, n_at, HEADS]), ALU.mult))

            def weigh(j, places):
                for s in places:
                    dve.wait_ge(sem(f"fetched{s}"), j * 16 + 16)
                    dve.wait_ge(sem("scattered6"), j * 4 + (s + 1))
                    V.tensor_tensor(
                        work[:, s % 2, :, 0:C].rearrange("p a (k d) -> p a k d", d=HD),
                        packed[:, s].rearrange("p a (k d) -> p a k d", d=HD),
                        su[:, ring_tiles(j, s), :].unsqueeze(3).to_broadcast([TILE, HALF, HEADS, HD]),
                        ALU.mult).then_inc(sem(f"msg_ready{s}"), 1)
            ring_loop(dve, E, weigh)
            dve_sums(dve, chain, 4, C + HEADS)
            for c in range(NCH):
                n = chunk(c)
                dve.wait_ge(sem("o_tr"), c + 1)
                got = bank(c % 2, n * (C + HEADS))[0:NP_, :].rearrange("p (a b) -> p a b", b=C + HEADS)
                den = tabn[:, 0, 0:n * HEADS].rearrange("p (a b) -> p a b", b=HEADS)
                y = yn[:, c * CH:c * CH + n, :]
                chain(V.tensor_scalar(den, got[:, :, C:C + HEADS], 1e-16, None, ALU.max))
                chain(V.reciprocal(den, den))
                V.tensor_tensor(y.rearrange("p a (k d) -> p a k d", d=HD),
                                got[:, :, 0:C].rearrange("p a (k d) -> p a k d", d=HD),
                                den.unsqueeze(3).to_broadcast([NP_, n, HEADS, HD]), ALU.mult)\
                    .then_inc(sem("o_ev"), 1)
                dve.wait_ge(sem("o_ev"), c + 1)
                chain(V.tensor_tensor(y, y, xn[:, c * CH:c * CH + n, :], ALU.add))
            dve_norm(dve, chain, 2)

        PAIRS = [(c, j) for c in range(NCH) for j in range(0, chunk(c), 2)]

        def pe_rel(pe, E):
            for step in range(NCH + 1):
                if step < NCH:
                    pe_back(pe, 2, step)
                if step >= 1:
                    c = step - 1
                    pe.wait_ge(sem("back_ev"), 2 * NCH + c + 1)
                    for n, (cc, j) in enumerate(PAIRS):
                        if cc != c:
                            continue
                        if n >= 4:
                            pe.wait_ge(sem("rel_ev"), n - 3)
                        for k in range(min(2, chunk(c) - j)):
                            t = c * CH + j + k
                            ins = M(bank(2 + n % 4, RELS * C, k * RELS * C)[0:NP_, :],
                                    xt[:, t * NP_:(t + 1) * NP_], wrel[:, :, :].rearrange("p r c -> p (r c)"),
                                    start=True, stop=True, skip_group_check=True)
                        ins.then_inc(sem("rel_mm"), 1)
            pe.wait_ge(sem("rel_ev"), len(PAIRS))
            pe_clear(C)
            for h in range(2):
                pe.sem_inc(sem(f"scattered5{h}"), 1)
            with pe.Fori(0, E.rounds) as i:
                for h in range(2):
                    at = pe_windows(pe, i, h)
                    pe.wait_ge(sem("weighted"), i * 2 + (h + 1))
                    pe.wait_ge(sem(f"landed{h}"), E.landed(5, i))
                    for k in range(HALF):
                        ins = pe_scatter(at[k], C, rows[:, h, k, 0:C], msk[:, h, k, :])
                    ins.then_inc(sem(f"scattered5{h}"), 1)
            M(bank(7, 8)[0:1, :], zeros[:, 0:1], zeros[:, 0:8], start=True, stop=True)\
                .then_inc(sem("summed"), 1)
            pe.wait_ge(sem("sums_ready"), 6 * NB)
            for c in range(NCH):
                pe.wait_ge(sem("y_ready"), c + 1)
                if c >= 2:
                    pe.wait_ge(sem("y_ev"), c - 1)
                for j, t in enumerate(tiles(c)):
                    ins = nc.tensor.transpose(bank(c % 2, C, j * C)[0:NP_, :], y1[0:C, t * NP_:(t + 1) * NP_],
                                              ident[0:C, 0:C])
                ins.then_inc(sem("y_tr"), 1)

        def act_rel(act, E):
            act_norm(act, 2)
            for step in range(NCH + 1):
                if step < NCH:
                    act_back(act, 2, step)
                if step >= 1:
                    c = step - 1
                    if c >= 2:
                        act.wait_ge(sem(f"table_out{c % 2}"), 16 * table_parts(3, c))
                    for n, (cc, j) in enumerate(PAIRS):
                        if cc == c:
                            m = min(2, chunk(c) - j) * RELS * C
                            act.wait_ge(sem("rel_mm"), n + 1)
                            A(tabn[:, c % 2, j * RELS * C:j * RELS * C + m], bank(2 + n % 4, m)[0:NP_, :],
                              ACT.Copy).then_inc(sem("rel_ev"), 1)
            stage_first(act, E, 5, rel_i)
            act.wait_ge(sem("bn_mean"), 1)
            A(y1[0:C, 0:N], xt[:, :], ACT.Square, bias=bnst[:, 1:2], accum_out=bnst[:, 2:3])\
                .then_inc(sem("bn_square"), 1)
            act.wait_ge(sem("bn_var"), 1)
            A(bnst[:, 4:5], bnst[:, 3:4], ACT.Sqrt).then_inc(sem("bn_sd"), 1)
            with act.Fori(0, E.rounds) as i:
                for h in range(2):
                    act.wait_ge(sem(f"scattered5{h}"), i + 2)
                    stage_next(5, rel_i, i, h)
            for step in range(NCH + 2):
                if step < NCH:
                    c = step
                    act.wait_ge(sem("hbn"), c + 1)
                    A(y1[0:C, cols(c)], y1[0:C, cols(c)], ACT.Relu, bias=bnst[:, 7:8])\
                        .then_inc(sem("relu_out"), 1)
                if step >= 2:
                    c = step - 2
                    act.wait_ge(sem("y_tr"), c + 1)
                    A(yn[:, c * CH:c * CH + chunk(c), :].rearrange("p a b -> p (a b)"),
                      bank(c % 2, chunk(c) * C)[0:NP_, :], ACT.Copy).then_inc(sem("y_ev"), 1)
            act_norm(act, 3)

        def dve_rel(dve, chain, E):
            dve.wait_ge(sem("back_ev"), 3 * NCH)
            chain(V.tensor_reduce(bnst[:, 0:1], xt[:, :], AX, ALU.add))
            V.tensor_scalar(bnst[:, 1:2], bnst[:, 0:1], -1.0 / N, None, ALU.mult).then_inc(sem("bn_mean"), 1)
            dve.wait_ge(sem("bn_square"), 1)
            V.tensor_scalar(bnst[:, 3:4], bnst[:, 2:3], 1.0 / N, 1e-05, ALU.mult, ALU.add)\
                .then_inc(sem("bn_var"), 1)
            dve.wait_ge(sem("bn_sd"), 1)
            chain(V.reciprocal(bnst[:, 5:6], bnst[:, 4:5]))
            chain(V.tensor_tensor(bnst[:, 6:7], bnst[:, 5:6], prm[0:C, P_GAMMA:P_GAMMA + 1], ALU.mult))
            V.scalar_tensor_tensor(out=bnst[:, 7:8], in0=bnst[:, 1:2], scalar=bnst[:, 6:7],
                                   in1=prm[0:C, P_BETA:P_BETA + 1], op0=ALU.mult, op1=ALU.add)\
                .then_inc(sem("bn_ready"), 1)
            with dve.Fori(0, E.rounds) as i:
                for h in range(2):
                    dve.wait_ge(sem(f"scattered5{h}"), i + 1)
                    V.tensor_tensor(msk[:, h], onehot[:, half_tiles(i, h), :],
                                    wgt[:, half_tiles(i, h)].unsqueeze(2).to_broadcast([TILE, HALF, WIN]),
                                    ALU.mult).then_inc(sem("weighted"), 1)
            dve_sums(dve, chain, 5, C)
            dve.wait_ge(sem("bn_ready"), 1)
            dve.wait_ge(sem("sums_ready"), 6 * NB)
            for step in range(NCH + 1):
                if step < NCH:
                    c = step
                    V.scalar_tensor_tensor(out=y1[0:C, cols(c)], in0=xt[:, cols(c)], scalar=bnst[:, 6:7],
                                           in1=agg[0:C, cols(c)], op0=ALU.mult, op1=ALU.add)\
                        .then_inc(sem("hbn"), 1)
                if step >= 1:
                    c = step - 1
                    dve.wait_ge(sem("relu_out"), c + 1)
                    V.tensor_tensor(y1[0:C, cols(c)], y1[0:C, cols(c)], xt[:, cols(c)], ALU.add)\
                        .then_inc(sem("y_ready"), 1)
            dve_norm(dve, chain, 3, lambda part: (sem("y_ev"), (4, NCH)[part]))

        def sp_rel(sp, E):
            for c in range(NCH):
                sp.wait_ge(sem("rel_ev"), sum(1 for cc, _ in PAIRS if cc <= c))
                for r in range(RELS):
                    sp.dma_start(
                        rel_tab[r * N + cols(c).start:r * N + cols(c).stop, :].rearrange("(i p) f -> p i f", p=NP_),
                        tabn[:, c % 2, 0:chunk(c) * RELS * C].rearrange("p (a b) -> p a b", b=RELS * C)
                        [:, :, r * C:(r + 1) * C]).then_inc(sem(f"table_out{c % 2}"), 16)

        def pool_rel(pool, E):
            pool.wait_ge(sem("table_out0"), 16 * table_parts(3, NCH + NCH % 2))
            pool.wait_ge(sem("table_out1"), 16 * table_parts(3, NCH + 1 - NCH % 2))
            pool_gather(pool, E, 5, rel_tab, C)

        def sp_out(sp):
            for part, (a, b) in enumerate(PARTS):
                sp.wait_ge(sem("xn_ready"), 7 + part)
                sp.dma_start(out[a * NP_:b * NP_, :].rearrange("(i p) f -> p i f", p=NP_), xn[:, a:b, :])\
                    .then_inc(sem("out_done"), 16)
            sp.wait_ge(sem("out_done"), 32)

        scratch = onehot[:, :, :].rearrange("p t j -> p (t j)")
        TG = T_GIVEN
        blk, member, rank, place = (scratch[:, k * TG:(k + 1) * TG] for k in range(4))
        blk_i = scratch[:, 4 * TG:5 * TG].bitcast(I32)
        place_i = scratch[:, 5 * TG:6 * TG].bitcast(I32)
        rest = scratch[:, 6 * TG:]
        RECORD = 4 + FE
        rec = rest[:, 0:HALF * RECORD].rearrange("p (k f) -> p k f", f=RECORD)
        rec_i = rest[:, 0:HALF * RECORD].bitcast(I32).rearrange("p (k f) -> p k f", f=RECORD)
        empty = rest[:, 320:320 + HALF * RECORD].rearrange("p (k f) -> p k f", f=RECORD)
        empty_i = rest[:, 320:320 + HALF * RECORD].bitcast(I32).rearrange("p (k f) -> p k f", f=RECORD)
        place_st = rest[:, 640:640 + HALF].bitcast(I32)
        lower = rest[:, 704:704 + 128]
        at_blk, first, held, before, full = (rest[:, 840 + k:841 + k] for k in range(5))
        full_i = rest[:, 848:849].bitcast(I32)
        spare = rest[:, 849:850]
        attr_s = rest[0:FE, 1024:1024 + HALF * TILE]
        dst_f = rest[:, 2048:2048 + T_SORTED]

        def dve_sort(dve, chain):
            dve.wait_ge(sem("edges_in"), 64)
            chain(V.memset(empty, 0.0))
            V.memset(empty_i[:, :, 1:2], FAR).then_inc(sem("empty_ready"), 1)
            chain(V.tensor_scalar(lower, iota_f[:, :], pidx_f[:, 0:1], None, ALU.is_gt))
            chain(V.tensor_scalar(blk_i, dst_i[:, 0:TG], WIN.bit_length() - 1, None, ALU.logical_shift_right))
            chain(V.tensor_copy(blk, blk_i))
            chain(V.memset(place, 0.0))
            chain(V.memset(rest[:, 840:850], 0.0))
            with chain.loop(BLOCKS, 13) as i:
                chain(V.tensor_scalar(member, blk, at_blk, None, ALU.is_equal))
                chain(V.tensor_tensor_scan(rank, member, member, 0.0, ALU.add, ALU.bypass))
                V.tensor_copy(held, rank[:, TG - 1:TG]).then_inc(sem("held"), 1)
                dve.wait_ge(sem("held_sums"), i + 1)
                chain(V.tensor_scalar(before, bank(0, 1), first, -1.0, ALU.add, ALU.add))
                chain(V.tensor_scalar(full, bank(0, 1, 1), float(TILE - 1), None, ALU.add))
                chain(V.tensor_scalar(rank, rank, before, None, ALU.add))
                chain(V.tensor_tensor(rank, rank, member, ALU.mult))
                chain(V.tensor_tensor(place, place, rank, ALU.add))
                chain(V.tensor_copy(full_i, full))
                chain(V.tensor_scalar(full_i, full_i, 7, None, ALU.logical_shift_right))
                chain(V.tensor_scalar(full_i, full_i, 7, None, ALU.logical_shift_left))
                chain(V.tensor_copy(full, full_i))
                chain(V.tensor_tensor(first, first, full, ALU.add))
                chain(V.tensor_scalar(at_blk, at_blk, 1.0, None, ALU.add))
            chain(V.tensor_scalar(spare, pidx_f[:, 0:1], float(T_SORTED * TILE), None, ALU.add))
            chain(V.tensor_scalar(member, blk, float(FAR // WIN), spare, ALU.is_equal, ALU.mult))
            chain(V.tensor_tensor(place, place, member, ALU.add))
            V.tensor_copy(place_i, place).then_inc(sem("places"), 1)
            E = ordered
            for c in range(E.nc):
                dve.wait_ge(sem("dst_tr"), c + 1)
                V.tensor_copy(dst_tm[0:E.ch, c, :], bank(3 + c % 2, TILE)[0:E.ch, :])\
                    .then_inc(sem("dst_tr_ev"), 1)
            dve.wait_ge(sem("dst_tr_ev"), E.nc)
            dve_min_max(dve, chain, E)

        def pe_sort(pe):
            pe.wait_ge(sem("empty_ready"), 1)
            with pe.Fori(0, BLOCKS) as i:
                pe.wait_ge(sem("held"), i + 1)
                M(bank(0, 1), lower, held, start=True, stop=True, skip_group_check=True)
                M(bank(0, 1, 1), ones[:, :], held, start=True, stop=True, skip_group_check=True)\
                    .then_inc(sem("held_sums"), 1)
            with pe.Fori(0, T_SORTED // HALF) as i:
                pe.wait_ge(sem("rec_back"), i * 16 + 16)
                for k in range(HALF):
                    ins = nc.tensor.transpose(bank(1 + k // 4, TILE, (k % 4) * TILE)[0:FE, :],
                                              rec[:, k, 4:RECORD], ident[:, :])
                ins.then_inc(sem("attr_tr"), 1)
            for c in range(ordered.nc):
                pe.wait_ge(sem("dst_back"), 1)
                if c >= 2:
                    pe.wait_ge(sem("dst_tr_ev"), c - 1)
                nc.tensor.transpose(bank(3 + c % 2, TILE)[0:ordered.ch, :],
                                    dst_f[:, c * ordered.ch:(c + 1) * ordered.ch], ident[:, :])\
                    .then_inc(sem("dst_tr"), 1)

        def act_sort(act):
            act.wait_ge(sem("consts"), 8)
            act.wait_ge(sem("edges_in"), 64)
            act.wait_ge(sem("places"), 1)
            act.sem_inc(sem("rec_free"), 1)
            with act.Fori(0, T_GIVEN // HALF) as i:
                act.wait_ge(sem("rec_free"), i + 1)
                eight = bass.ds(i * HALF, HALF)
                A(place_st, place_i[:, eight], ACT.Copy).then_inc(sem("rec_cols"), 1)
                for f, of in enumerate((src_i, dst_i, rel_i)):
                    A(rec_i[:, :, f], of[:, eight], ACT.Copy).then_inc(sem("rec_cols"), 1)
                A(rec[:, :, 3], wgt[:, eight], ACT.Copy).then_inc(sem("rec_cols"), 1)
            with act.Fori(0, T_SORTED // HALF) as i:
                act.wait_ge(sem("rec_back"), i * 16 + 16)
                eight = bass.ds(i * HALF, HALF)
                for f, to in enumerate((src_i, dst_i, rel_i)):
                    A(to[:, eight], rec_i[:, :, f], ACT.Copy)
                A(dst_f[:, eight], rec_i[:, :, 1], ACT.Copy)
                A(wgt[:, eight], rec[:, :, 3], ACT.Copy)
                act.wait_ge(sem("attr_tr"), i + 1)
                act.wait_ge(sem("attr_stored"), i * 16 + 16)
                A(attr_s, ps[0:FE, BANK:3 * BANK], ACT.Copy).then_inc(sem("attr_back"), 1)
            act.wait_ge(sem("attr_back"), T_SORTED // HALF + 1)
            act.wait_ge(sem("attr_stored"), 16 * (T_SORTED // HALF + 1))
            act.sem_inc(sem("dst_back"), 1)

        def sp_sort(sp):
            sp.wait_ge(sem("empty_ready"), 1)
            with sp.Fori(0, T_SORTED // HALF + 1) as i:
                sp.dma_start(records[bass.ds(i * (HALF * TILE), HALF * TILE), :]
                             .rearrange("(k p) f -> p k f", p=TILE), empty).then_inc(sem("emptied"), 16)
            with sp.Fori(0, T_GIVEN // HALF) as i:
                sp.wait_ge(sem("rec_free"), i + 1)
                sp.dma_start(rec[:, :, 4:RECORD], I["attr_r"][bass.ds(i * (HALF * TILE), HALF * TILE), :]
                             .rearrange("(k p) f -> p k f", p=TILE)).then_inc(sem("rec_attr"), 16)
            sp.wait_ge(sem("rec_free"), T_GIVEN // HALF + 1)
            sp.sem_inc(sem("attr_back"), 1)
            sp.sem_inc(sem("attr_stored"), 16)
            with sp.Fori(0, T_SORTED // HALF) as i:
                at = sp.snap(i * (HALF * TILE), min_val=0, max_val=(T_SORTED - HALF) * TILE)
                sp.wait_ge(sem("attr_back"), i + 1)
                sp.dma_start(rec, records[bass.ds(at, HALF * TILE), :]
                             .rearrange("(k p) f -> p k f", p=TILE)).then_inc(sem("rec_back"), 16)
                sp.wait_ge(sem("attr_back"), i + 2)
                sp.sem_inc(sem("store_started"), 1)
                sp.dma_start(attr_sorted[:, bass.ds(at, HALF * TILE)], attr_s)\
                    .then_inc(sem("attr_stored"), 16)
            sp.wait_ge(sem("attr_stored"), 16 * (T_SORTED // HALF + 1))

        def pool_sort(pool):
            pool.wait_ge(sem("emptied"), 16 * (T_SORTED // HALF + 1))
            with pool.Fori(0, T_GIVEN // HALF) as i:
                pool.wait_ge(sem("rec_attr"), i * 16 + 16)
                pool.wait_ge(sem("rec_cols"), i * 5 + 5)
                pool.sem_inc(sem("gather_started"), 1)
                for k in range(HALF):
                    nc.gpsimd.indirect_dma_start(
                        out=records, out_offset=bass.IndirectOffsetOnAxis(ap=place_st[:, k:k + 1], axis=0),
                        in_=rec[:, k, :], in_offset=None).then_inc(sem("scattered_rec"), 16)
                pool.wait_ge(sem("scattered_rec"), i * (16 * HALF) + 16 * HALF)
                pool.sem_inc(sem("rec_free"), 1)

        def fits(eng):
            eng.wait_ge(sem("flag"), 1)
            return eng.value_load(flag[0:1, 0:1], min_val=0, max_val=1)

        def sp_passes(sp, E):
            sp_gin(sp, E)
            sp_edge(sp, E)
            sp_att_tables(sp, E)
            sp_signs(sp, E)
            sp_va(sp, E)
            sp_soft(sp, E)
            sp_rel(sp, E)
            sp_out(sp)

        def pool_passes(pool, E):
            pool_gin(pool, E)
            pool_edge(pool, E)
            pool_att_tables(pool, E)
            pool_gather(pool, E, 4, att_tab, ROW2)
            pool_va(pool, E)
            pool_rel(pool, E)

        def act_passes(act, E):
            act_gin(act, E)
            act_edge(act, E)
            act_att_tables(act, E)
            act_signs(act, Chain(act, sem("act")), E)
            act_va(act, E)
            act_soft(act, E)
            act_rel(act, E)

        def dve_passes(dve, chain, E):
            dve_edges(dve, chain, E)
            dve_gin(dve, chain, E)
            dve_edge(dve, chain, E)
            dve_att_tables(dve, chain, E)
            dve_signs(dve, chain, E)
            dve_va(dve, chain, E)
            dve_soft(dve, chain, E)
            dve_rel(dve, chain, E)

        def pe_passes(pe, E):
            pe_edges(pe, E)
            pe_gin(pe, E)
            pe_edge(pe, E)
            pe_att_tables(pe, E)
            pe_signs(pe, E)
            pe_va(pe, E)
            pe_soft(pe, E)
            pe_rel(pe, E)

        block = ctx.enter_context(nc.Block())

        @block.sync
        def _(sp):
            sp_start(sp)
            with sp.If(fits(sp)):
                sp_passes(sp, given)
            with sp.Else():
                sp_sort(sp)
                sp_passes(sp, ordered)

        @block.gpsimd
        def _(pool):
            pool_start(pool)
            with pool.If(fits(pool)):
                pool_passes(pool, given)
            with pool.Else():
                pool_sort(pool)
                pool_passes(pool, ordered)

        @block.scalar
        def _(act):
            with act.If(fits(act)):
                act_passes(act, given)
            with act.Else():
                act_sort(act)
                act_passes(act, ordered)

        @block.vector
        def _(dve):
            nonlocal dve_regs
            dve_regs = [dve.alloc_register(f"base{k}") for k in range(HALF)]
            chain = Chain(dve, sem("dve"))
            dve_start(dve, chain)
            steps = chain.n
            with dve.If(fits(dve)):
                dve_passes(dve, chain, given)
            with dve.Else():
                chain.n = steps
                dve_sort(dve, chain)
                dve_passes(dve, chain, ordered)

        @block.tensor
        def _(pe):
            nonlocal pe_regs
            pe_regs = [pe.alloc_register(f"window{k}") for k in range(HALF)]
            pe_start(pe)
            with pe.If(fits(pe)):
                pe_passes(pe, given)
            with pe.Else():
                pe_sort(pe)
                pe_passes(pe, ordered)


def lay_out(inputs):
    import numpy as np

    a = {k: np.asarray(v) for k, v in inputs.items()}
    pad = T_GIVEN * TILE - E_EDGES

    def tiled(v, fill):
        return np.ascontiguousarray(np.pad(v, (0, pad), constant_values=fill).reshape(T_GIVEN, TILE).T)

    dst = np.pad(a["dst"], (0, pad), constant_values=FAR).reshape(4, T_GIVEN // 4, TILE)
    prm = np.zeros((128, P_COLS), np.float32)
    for at, name in ((P_B1, "L0_gnn_b1"), (P_G1, "L0_gnn_g1"), (P_BE1, "L0_gnn_be1"), (P_B2, "L0_gnn_b2"),
                     (P_G2, "L0_gnn_g2"), (P_BE2, "L0_gnn_be2"), (P_BNG, "L0_gnn_bn_g"),
                     (P_BNB, "L0_gnn_bn_be")):
        prm[0:C, at:at + 3] = a[name].T
    prm[0:C, P_EPS:P_EPS + 3] = a["L0_gnn_eps"][None, :]
    prm[:, P_L1B3] = a["L1_gnn_b3"]
    for at, name in ((P_BL, "L2_gnn_bl"), (P_BD, "L2_gnn_bd"),
                     (P_GAMMA, "L3_gnn_gamma"), (P_BETA, "L3_gnn_beta")):
        prm[0:C, at] = a[name]
    prm[:, P_BA], prm[:, P_BF] = a["L2_gnn_ba"][0], a["L2_gnn_bf"][0]
    prm[0:C, P_WF:P_WF + 3] = a["L2_gnn_Wf"].reshape(3, C).T
    for k in range(HEADS):
        prm[k * HD:(k + 1) * HD, P_A1 + k] = a["L2_gnn_Wa"][0:HD, 0]
        prm[k * HD:(k + 1) * HD, P_A2 + k] = a["L2_gnn_Wa"][HD:2 * HD, 0]
    got = {
        "x": a["x"], "x_t": np.ascontiguousarray(a["x"].T), "params": prm,
        "src_e": tiled(a["src"], 0), "dst_e": tiled(a["dst"], FAR), "rel_e": tiled(a["edge_type_3"], 0),
        "wgt_e": tiled(a["edge_weight"], 0), "dst_t": np.ascontiguousarray(dst.transpose(1, 0, 2)),
        "attr_r": np.pad(a["edge_attr_32"], ((0, pad), (0, 0))),
        "attr_t": np.ascontiguousarray(np.pad(a["edge_attr_32"], ((0, pad), (0, 0))).T),
        "b1_row": a["L1_gnn_b1"][None, :],
        "brow": np.concatenate([a["L1_gnn_b2"], a["L1_gnn_b4"]])[None, :],
        "nought": np.zeros((WIN, WIN), np.float32),
    }
    for name in ("L0_gnn_W1", "L0_gnn_W2", "L1_gnn_W1", "L1_gnn_W2", "L1_gnn_W3", "L1_gnn_W4",
                 "L2_gnn_Wl", "L2_gnn_Wd", "L3_gnn_weight"):
        got[name] = a[name]
    return got


def kernel(**inputs):
    import numpy as np
    import concourse.bacc as bacc
    from concourse.bass_utils import run_bass_kernel_spmd

    arrays = {f"in_{k}": v for k, v in lay_out(inputs).items()}
    nc = bacc.Bacc("TRN2", target_bir_lowering=False, num_devices=1)
    args = {k[3:]: nc.dram_tensor(k, v.shape, mybir.dt.from_np(v.dtype), kind="ExternalInput").ap()
            for k, v in arrays.items()}
    out = nc.dram_tensor("out", [N, C], F32, kind="ExternalOutput").ap()
    build(nc, args, out)
    got = run_bass_kernel_spmd(nc, [arrays], core_ids=[0])
    return np.asarray(got.results[0]["out"])
```

```python
from contextlib import ExitStack, contextmanager

import concourse.bass as bass
from concourse import mybir
from concourse.alu_op_type import AluOpType as ALU

F32 = mybir.dt.float32
I32 = mybir.dt.int32
BF16 = mybir.dt.bfloat16
ACT = mybir.ActivationFunctionType
AX = mybir.AxisListType.X

N = 3125
C = 64
E_EDGES = 53125
FE = 32
HID = 128
HEADS, HD = 4, 16
RELS = 3
TILE = 128
WIN = 32
NP_, NT = 125, 25
BANK = 512
STEP = BANK - WIN
NB = -(-N // STEP)
HALF = 8
BODY = 2 * HALF
T_GIVEN = -(-E_EDGES // (TILE * BODY)) * BODY
BLOCKS = -(-N // WIN)
T_SORTED = -(-(T_GIVEN + BLOCKS) // BODY) * BODY
CH = 4
NCH = -(-NT // CH)
ROW2 = C + 2 * HEADS + 2
FAR = 1 << 20
BIG = 1.0e30
NEG_SLOPE = 0.01
BN_C = 1.0 / (1.0 + 1e-05) ** 0.5
N_LOADS = 16
P_B1, P_G1, P_BE1, P_B2, P_G2, P_BE2, P_BNG, P_BNB, P_EPS = range(0, 27, 3)
P_L1B3, P_BL, P_BD, P_GAMMA, P_BETA, P_BA, P_BF = range(27, 34)
P_WF, P_A1, P_A2, P_COLS = 34, 37, 41, 45


def cols(c):
    return slice(c * CH * NP_, min((c + 1) * CH, NT) * NP_)


def tiles(c):
    return range(c * CH, min((c + 1) * CH, NT))


class Chain:

    def __init__(self, eng, sem):
        self.eng, self.sem, self.n, self.i = eng, sem, 0, None

    def __call__(self, ins):
        ins.then_inc(self.sem, 1)
        self.n += 1
        if self.i is None:
            self.eng.wait_ge(self.sem, self.n)
        else:
            self.eng.wait_ge(self.sem, self.i * self.per + self.n)

    @contextmanager
    def loop(self, rounds, per):
        before = self.n
        with self.eng.Fori(0, rounds) as i:
            self.i, self.per = i, per
            yield i
            assert self.n == before + per, (self.n - before, per)
        self.i, self.n = None, before + per * rounds


class Edges:

    def __init__(self, t, ch, src, dst, rel, wgt, dst_t, attr):
        self.t, self.ch, self.nc, self.rounds = t, ch, t // ch, t // BODY
        self.src, self.dst, self.rel, self.wgt, self.dst_t, self.attr = src, dst, rel, wgt, dst_t, attr
        assert self.nc * ch == t and ch % 4 == 0 and ch <= 128 and self.nc <= 6

    def landed(self, s, i):
        return i * (16 * HALF) + (s * self.rounds + 1) * (16 * HALF)

    def staged(self, s, i):
        return i + (s * (self.rounds + 1) + 1)


def build(nc, I, out):
    def dram(name, shape, dt=F32):
        return nc.dram_tensor(name, shape, dt, kind="Internal").ap()

    given = Edges(T_GIVEN, T_GIVEN // 4, I["src_e"], I["dst_e"], I["rel_e"], I["wgt_e"], I["dst_t"],
                  I["attr_t"])
    records = dram("records", [(T_SORTED + HALF) * TILE, 4 + FE])
    attr_sorted = dram("attr_sorted", [FE, T_SORTED * TILE])
    ordered = Edges(T_SORTED, T_SORTED // 6, None, None, None, None, None, attr_sorted)
    gin_tab = [dram(f"gin_tab{k}", [N, C]) for k in range(2)]
    edge_tab = dram("edge_tab", [N, HID])
    att_tab = dram("att_tab", [N, ROW2])
    va_tab = dram("va_tab", [N + WIN, 2 * HEADS])
    rel_tab = dram("rel_tab", [RELS * N, C])
    oh_stash = dram("oh_stash", [T_SORTED // HALF * TILE, HALF * WIN])
    stash = dram("stash", [T_SORTED // HALF * TILE, HALF, C])

    with ExitStack() as ctx:
        def sb(name, shape, dt=F32):
            return ctx.enter_context(nc.sbuf_tensor(name, shape, dt))
        TM = T_SORTED
        onehot = sb("onehot", [TILE, TM, WIN])
        src_i = sb("src_i", [TILE, TM + BODY], I32)
        dst_i = sb("dst_i", [TILE, TM], I32)
        rel_i = sb("rel_i", [TILE, TM + BODY], I32)
        wgt = sb("wgt", [TILE, TM])
        dst_loc = sb("dst_loc", [TILE, TM])
        late_row = sb("late_row", [1, TM + 2 * BODY], I32)
        off_row = sb("off_row", [1, TM], I32)
        base_f = sb("base_f", [128, 6])
        base_i = sb("base_i", [128, 6], I32)
        off_f = sb("off_f", [128, 6])
        bank_from = sb("bank_from", [128, 8])
        past = sb("past", [128, 6 * 8])
        span = sb("span", [128, 8])
        flag_f = sb("flag_f", [1, 2])
        flag = sb("flag", [1, 1], I32)
        ident = sb("ident", [128, 128])
        iota_f = sb("iota_f", [128, 128])
        pidx_i = sb("pidx_i", [128, 4], I32)
        pidx_f = sb("pidx_f", [128, 4])
        jmask = sb("jmask", [128, WIN])
        kmask = sb("kmask", [128, HEADS])
        m4 = sb("m4", [128, 4])
        ones = sb("ones", [128, 128])
        zeros = sb("zeros", [128, BANK], BF16)
        prm = sb("prm", [128, P_COLS])
        fold = sb("fold", [C, 6, 3])
        wgin = sb("wgin", [C, 6, C])
        w1a, w1b = sb("w1a", [C, HID]), sb("w1b", [FE + 1, HID])
        w2, w4 = sb("w2", [HID, C]), sb("w4", [HID, C])
        w3_rows, w23 = sb("w3_rows", [C + 2, HID]), sb("w23", [HID, HID])
        wl, wd = sb("wl", [C, C]), sb("wd", [C, C])
        wrel = sb("wrel", [C, RELS, C])
        brow = sb("brow", [1, 2 * C])
        b23 = sb("b23", [1, HID])
        hproj = sb("hproj", [C, C + 2 * HEADS])
        watt, batt = sb("watt", [C + 2, ROW2]), sb("batt", [1, ROW2])
        wvq = sb("wvq", [C + 2, WIN + HEADS])
        fpq = sb("fpq", [C, 2])
        xt_rows = sb("xt_rows", [C + 2, N])
        xn = sb("xn", [NP_, NT, C])
        yn = sb("yn", [NP_, NT, C])
        agg = sb("agg", [128, N])
        y1 = sb("y1", [128, N + WIN])
        row_t = sb("row_t", [1, NB - 1, WIN])
        tabn = sb("tabn", [NP_, 2, CH * RELS * C])
        stat = sb("stat", [NP_, 4, NT])
        bnst = sb("bnst", [C, 8])
        rows = sb("rows", [TILE, 2, HALF, HID])
        stage = sb("stage", [TILE, 2, HALF], I32)
        attr_buf = sb("attr_buf", [128, 2 * HALF * TILE])
        work = sb("work", [TILE, 2, HALF, HID])
        trio = sb("trio", [TILE, 3, 2, HALF, WIN])
        zbuf = sb("zbuf", [TILE, 2, 3, HALF])
        late = sb("late", [128, 3 * HEADS * TM])
        sg = sb("sg", [TILE, TM])
        signed_w = sb("signed_w", [TILE, 2, HALF, HEADS])
        mxg = sb("mxg", [128, 2, HALF])
        mxe = sb("mxe", [128, 2, HALF, WIN])
        ps = ctx.enter_context(nc.psum_tensor("ps", [128, 8 * BANK], F32))
        attr = attr_buf[0:FE + 1, :].rearrange("p (h n) -> p h n", h=2)
        winv = attr_buf[:, 0:6 * WIN * 2 * HEADS].rearrange("p (c n) -> p c n", c=6)
        iota_i = attr_buf[:, 0:128].bitcast(I32)
        ohs, msk = trio[:, 0], trio[:, 1]
        ohT = trio[:, 2].rearrange("p h a b -> p h (a b)")
        dst_tm = trio[:, :, :, :, :].bitcast(I32).rearrange("p a h k w -> p (a h k w)")[:, 0:6 * TILE]\
            .rearrange("p (c n) -> p c n", n=TILE)
        row2 = late[0:1, 0:2 * N].rearrange("p (a n) -> p a n", a=2)
        su = late[:, 0:HEADS * TM].rearrange("p (t k) -> p t k", k=HEADS)
        wtv = late[:, HEADS * TM:].rearrange("p (t k) -> p t k", k=2 * HEADS)
        q_row = late[0:1, HEADS * TM:HEADS * TM + N + WIN]
        w2_t, b2_col = late[0:C, 2 * C:2 * C + HID], late[0:C, 256:257]
        xt, w3a = xt_rows[0:C, :], w3_rows[0:C, :]
        w3b, b4b = w23[0:C, :], w2[0:NP_, :]
        rcp_all = late[:, N:2 * N]
        attw_t = late[0:C, 0:2 * C].rearrange("p (a n) -> p a n", a=2)
        sq = agg[0:NP_, 0:NT * C].rearrange("p (i f) -> p i f", f=C)
        packed = rows[:, :, :, :].rearrange("p h a b -> p (h a b)")\
            .rearrange("p (s k f) -> p s k f", s=4, f=C)
        ohT4 = attr_buf[:, :].rearrange("p (s h n) -> p s h n", s=4, h=2)
        smax = y1[0:HEADS, :]
        vt = agg[0:HEADS, :]
        diag = work

        pe_regs = dve_regs = None

        def bank(b, n=BANK, off=0):
            return ps[:, b * BANK + off:b * BANK + off + n]

        sems = {}

        def sem(name):
            if name not in sems:
                sems[name] = ctx.enter_context(nc.semaphore(name))
            return sems[name]

        PARTS = ((0, 16), (16, NT))
        V, A, M = nc.vector, nc.scalar.activation, nc.tensor.matmul

        def chunk(c):
            return len(tiles(c))

        def table_parts(k, c):
            return k * ((NCH + 1 - c % 2) // 2) + (RELS if k == 3 else 1) * (c // 2)

        def norm_row(k, l, n):
            return tabn[:, 0:1, (3 * k + l) * C:(3 * k + l + 1) * C].to_broadcast([NP_, n, C])

        def half_tiles(i, h):
            return bass.ds(i * BODY + h * HALF, HALF)

        def sp_start(sp):
            sp.dma_start(dst_tm[0:given.ch, 0:given.nc, :], I["dst_t"]).then_inc(sem("dst_in"), 16)
            sp_edges(sp, given)
            loads = [(prm[:, :], I["params"]), (xt[:, :], I["x_t"]),
                     (xn[:, :, :], I["x"].rearrange("(i p) c -> p i c", p=NP_)),
                     (wgin[:, 0:3, :], I["L0_gnn_W1"].rearrange("l a b -> a l b")),
                     (wgin[:, 3:6, :], I["L0_gnn_W2"].rearrange("l a b -> a l b")),
                     (w1a[:, :], I["L1_gnn_W1"][0:C, :]), (w1b[0:FE, :], I["L1_gnn_W1"][C:C + FE, :]),
                     (w1b[FE:FE + 1, :], I["b1_row"]),
                     (w2[:, :], I["L1_gnn_W2"]), (w3a[:, :], I["L1_gnn_W3"][0:C, :]),
                     (w3b[:, :], I["L1_gnn_W3"][C:2 * C, :]), (w4[:, :], I["L1_gnn_W4"]),
                     (wl[:, :], I["L2_gnn_Wl"]), (wd[:, :], I["L2_gnn_Wd"]),
                     (wrel[:, :, :], I["L3_gnn_weight"].rearrange("r a b -> a r b")),
                     (brow[:, :], I["brow"])]
            assert len(loads) == N_LOADS
            for to, of in loads:
                sp.dma_start(to, of).then_inc(sem("params"), 16)

        def pool_start(pool):
            g = nc.gpsimd
            chain = Chain(pool, sem("pool"))
            g.iota(iota_i[:, :], pattern=[[1, 128]], base=0, channel_multiplier=0).then_inc(sem("consts"), 1)
            g.iota(pidx_i[:, 0:1], pattern=[[0, 1]], base=0, channel_multiplier=1).then_inc(sem("consts"), 1)
            g.memset(ones[:, :], 1.0).then_inc(sem("consts"), 1)
            g.memset(zeros[:, :], 0.0).then_inc(sem("consts"), 1)
            g.memset(src_i[:, T_GIVEN:TM + BODY], 0).then_inc(sem("consts"), 1)
            g.memset(rel_i[:, T_GIVEN:TM + BODY], 0).then_inc(sem("consts"), 1)
            g.memset(rows[:, :, :, C:C + 1], 1.0).then_inc(sem("consts"), 1)
            chain(g.memset(ident[:, :], 0.0))
            g.affine_select(out=ident[:, :], in_=ident[:, :], compare_op=ALU.not_equal, fill=1.0,
                            base=0, pattern=[[-1, 128]], channel_multiplier=1).then_inc(sem("consts"), 1)

        def dve_min_max(dve, chain, E):
            d = dst_tm[0:E.ch, 0:E.nc, :]
            near = work[0:E.ch, 0, 0:E.nc, :]
            V.scalar_tensor_tensor(out=near, in0=d, scalar=float(FAR), in1=d, op0=ALU.is_lt,
                                   op1=ALU.mult).then_inc(sem("dve"), 1)
            chain.n += 1
            chain(V.tensor_reduce(base_f[0:E.ch, 0:E.nc], d, AX, ALU.min))
            chain(V.tensor_reduce(span[0:E.ch, 0:E.nc], near, AX, ALU.max))
            chain(V.tensor_tensor(span[0:E.ch, 0:E.nc], span[0:E.ch, 0:E.nc], base_f[0:E.ch, 0:E.nc],
                                  ALU.subtract))
            chain(V.tensor_scalar(base_f[0:E.ch, 0:E.nc], base_f[0:E.ch, 0:E.nc], float(N - 1), None,
                                  ALU.min))
            V.tensor_reduce(span[0:E.ch, 7:8], span[0:E.ch, 0:E.nc], AX, ALU.max)\
                .then_inc(sem("span_ready"), 1)

        def dve_start(dve, chain):
            dve.wait_ge(sem("dst_in"), 16)
            dve_min_max(dve, chain, given)
            dve.wait_ge(sem("span_row"), 1)
            chain(V.tensor_reduce(flag_f[:, 0:1], bank(0, given.ch)[0:1, :], AX, ALU.max))
            V.tensor_scalar(flag[:, :], flag_f[:, 0:1], float(WIN - 1), None, ALU.is_le)\
                .then_inc(sem("flag"), 1)
            dve.wait_ge(sem("consts"), 8)
            V.tensor_copy(iota_f[:, :], iota_i[:, :]).then_inc(sem("dve"), 1)
            V.tensor_scalar(pidx_i[:, 1:2], pidx_i[:, 0:1], 31, None, ALU.bitwise_and).then_inc(sem("dve"), 1)
            V.tensor_scalar(pidx_i[:, 2:3], pidx_i[:, 0:1], 5, None, ALU.logical_shift_right)\
                .then_inc(sem("dve"), 1)
            chain.n += 3
            chain(V.tensor_scalar(pidx_i[:, 3:4], pidx_i[:, 0:1], 3, None, ALU.bitwise_and))
            chain(V.tensor_copy(pidx_f[:, :], pidx_i[:, :]))
            for mask, n, c in ((jmask, WIN, 1), (kmask, HEADS, 2), (m4, 4, 3)):
                V.tensor_scalar(mask[:, :], iota_f[:, 0:n], pidx_f[:, c:c + 1], None, ALU.is_equal)
            dve.wait_ge(sem("params"), 16 * N_LOADS)

            def p(k):
                return prm[0:C, k:k + 3]
            for o, (g, b, be) in ((0, (P_G1, P_B1, P_BE1)), (2, (P_G2, P_B2, P_BE2))):
                chain(V.tensor_scalar(fold[:, o, :], p(g), BN_C, None, ALU.mult))
                chain(V.tensor_tensor(fold[:, o + 1, :], fold[:, o, :], p(b), ALU.mult))
                chain(V.tensor_tensor(fold[:, o + 1, :], fold[:, o + 1, :], p(be), ALU.add))
            chain(V.tensor_scalar(fold[:, 4, :], p(P_BNG), BN_C, None, ALU.mult))
            chain(V.tensor_scalar(fold[:, 5, :], p(P_EPS), 1.0, None, ALU.add))
            chain(V.tensor_tensor(fpq[:, 0:1], prm[0:C, P_WF:P_WF + 1], prm[0:C, P_WF + 2:P_WF + 3], ALU.add))
            chain(V.tensor_tensor(fpq[:, 1:2], prm[0:C, P_WF + 1:P_WF + 2], prm[0:C, P_WF + 2:P_WF + 3],
                                  ALU.subtract))
            for k, of in ((0, fold[:, 2:5, :].rearrange("p a b -> p (a b)")), (9, prm[0:C, P_BNB:P_BNB + 3])):
                n = of.shape[1]
                chain(V.tensor_tensor(tabn[0:C, 1, k * C:(k + n) * C].rearrange("p (a b) -> p a b", b=C),
                                      ident[0:C, 0:C].unsqueeze(1).to_broadcast([C, n, C]),
                                      of.unsqueeze(2).to_broadcast([C, n, C]), ALU.mult))
            chain(V.memset(w3_rows[C:C + 2, :], 0.0))
            chain(V.memset(watt[C:C + 2, :], 0.0))
            chain(V.memset(wvq[:, :], 0.0))
            V.tensor_copy(hproj[:, C:C + 2 * HEADS], prm[0:C, P_A1:P_A1 + 2 * HEADS]).then_inc(sem("folded"), 1)

        def pe_start(pe):
            pe.wait_ge(sem("consts"), 8)
            pe.wait_ge(sem("span_ready"), 1)
            nc.tensor.transpose(bank(0, given.ch)[0:1, :], span[0:given.ch, 7:8],
                                ident[0:given.ch, 0:given.ch]).then_inc(sem("span_row"), 1)

        def sp_edges(sp, E):
            for to, of in ((src_i[:, 0:E.t], E.src), (dst_i[:, 0:E.t], E.dst), (rel_i[:, 0:E.t], E.rel),
                           (wgt[:, 0:E.t], E.wgt)):
                sp.dma_start(to, of).then_inc(sem("edges_in"), 16)

        def dve_edges(dve, chain, E):
            ch = E.ch
            b = base_f[0:ch, 0:E.nc]
            chain(V.tensor_scalar(bank_from[0:ch, 0:NB - 1], iota_f[0:ch, 1:NB], float(STEP), None, ALU.mult))
            chain(V.tensor_copy(base_i[0:ch, 0:E.nc], b))
            chain(V.memset(late_row[:, :], 0))
            cmp = past[0:ch, 0:E.nc * (NB - 1)].rearrange("p (c m) -> p c m", m=NB - 1)
            chain(V.tensor_tensor(cmp, b.unsqueeze(2).to_broadcast([ch, E.nc, NB - 1]),
                                  bank_from[0:ch, 0:NB - 1].unsqueeze(1).to_broadcast([ch, E.nc, NB - 1]), ALU.is_ge))
            chain(V.tensor_reduce(off_f[0:ch, 0:E.nc], cmp, AX, ALU.add))
            chain(V.scalar_tensor_tensor(out=off_f[0:ch, 0:E.nc], in0=off_f[0:ch, 0:E.nc], scalar=float(WIN),
                                         in1=b, op0=ALU.mult, op1=ALU.add))
            for c in range(E.nc):
                V.tensor_scalar(diag[0:ch, 0, c, 0:ch], ident[0:ch, 0:ch], base_f[0:ch, c:c + 1], None,
                                ALU.mult)
                V.tensor_scalar(diag[0:ch, 1, c, 0:ch], ident[0:ch, 0:ch], off_f[0:ch, c:c + 1], None,
                                ALU.mult).then_inc(sem("diag_ready"), 1)
            dve.wait_ge(sem("edges_in"), 64)
            for c in range(E.nc):
                at = slice(c * ch, (c + 1) * ch)
                dve.wait_ge(sem("base_out"), c + 1)
                V.tensor_copy(late_row[:, HALF + c * ch:HALF + (c + 1) * ch], bank(c, ch)[0:1, :])
                V.tensor_copy(off_row[:, at], bank(c, ch, 256)[0:1, :])
                chain(V.tensor_tensor(dst_loc[:, at], dst_i[:, at], bank(c, ch), ALU.subtract))
            with dve.Fori(0, E.rounds) as i:
                at = bass.ds(i * BODY, BODY)
                V.tensor_tensor(onehot[:, at, :], dst_loc[:, at].unsqueeze(2).to_broadcast([TILE, BODY, WIN]),
                                iota_f[:, 0:WIN].unsqueeze(1).to_broadcast([TILE, BODY, WIN]), ALU.is_equal)\
                    .then_inc(sem("onehot_ready"), 1)
            V.scalar_tensor_tensor(out=rel_i[:, 0:E.t], in0=rel_i[:, 0:E.t], scalar=float(N),
                                   in1=src_i[:, 0:E.t], op0=ALU.mult, op1=ALU.add)
            dve.wait_ge(sem("weights_made"), 7)
            V.tensor_tensor(wgin[:, 3:6, :].rearrange("p a b -> p (a b)"),
                            wgin[:, 3:6, :].rearrange("p a b -> p (a b)"), tabn[0:C, 0, 0:3 * C], ALU.mult)\
                .then_inc(sem("w2_scaled"), 1)

        def pe_edges(pe, E):
            for c in range(E.nc):
                pe.wait_ge(sem("diag_ready"), c + 1)
                M(bank(c, E.ch), ones[0:E.ch, :], diag[0:E.ch, 0, c, 0:E.ch], start=True, stop=True)
                M(bank(c, E.ch, 256)[0:1, :], ones[0:E.ch, 0:1], diag[0:E.ch, 1, c, 0:E.ch],
                  start=True, stop=True, skip_group_check=True).then_inc(sem("base_out"), 1)

        def pool_gather(pool, E, s, table, width):
            with pool.Fori(0, E.rounds) as i:
                for h in range(2):
                    pool.wait_ge(sem(f"staged{h}"), E.staged(s, i))
                    pool.sem_inc(sem("gather_started"), 1)
                    for k in range(HALF):
                        nc.gpsimd.indirect_dma_start(
                            out=rows[:, h, k, 0:width], out_offset=None, in_=table,
                            in_offset=bass.IndirectOffsetOnAxis(ap=stage[:, h, k:k + 1], axis=0))\
                            .then_inc(sem(f"landed{h}"), 16)

        def stage_first(act, E, s, idx):
            for h in range(2):
                A(stage[:, h, :], idx[:, h * HALF:(h + 1) * HALF], ACT.Copy).then_inc(sem(f"staged{h}"), 1)

        def stage_next(s, idx, i, h):
            A(stage[:, h, :], idx[:, bass.ds(i * BODY + BODY + h * HALF, HALF)], ACT.Copy)\
                .then_inc(sem(f"staged{h}"), 1)

        def pe_clear(m):
            for b in range(NB):
                M(bank(b)[0:m, :], zeros[:, 0:m], zeros[:, :], start=True, stop=False, skip_group_check=True)

        def pe_windows(pe, i, h):
            pe.reg_load(pe_regs, off_row[:, half_tiles(i, h)])
            return [pe.snap(r, min_val=0, max_val=NB * BANK - WIN) for r in pe_regs]

        def pe_scatter(col, m, lhsT, rhs):
            return M(ps[0:m, bass.ds(col, WIN)], lhsT, rhs, start=False, stop=False, skip_group_check=True)

        def onehot_tile(i, h, k):
            return onehot[:, bass.ds(i * BODY + h * HALF + k, 1), :].rearrange("p a b -> p (a b)")

        def dve_sums(dve, chain, s, m):
            dve.wait_ge(sem("summed"), s + 1)
            for b in range(NB):
                n = min(STEP, N - b * STEP)
                ins = V.tensor_copy(agg[0:m, b * STEP:b * STEP + n], bank(b, n)[0:m, :])
                if b:
                    chain(ins)
                    at = agg[0:m, b * STEP:b * STEP + WIN]
                    ins = V.tensor_tensor(at, at, bank(b - 1, WIN, STEP)[0:m, :], ALU.add)
                ins.then_inc(sem("sums_ready"), 1)

        def dve_norm(dve, chain, q, after=None):
            for part, (a, b) in enumerate(PARTS):
                if after is not None:
                    dve.wait_ge(*after(part))
                n = b - a
                y, s = yn[:, a:b, :], sq[:, a:b, :]
                wide = [NP_, n, C]
                chain(V.tensor_reduce(stat[:, 0, a:b], y, AX, ALU.add))
                chain(V.tensor_scalar(stat[:, 0, a:b], stat[:, 0, a:b], -1.0 / C, None, ALU.mult))
                chain(V.tensor_tensor(y, y, stat[:, 0, a:b].unsqueeze(2).to_broadcast(wide), ALU.add))
                chain(V.tensor_tensor(s, y, y, ALU.mult))
                chain(V.tensor_reduce(stat[:, 1, a:b], s, AX, ALU.add))
                V.tensor_scalar(stat[:, 1, a:b], stat[:, 1, a:b], 1.0 / C, 1e-05, ALU.mult, ALU.add)\
                    .then_inc(sem("ln_var"), 1)
                dve.wait_ge(sem("ln_sd"), 2 * q + part + 1)
                chain(V.reciprocal(stat[:, 3, a:b], stat[:, 2, a:b]))
                V.tensor_tensor(xn[:, a:b, :], yn[:, a:b, :], stat[:, 3, a:b].unsqueeze(2).to_broadcast(wide),
                                ALU.mult).then_inc(sem("xn_ready"), 1)

        def act_norm(act, q):
            for part, (a, b) in enumerate(PARTS):
                act.wait_ge(sem("ln_var"), 2 * q + part + 1)
                A(stat[:, 2, a:b], stat[:, 1, a:b], ACT.Sqrt).then_inc(sem("ln_sd"), 1)

        def pe_back(pe, q, c):
            pe.wait_ge(sem("xn_ready"), 2 * q + (1 if tiles(c)[-1] < PARTS[0][1] else 2))
            if c >= 2:
                pe.wait_ge(sem("back_ev"), q * NCH + c - 1)
            for j, t in enumerate(tiles(c)):
                ins = nc.tensor.transpose(bank(c % 2, NP_, j * NP_)[0:C, :], xn[:, t, :], ident[0:NP_, 0:NP_])
            ins.then_inc(sem("back"), 1)

        def act_back(act, q, c):
            act.wait_ge(sem("back"), q * NCH + c + 1)
            A(xt[:, cols(c)], bank(c % 2, chunk(c) * NP_)[0:C, :], ACT.Copy).then_inc(sem("back_ev"), 1)

        def pool_gin(pool, E):
            pool.wait_ge(sem("consts"), 8)
            for l in range(3):
                if l:
                    pool.wait_ge(sem("gin_out"), 16 * NCH * l)
                pool_gather(pool, E, l, I["x"] if l == 0 else gin_tab[l - 1], C)

        def pe_gin(pe, E):
            pe_made_weights(pe)
            pe.wait_ge(sem("weights_made"), 7)
            pe.wait_ge(sem("onehot_ready"), 1)
            for l in range(3):
                m = C + (l == 0)
                if l:
                    pe.wait_ge(sem("h_read"), NCH * l)
                    pe.wait_ge(sem("a2"), NCH * l)
                pe_clear(m)
                if l == 1:
                    pe.sem_inc(sem("oh_tr_ev"), 1)
                with pe.Fori(0, E.rounds) as i:
                    for h in range(2):
                        at = pe_windows(pe, i, h)
                        if l == 0:
                            pe.wait_ge(sem("onehot_ready"), i + 1)
                        pe.wait_ge(sem(f"landed{h}"), E.landed(l, i))
                        for k in range(HALF):
                            ins = pe_scatter(at[k], m, rows[:, h, k, 0:m], onehot_tile(i, h, k))
                        ins.then_inc(sem(f"taken{l}{h}"), 1)
                        if l == 1:
                            pe.wait_ge(sem("oh_copy"), i * 2 + (h + 1))
                            pe.wait_ge(sem("oh_tr_ev"), i * 2 + (h + 1))
                            for q in range(2):
                                ins = nc.tensor.transpose(
                                    bank(7, TILE, q * TILE),
                                    ohs[:, h, 4 * q:4 * q + 4, :].rearrange("p a b -> p (a b)"), ident[:, :])
                            ins.then_inc(sem("oh_tr"), 1)
                if l == 1:
                    pe.wait_ge(sem("oh_tr_ev"), 2 * E.rounds + 1)
                M(bank(7, 8)[0:1, :], zeros[:, 0:1], zeros[:, 0:8], start=True, stop=True)\
                    .then_inc(sem("summed"), 1)
                if l == 0:
                    pe.wait_ge(sem("count_out"), 1)
                    pe.wait_ge(sem("w2_scaled"), 1)
                for step in range(NCH + 1):
                    if step < NCH:
                        c = step
                        n = chunk(c) * NP_
                        pe.wait_ge(sem("sums_ready"), l * NB + min(c + 2, NB))
                        if c >= 2:
                            pe.wait_ge(sem("a1"), l * NCH + c - 1)
                        M(bank((7, 0)[c % 2], n)[0:C, :], wgin[:, l, :], agg[0:C, cols(c)],
                          start=True, stop=True).then_inc(sem("mm1"), 1)
                    if step >= 1:
                        c = step - 1
                        pe.wait_ge(sem("a1"), l * NCH + c + 1)
                        pe.wait_ge(sem("sums_ready"), l * NB + min(c + 4, NB))
                        if c >= 2:
                            pe.wait_ge(sem("h_read"), l * NCH + c - 1)
                        for j, t in enumerate(tiles(c)):
                            ins = M(bank(1 + c % 2, C, j * C)[0:NP_, :], y1[0:C, t * NP_:(t + 1) * NP_],
                                    wgin[:, 3 + l, :], start=True, stop=True, skip_group_check=True)
                        ins.then_inc(sem("mm2"), 1)
                if l < 2:
                    pe.wait_ge(sem("sums_ready"), (l + 1) * NB)
                    for c in range(NCH):
                        if c >= 2:
                            pe.wait_ge(sem("a2"), l * NCH + c - 1)
                        M(bank(5 + c % 2, chunk(c) * NP_)[0:C, :], wgin[:, 3 + l, :], y1[0:C, cols(c)],
                          start=True, stop=True).then_inc(sem("mm3"), 1)

        def act_gin(act, E):
            act.wait_ge(sem("consts"), 8)
            act.wait_ge(sem("edges_in"), 64)
            stage_first(act, E, 0, src_i)
            act_made_weights(act)
            for l in range(3):
                with act.Fori(0, E.rounds) as i:
                    for h in range(2):
                        if l == 1:
                            A(ohs[:, h], onehot[:, half_tiles(i, h), :], ACT.Copy).then_inc(sem("oh_copy"), 1)
                        act.wait_ge(sem(f"taken{l}{h}"), i + 1)
                        stage_next(l, src_i, i, h)
                        if l == 1:
                            act.wait_ge(sem("oh_tr"), i * 2 + (h + 1))
                            act.wait_ge(sem(f"oh_stashed{h}"), i * 16 + 16)
                            A(ohT[:, h, :], bank(7, HALF * WIN), ACT.Copy).then_inc(sem("oh_tr_ev"), 1)
                if l == 0:
                    act.wait_ge(sem("folded"), 1)
                    act.wait_ge(sem("summed"), 1)
                    banks = ps[C:C + 1, 0:(NB - 1) * BANK].rearrange("p (b n) -> p b n", n=BANK)
                    A(row2[:, 0, 0:(NB - 1) * STEP].rearrange("p (b n) -> p b n", n=STEP),
                      banks[:, :, 0:STEP], ACT.Copy)
                    A(row2[:, 0, (NB - 1) * STEP:N], bank(NB - 1, N - (NB - 1) * STEP)[C:C + 1, :], ACT.Copy)
                    A(row_t[:, :, :], banks[:, :, STEP:BANK], ACT.Copy).then_inc(sem("count_out"), 1)
                for step in range(NCH + 2):
                    if step < NCH:
                        c = step
                        act.wait_ge(sem("mm1"), l * NCH + c + 1)
                        A(y1[0:C, cols(c)], bank((7, 0)[c % 2], chunk(c) * NP_)[0:C, :], ACT.Relu,
                          bias=fold[:, 1, l:l + 1], scale=fold[:, 0, l:l + 1]).then_inc(sem("a1"), 1)
                    if step >= 2 and l < 2:
                        c = step - 2
                        act.wait_ge(sem("h_linear"), l * NCH + c + 1)
                        y = yn[:, c * CH:c * CH + chunk(c), :].rearrange("p a b -> p (a b)")
                        A(y, y, ACT.Relu).then_inc(sem("ev"), 1)
                if l < 2:
                    stage_first(act, E, l + 1, src_i)
                    for c in range(NCH):
                        act.wait_ge(sem("mm3"), l * NCH + c + 1)
                        A(y1[0:C, cols(c)], bank(5 + c % 2, chunk(c) * NP_)[0:C, :], ACT.Relu,
                          bias=fold[:, 3, l:l + 1]).then_inc(sem("a2"), 1)

        def dve_gin(dve, chain, E):
            for l in range(3):
                dve.wait_ge(sem("summed"), l + 1)
                if l:
                    dve.wait_ge(sem("x_new"), l * NCH)
                for b in range(NB):
                    n = min(STEP, N - b * STEP)
                    at = slice(b * STEP, b * STEP + n)
                    ins = V.scalar_tensor_tensor(out=agg[0:C, at], in0=xt[:, at], scalar=fold[:, 5, l:l + 1],
                                                 in1=bank(b, n)[0:C, :], op0=ALU.mult, op1=ALU.add)
                    if b:
                        chain(ins)
                        at = agg[0:C, b * STEP:b * STEP + WIN]
                        ins = V.tensor_tensor(at, at, bank(b - 1, WIN, STEP)[0:C, :], ALU.add)
                    ins.then_inc(sem("sums_ready"), 1)
                for c in range(NCH):
                    dve.wait_ge(sem("mm2"), l * NCH + c + 1)
                    n = chunk(c)
                    at = slice(c * CH, c * CH + n)
                    y = yn[:, at, :]
                    V.tensor_tensor(y, bank(1 + c % 2, n * C)[0:NP_, :].rearrange("p (a b) -> p a b", b=C),
                                    norm_row(1, l, n), ALU.add).then_inc(sem("h_read"), 1)
                    dve.wait_ge(sem("h_read"), l * NCH + c + 1)
                    chain(V.scalar_tensor_tensor(out=y, in0=y, scalar=0.0, in1=norm_row(2, l, n),
                                                 op0=ALU.max, op1=ALU.mult))
                    ins = V.tensor_tensor(y, y, norm_row(3, l, n), ALU.add)
                    if l < 2:
                        ins.then_inc(sem("h_linear"), 1)
                    else:
                        chain(ins)
                        V.tensor_tensor(y, y, xn[:, at, :], ALU.add).then_inc(sem("ev"), 1)
                for c in range(NCH if l < 2 else 0):
                    dve.wait_ge(sem("a2"), l * NCH + c + 1)
                    chain(V.tensor_scalar(xt[:, cols(c)], y1[0:C, cols(c)], fold[:, 4, l:l + 1],
                                          prm[0:C, P_BNB + l:P_BNB + l + 1], ALU.mult, ALU.add))
                    V.tensor_scalar(xt[:, cols(c)], xt[:, cols(c)], 0.0, None, ALU.max).then_inc(sem("x_new"), 1)
                if l == 0:
                    dve.wait_ge(sem("count_out"), 1)
                    for b in range(1, NB):
                        at = row2[:, 0, b * STEP:b * STEP + WIN]
                        ins = V.tensor_tensor(at, at, row_t[:, b - 1, :], ALU.add)
                    chain(ins)
                    chain(V.tensor_scalar(row2[:, 1, :], row2[:, 0, :], 1.0, None, ALU.max))
                    chain(V.reciprocal(row2[:, 1, :], row2[:, 1, :]))
                    V.tensor_tensor(row2[:, 0, :], row2[:, 0, :], row2[:, 1, :], ALU.mult)\
                        .then_inc(sem("count_ready"), 1)
            dve.wait_ge(sem("ev"), 3 * NCH)
            dve_norm(dve, chain, 0)

        def sp_gin(sp, E):
            sp.wait_ge(sem("weights_made"), 7)
            for to, of in ((w3_rows[C:C + 1, :], b23[:, :]), (watt[C + 1:C + 2, :], batt[:, :]),
                           (xt_rows[C + 1:C + 2, :], ones[0:NT, 0:NP_])):
                sp.dma_start(to, of).then_inc(sem("rows_in"), 16)
            for l in range(2):
                if l == 1:
                    for h in range(2):
                        sp.sem_inc(sem(f"oh_stashed{h}"), 16)
                    with sp.Fori(0, E.rounds) as i:
                        for h in range(2):
                            sp.wait_ge(sem("oh_tr_ev"), i * 2 + (h + 2))
                            sp.dma_start(oh_stash[bass.ds(i * (2 * TILE) + h * TILE, TILE), :], ohT[:, h, :])\
                                .then_inc(sem(f"oh_stashed{h}"), 16)
                for c in range(NCH):
                    sp.wait_ge(sem("ev"), l * NCH + c + 1)
                    sp.dma_start(gin_tab[l][cols(c), :].rearrange("(i p) f -> p i f", p=NP_),
                                 yn[:, c * CH:c * CH + chunk(c), :]).then_inc(sem("gin_out"), 16)
            sp.wait_ge(sem("count_ready"), 1)
            sp.dma_start(xt_rows[C:C + 1, :], row2[:, 0, :]).then_inc(sem("rows_in"), 16)


        def pe_edge(pe, E):
            for step in range(NCH + 1):
                if step < NCH:
                    pe_back(pe, 0, step)
                if step >= 1:
                    c = step - 1
                    pe.wait_ge(sem("back_ev"), c + 1)
                    if c >= 2:
                        pe.wait_ge(sem("e_ev"), c - 1)
                    for j, t in enumerate(tiles(c)):
                        ins = M(bank(2 + c % 2, HID, j * HID)[0:NP_, :], xt[:, t * NP_:(t + 1) * NP_], w1a[:, :],
                                start=True, stop=True, skip_group_check=True)
                    ins.then_inc(sem("e_mm"), 1)
            for c in range(NCH):
                if c >= 2:
                    pe.wait_ge(sem("mean_ev"), c - 1)
                M(bank(4 + c % 2, chunk(c) * NP_), ones[0:1, :], row2[:, 1, cols(c)], start=True, stop=True)\
                    .then_inc(sem("mean_mm"), 1)
            pe.wait_ge(sem("e_ev"), NCH)
            pe.wait_ge(sem("mean_ev"), NCH)
            pe_clear(HID)
            pe.sem_inc(sem("scattered30"), 1)
            pe.sem_inc(sem("scattered31"), 1)
            pe.sem_inc(sem("px_added"), 1)
            pe.wait_ge(sem("ones_row"), 1)
            with pe.Fori(0, E.rounds) as i:
                for h in range(2):
                    at = pe_windows(pe, i, h)
                    pe.wait_ge(sem(f"attr_in{h}"), i * 16 + 16)

                    def project(p):
                        pe.wait_ge(sem("px_added"), i * 4 + (2 * h + p + 1))
                        for k in range(4 * p, 4 * p + 4):
                            ins = M(bank(7, HID, (k % 4) * HID),
                                    attr[:, h, k * TILE:(k + 1) * TILE], w1b[:, :], start=True, stop=True,
                                    skip_group_check=True)
                        ins.then_inc(sem("px_full"), 1)

                    def scatter(p):
                        pe.wait_ge(sem("relued"), i * 4 + (2 * h + p + 1))
                        for k in range(4 * p, 4 * p + 4):
                            ins = pe_scatter(at[k], HID, work[:, h, k, :], onehot_tile(i, h, k))
                        return ins

                    project(0)
                    project(1)
                    scatter(0)
                    scatter(1).then_inc(sem(f"scattered3{h}"), 1)
            M(bank(7, 8)[0:1, :], zeros[:, 0:1], zeros[:, 0:8], start=True, stop=True)\
                .then_inc(sem("summed"), 1)
            pe.wait_ge(sem("rows_in"), 64)
            for step in range(NCH + 1):
                if step < NCH:
                    c = step
                    to = bank((7, 0)[c % 2], chunk(c) * NP_)
                    pe.wait_ge(sem("sums_ready"), 3 * NB + min(c + 2, NB))
                    if c >= 2:
                        pe.wait_ge(sem("m_relu"), c - 1)
                    M(to, w3_rows[:, :], xt_rows[:, cols(c)], start=True, stop=False)
                    M(to, w23[:, :], agg[:, cols(c)], start=False, stop=True).then_inc(sem("m_hid"), 1)
                if step >= 1:
                    c = step - 1
                    pe.wait_ge(sem("m_relu"), c + 1)
                    pe.wait_ge(sem("sums_ready"), 3 * NB + min(c + 4, NB))
                    if c >= 2:
                        pe.wait_ge(sem("m_ev"), c - 1)
                    for j, t in enumerate(tiles(c)):
                        ins = M(bank(1 + c % 2, C, j * C)[0:NP_, :], y1[:, t * NP_:(t + 1) * NP_], w4[:, :],
                                start=True, stop=True, skip_group_check=True)
                    ins.then_inc(sem("m_out"), 1)

        def dve_edge(dve, chain, E):
            V.memset(attr[FE:FE + 1, :, :], 1.0).then_inc(sem("ones_row"), 1)
            dve.wait_ge(sem("back_ev"), NCH)
            V.tensor_tensor(xn[:, :, :], xn[:, :, :], b4b[:, :].unsqueeze(1).to_broadcast([NP_, NT, C]), ALU.add)\
                .then_inc(sem("x_b4"), 1)
            for c in range(NCH):
                dve.wait_ge(sem("mean_mm"), c + 1)
                V.tensor_copy(rcp_all[:, cols(c)], bank(4 + c % 2, chunk(c) * NP_)).then_inc(sem("mean_ev"), 1)
            with dve.Fori(0, E.rounds) as i:
                for h in range(2):
                    dve.wait_ge(sem(f"landed{h}"), E.landed(3, i))
                    dve.wait_ge(sem(f"scattered3{h}"), i + 1)
                    for p in range(2):
                        dve.wait_ge(sem("px_full"), i * 4 + (2 * h + p + 1))
                        V.tensor_tensor(work[:, h, 4 * p:4 * p + 4, :], rows[:, h, 4 * p:4 * p + 4, :],
                                        bank(7).rearrange("p (a b) -> p a b", b=HID),
                                        ALU.add).then_inc(sem("px_added"), 1)
            dve.wait_ge(sem("summed"), 4)
            for b in range(NB):
                n = min(STEP, N - b * STEP)
                at = slice(b * STEP, b * STEP + n)
                ins = V.tensor_tensor(agg[:, at], bank(b, n), rcp_all[:, at], ALU.mult)
                if b:
                    over = slice(b * STEP, b * STEP + WIN)
                    chain(V.tensor_tensor(work[:, 0, b, 0:WIN], bank(b - 1, WIN, STEP), rcp_all[:, over], ALU.mult))
                    ins = V.tensor_tensor(agg[:, over], agg[:, over], work[:, 0, b, 0:WIN], ALU.add)
                ins.then_inc(sem("sums_ready"), 1)
            dve.wait_ge(sem("x_b4"), 1)
            for c in range(NCH):
                dve.wait_ge(sem("m_out"), c + 1)
                at = slice(c * CH, c * CH + chunk(c))
                V.tensor_tensor(yn[:, at, :], bank(1 + c % 2, chunk(c) * C)[0:NP_, :]
                                .rearrange("p (a b) -> p a b", b=C), xn[:, at, :], ALU.add).then_inc(sem("m_ev"), 1)
            dve_norm(dve, chain, 1, lambda part: (sem("m_ev"), (4, NCH)[part]))

        def act_edge(act, E):
            act.wait_ge(sem("rows_in"), 64)
            A(wvq[:, 0:1], watt[:, ROW2 - 1:ROW2], ACT.Copy)
            A(wvq[:, WIN:WIN + HEADS], watt[:, C + HEADS:C + 2 * HEADS], ACT.Copy).then_inc(sem("weights_made"), 1)
            act_norm(act, 0)
            for step in range(NCH + 1):
                if step < NCH:
                    act_back(act, 0, step)
                if step >= 1:
                    c = step - 1
                    act.wait_ge(sem("e_mm"), c + 1)
                    if c >= 2:
                        act.wait_ge(sem(f"table_out{c % 2}"), 16 * table_parts(0, c))
                    A(tabn[:, c % 2, 0:chunk(c) * HID], bank(2 + c % 2, chunk(c) * HID)[0:NP_, :], ACT.Copy)\
                        .then_inc(sem("e_ev"), 1)
            stage_first(act, E, 3, src_i)
            with act.Fori(0, E.rounds) as i:
                for h in range(2):
                    for p in range(2):
                        act.wait_ge(sem("px_added"), i * 4 + (2 * h + p + 2))
                        four = work[:, h, 4 * p:4 * p + 4, :]
                        A(four, four, ACT.Relu).then_inc(sem("relued"), 1)
                    stage_next(3, src_i, i, h)
            for c in range(NCH):
                act.wait_ge(sem("m_hid"), c + 1)
                A(y1[:, cols(c)], bank((7, 0)[c % 2], chunk(c) * NP_), ACT.Relu,
                  bias=prm[:, P_L1B3:P_L1B3 + 1]).then_inc(sem("m_relu"), 1)
            act_norm(act, 1)

        def sp_edge(sp, E):
            for c in range(NCH):
                sp.wait_ge(sem("e_ev"), c + 1)
                sp.dma_start(edge_tab[cols(c), :].rearrange("(i p) f -> p i f", p=NP_),
                             tabn[:, c % 2, 0:chunk(c) * HID].rearrange("p (a b) -> p a b", b=HID))\
                    .then_inc(sem(f"table_out{c % 2}"), 16)
            with sp.Fori(0, E.rounds) as i:
                for h in range(2):
                    sp.wait_ge(sem(f"scattered3{h}"), i + 1)
                    sp.dma_start(attr[0:FE, h, :],
                                 E.attr[:, bass.ds(i * (BODY * TILE) + h * HALF * TILE, HALF * TILE)])\
                        .then_inc(sem(f"attr_in{h}"), 16)

        def pool_edge(pool, E):
            pool.wait_ge(sem("table_out0"), 16 * table_parts(0, NCH + NCH % 2))
            pool.wait_ge(sem("table_out1"), 16 * table_parts(0, NCH + 1 - NCH % 2))
            pool_gather(pool, E, 3, edge_tab, HID)

        def pe_made_weights(pe):
            pe.wait_ge(sem("folded"), 1)
            nc.tensor.transpose(bank(7, C)[0:C, :], wl[:, :], ident[0:C, 0:C])
            nc.tensor.transpose(bank(7, C, C)[0:C, :], wd[:, :], ident[0:C, 0:C])
            nc.tensor.transpose(bank(7, HID, 2 * C)[0:C, :], w2[:, :], ident[:, :])
            M(bank(7, 1, 256)[0:C, :], brow[:, 0:C], ones[0:1, 0:1], start=True, stop=True,
              skip_group_check=True).then_inc(sem("weights_made"), 1)
            pe.wait_ge(sem("weights_made"), 2)
            for lhsT, rows_, at in ((attw_t[:, 0, :], C, 128), (prm[0:C, P_BL:P_BL + 1], 1, 256)):
                M(bank(7, 2 * HEADS, at + C)[0:rows_, :], lhsT, hproj[:, C:C + 2 * HEADS],
                  start=True, stop=True, skip_group_check=True)
            for lhsT, rows_, at in ((attw_t[:, 1, :], C, 128), (prm[0:C, P_BD:P_BD + 1], 1, 256)):
                M(bank(7, 2, at + C + 2 * HEADS)[0:rows_, :], lhsT, fpq[:, :],
                  start=True, stop=True, skip_group_check=True)
            M(bank(7, C, 256)[0:1, :], prm[0:C, P_BL:P_BL + 1], ident[0:C, 0:C],
              start=True, stop=True, skip_group_check=True)
            M(bank(6, HID), w2_t, w3b[:, :], start=True, stop=True, skip_group_check=True)
            M(bank(6, HID, HID)[0:1, :], b2_col, w3b[:, :], start=True, stop=True, skip_group_check=True)
            M(bank(6, C, 2 * HID)[0:NP_, :], ones[0:1, 0:NP_], brow[:, C:2 * C], start=True, stop=True,
              skip_group_check=True).then_inc(sem("weights_made"), 1)
            pe.wait_ge(sem("weights_made"), 5)
            M(bank(6)[0:NP_, :], ones[0:C, 0:NP_], tabn[0:C, 1, 0:BANK], start=True, stop=True)
            M(bank(7, 12 * C - BANK)[0:NP_, :], ones[0:C, 0:NP_], tabn[0:C, 1, BANK:12 * C],
              start=True, stop=True).then_inc(sem("weights_made"), 1)

        def act_made_weights(act):
            act.wait_ge(sem("weights_made"), 1)
            A(late[0:C, 0:257], bank(7, 257)[0:C, :], ACT.Copy)\
                .then_inc(sem("weights_made"), 1)
            A(watt[0:C, 0:C], wl[:, :], ACT.Copy)
            act.wait_ge(sem("weights_made"), 3)
            A(watt[0:C, C:ROW2], bank(7, ROW2 - C, 128 + C)[0:C, :], ACT.Copy)
            A(w23[:, :], bank(6, HID), ACT.Copy)
            A(b23[:, :], bank(6, HID, HID)[0:1, :], ACT.Copy)
            A(b4b[:, :], bank(6, C, 2 * HID)[0:NP_, :], ACT.Copy)
            A(batt[:, :], bank(7, ROW2, 256)[0:1, :], ACT.Copy).then_inc(sem("weights_made"), 1)
            act.wait_ge(sem("weights_made"), 4)
            A(batt[:, C + HEADS:C + 2 * HEADS], batt[:, C + HEADS:C + 2 * HEADS], ACT.Identity,
              bias=prm[0:1, P_BA:P_BA + 1])
            A(batt[:, ROW2 - 1:ROW2], batt[:, ROW2 - 1:ROW2], ACT.Identity, bias=prm[0:1, P_BF:P_BF + 1])\
                .then_inc(sem("weights_made"), 1)
            act.wait_ge(sem("weights_made"), 6)
            A(tabn[:, 0, 0:12 * C], ps[0:NP_, 6 * BANK:6 * BANK + 12 * C], ACT.Copy).then_inc(sem("weights_made"), 1)

        def pe_att_tables(pe, E):
            for step in range(NCH + 1):
                if step < NCH:
                    pe_back(pe, 1, step)
                if step >= 1:
                    c = step - 1
                    pe.wait_ge(sem("back_ev"), NCH + c + 1)
                    if c >= 2:
                        pe.wait_ge(sem("hup_ev"), c - 1)
                    for j, t in enumerate(tiles(c)):
                        ins = M(bank(2 + c % 2, ROW2, j * ROW2)[0:NP_, :], xt_rows[:, t * NP_:(t + 1) * NP_],
                                watt[:, :], start=True, stop=True, skip_group_check=True)
                    ins.then_inc(sem("hup"), 1)
            pe.wait_ge(sem("weights_made"), 8)
            for c in range(NCH):
                if c >= 2:
                    pe.wait_ge(sem("vq_ev"), 2 * (c - 1))
                M(bank(4 + c % 2, chunk(c) * NP_)[0:WIN + HEADS, :], wvq[:, :], xt_rows[:, cols(c)],
                  start=True, stop=True).then_inc(sem("vq"), 1)

        def act_att_tables(act, E):
            for step in range(NCH + 1):
                if step < NCH:
                    act_back(act, 1, step)
                if step >= 1:
                    c = step - 1
                    act.wait_ge(sem("hup"), c + 1)
                    if c >= 2:
                        act.wait_ge(sem(f"table_out{c % 2}"), 16 * table_parts(1, c))
                    A(tabn[:, c % 2, 0:chunk(c) * ROW2], bank(2 + c % 2, chunk(c) * ROW2)[0:NP_, :],
                      ACT.Copy).then_inc(sem("hup_ev"), 1)
            stage_first(act, E, 4, src_i)

        def dve_att_tables(dve, chain, E):
            for c in range(NCH):
                n = chunk(c) * NP_
                dve.wait_ge(sem("vq"), c + 1)
                V.tensor_copy(q_row[:, cols(c)], bank(4 + c % 2, n)[0:1, :]).then_inc(sem("vq_ev"), 1)
                V.tensor_copy(vt[:, cols(c)], bank(4 + c % 2, n)[WIN:WIN + HEADS, :]).then_inc(sem("vq_ev"), 1)
            chain(V.memset(smax[:, :], -BIG))

        def sp_att_tables(sp, E):
            for c in range(NCH):
                sp.wait_ge(sem("hup_ev"), c + 1)
                sp.dma_start(att_tab[cols(c), :].rearrange("(i p) f -> p i f", p=NP_),
                             tabn[:, c % 2, 0:chunk(c) * ROW2].rearrange("p (a b) -> p a b", b=ROW2))\
                    .then_inc(sem(f"table_out{c % 2}"), 16)
            sp.dma_start(va_tab[N:N + WIN, :], I["nought"][:, 0:2 * HEADS]).then_inc(sem("va_tail"), 16)

        def pool_att_tables(pool, E):
            pool.wait_ge(sem("table_out0"), 16 * table_parts(1, NCH + NCH % 2))
            pool.wait_ge(sem("table_out1"), 16 * table_parts(1, NCH + 1 - NCH % 2))

        def act_signs(act, chain, E):
            with chain.loop(E.rounds, 2) as i:
                for h in range(2):
                    act.wait_ge(sem(f"l_ready{h}"), i + 1)
                    A(msk[:, h], onehot[:, half_tiles(i, h), :], ACT.Copy, bias=-BIG, scale=BIG)\
                        .then_inc(sem("mask"), 1)
                for h in range(2):
                    act.wait_ge(sem("z_ready"), i * 2 + (h + 1))
                    chain(A(zbuf[:, h, 1, :], zbuf[:, h, 0, :], ACT.Tanh))
                    A(sg[:, half_tiles(i, h)], zbuf[:, h, 1, :], ACT.Sign).then_inc(sem("sg_ready"), 1)
                    act.wait_ge(sem(f"su_ready{h}"), i + 1)
                    act.wait_ge(sem(f"stashed{h}"), i * 16 + 16)
                    stage_next(4, src_i, i, h)

        def pe_signs(pe, E):
            pe.wait_ge(sem("vq_ev"), 2 * NCH)
            pe.wait_ge(sem("hup_ev"), NCH)
            for h in range(2):
                pe.sem_inc(sem(f"l_ready{h}"), 1)
            pe.sem_inc(sem("l_max"), 1)
            pe.sem_inc(sem("q_taken"), 2)

            def windows_of_q(at, h, before):
                pe.reg_load(pe_regs, late_row[:, at])
                base = [pe.snap(r, min_val=0, max_val=N) for r in pe_regs]
                pe.wait_ge(sem("q_taken"), before)
                for k in range(HALF):
                    ins = M(bank(h, WIN, k * WIN), ones[0:1, :], q_row[:, bass.ds(base[k], WIN)],
                            start=True, stop=True, skip_group_check=True)
                ins.then_inc(sem("q_edge"), 1)

            windows_of_q(slice(HALF, 2 * HALF), 0, 1)
            pe.wait_ge(sem("no_max"), 1)
            M(bank(7, HALF * WIN)[0:HEADS, :], kmask[:, :], mxe[:, 1].rearrange("p a b -> p (a b)"),
              start=True, stop=True).then_inc(sem("max_row"), 1)
            with pe.Fori(0, E.rounds) as i:
                for h in range(2):
                    windows_of_q(bass.ds(i * BODY + (h + 2) * HALF, HALF), 1 - h, i * 2 + (h + 2))
                    pe.wait_ge(sem("l_max"), i * 2 + (h + 1))
                    pe.wait_ge(sem("l_half"), i * 2 + (h + 1))
                    for k in range(HALF):
                        if k == HALF // 2:
                            pe.wait_ge(sem(f"l_ready{h}"), i + 2)
                        ins = nc.tensor.transpose(bank(4 + k // 4, TILE, (k % 4) * TILE), work[:, h, k, :],
                                                  ident[:, :])
                    ins.then_inc(sem("l_tr"), 1)
                    pe.wait_ge(sem("max_spread"), i * 2 + (h + 1))
                    M(bank(6 + h, HALF * WIN)[0:HEADS, :], kmask[:, :],
                      mxe[:, h].rearrange("p a b -> p (a b)"), start=True, stop=True)\
                        .then_inc(sem("max_row"), 1)

        def dve_signs(dve, chain, E):
            def update(at, h, after):
                dve.reg_load(dve_regs, late_row[:, at])
                base = [dve.snap(r, min_val=0, max_val=N) for r in dve_regs]
                dve.wait_ge(sem("max_row"), after)
                for k in range(HALF):
                    if k == HALF // 2:
                        yield
                    to = smax[:, bass.ds(base[k], WIN)]
                    chain(V.tensor_tensor(to, to, bank(6 + h, WIN, k * WIN)[0:HEADS, :], ALU.max))

            V.memset(mxe[:, 1], -BIG).then_inc(sem("no_max"), 1)
            with chain.loop(E.rounds, 2 * HALF + 2) as i:
                for h in range(2):
                    dve.wait_ge(sem("q_edge"), i * 2 + (h + 1))
                    V.tensor_tensor(ohs[:, h], onehot[:, half_tiles(i, h), :],
                                    bank(h, HALF * WIN).rearrange("p (t j) -> p t j", j=WIN), ALU.mult)\
                        .then_inc(sem("q_taken"), 1)
                    dve.wait_ge(sem("q_taken"), i * 2 + (h + 3))
                    chain(V.tensor_reduce(zbuf[:, h, 2, :], ohs[:, h], AX, ALU.add))
                    dve.wait_ge(sem(f"landed{h}"), E.landed(4, i))
                    V.tensor_tensor(zbuf[:, h, 0, :], zbuf[:, h, 2, :], rows[:, h, :, C + 2 * HEADS], ALU.add)\
                        .then_inc(sem("z_ready"), 1)
                    updates = update(half_tiles(i, h), 1 - h, i * 2 + (h + 1))
                    next(updates)
                    dve.wait_ge(sem("sg_ready"), i * 2 + (h + 1))
                    at = su[:, half_tiles(i, h), :]
                    V.tensor_tensor(at, rows[:, h, :, C:C + HEADS],
                                    sg[:, half_tiles(i, h)].unsqueeze(2).to_broadcast([TILE, HALF, HEADS]),
                                    ALU.mult).then_inc(sem(f"su_ready{h}"), 1)
                    dve.wait_ge(sem(f"su_ready{h}"), i + 1)
                    dve.wait_ge(sem("mask"), i * 2 + (h + 1))
                    wide = [TILE, HALF // 2, HEADS, WIN]
                    for p, done in enumerate(("l_half", f"l_ready{h}")):
                        four = slice(4 * p, 4 * p + 4)
                        four_su = su[:, bass.ds(i * BODY + (h * HALF + 4 * p), 4), :]
                        V.tensor_tensor(work[:, h, four].rearrange("p a (k j) -> p a k j", j=WIN),
                                        four_su.unsqueeze(3).to_broadcast(wide),
                                        msk[:, h, four].unsqueeze(2).to_broadcast(wide), ALU.add)\
                            .then_inc(sem(done), 1)
                    next(updates, None)
                    dve.wait_ge(sem("l_tr"), i * 2 + (h + 1))
                    V.tensor_reduce(mxg[:, h, :], ps[:, 4 * BANK:6 * BANK].rearrange("p (a b) -> p a b", b=TILE),
                                    AX, ALU.max).then_inc(sem("l_max"), 1)
                    dve.wait_ge(sem("l_max"), i * 2 + (h + 2))
                    wide = [128, HALF, WIN]
                    V.tensor_tensor(mxe[:, h], mxg[:, h, :].unsqueeze(2).to_broadcast(wide),
                                    jmask[:, :].unsqueeze(1).to_broadcast(wide), ALU.mult)\
                        .then_inc(sem("max_spread"), 1)
            for _ in update(slice(E.t, E.t + HALF), 1, 2 * E.rounds + 1):
                pass
            for c in range(NCH):
                at = smax[:, cols(c)]
                chain(V.tensor_tensor(at, at, vt[:, cols(c)], ALU.add))
                V.scalar_tensor_tensor(out=at, in0=at, scalar=NEG_SLOPE, in1=at, op0=ALU.mult, op1=ALU.max)\
                    .then_inc(sem("am_ready"), 1)

        def sp_signs(sp, E):
            with sp.Fori(0, E.rounds) as i:
                for h in range(2):
                    sp.wait_ge(sem(f"landed{h}"), E.landed(4, i))
                    sp.dma_start(stash[bass.ds(i * (2 * TILE) + h * TILE, TILE), :, :], rows[:, h, :, 0:C])\
                        .then_inc(sem(f"stashed{h}"), 16)

        def pe_va(pe, E):
            for c in range(NCH):
                pe.wait_ge(sem("am_ready"), c + 1)
                if c >= 2:
                    pe.wait_ge(sem("va_ev"), c - 1)
                for j, t in enumerate(tiles(c)):
                    for k, of in enumerate((vt, smax)):
                        ins = nc.tensor.transpose(bank(c % 2, HEADS, (2 * j + k) * HEADS)[0:NP_, :],
                                                  of[:, t * NP_:(t + 1) * NP_], ident[0:HEADS, 0:HEADS])
                ins.then_inc(sem("va_tr"), 1)
            for c in range(E.nc):
                pe.wait_ge(sem("wv_spread"), c + 1)
                if c >= 2:
                    pe.wait_ge(sem("wv_ev"), 2 * (c - 1))
                for f in range(2 * HEADS):
                    ins = nc.tensor.transpose(bank(2 + 2 * (c % 2) + f // 4, E.ch, (f % 4) * E.ch),
                                              work[0:E.ch, c % 2, f, :], ident[0:E.ch, 0:E.ch])
                    if f % 4 == 3:
                        ins.then_inc(sem("wv_tr"), 1)

        def act_va(act, E):
            act.wait_ge(sem("table_out0"), 16 * table_parts(1, NCH + NCH % 2))
            act.wait_ge(sem("table_out1"), 16 * table_parts(1, NCH + 1 - NCH % 2))
            for c in range(NCH):
                act.wait_ge(sem("va_tr"), c + 1)
                if c >= 2:
                    act.wait_ge(sem(f"table_out{c % 2}"), 16 * table_parts(2, c))
                A(tabn[:, c % 2, 0:chunk(c) * 2 * HEADS], bank(c % 2, chunk(c) * 2 * HEADS)[0:NP_, :], ACT.Copy)\
                    .then_inc(sem("va_ev"), 1)
            for c in range(E.nc):
                for g in range(2):
                    act.wait_ge(sem("wv_tr"), 2 * c + g + 1)
                    A(wtv[:, c * E.ch:(c + 1) * E.ch, 4 * g:4 * g + 4].rearrange("p t f -> p f t"),
                      bank(2 + 2 * (c % 2) + g, 4 * E.ch).rearrange("p (f t) -> p f t", f=4), ACT.Copy)\
                        .then_inc(sem("wv_ev"), 1)

        def dve_va(dve, chain, E):
            dve.wait_ge(sem("wv_in"), 16 * E.nc)
            for c in range(E.nc):
                if c >= 2:
                    dve.wait_ge(sem("wv_tr"), 2 * (c - 1))
                wide = [E.ch, 4, WIN]
                for f in range(2 * HEADS):
                    ins = V.tensor_tensor(
                        work[0:E.ch, c % 2, f, :].rearrange("p (a b) -> p a b", b=WIN),
                        winv[0:E.ch, c, :].rearrange("p (j f) -> p f j", f=2 * HEADS)[:, f:f + 1, :].to_broadcast(wide),
                        m4[0:E.ch, :].unsqueeze(2).to_broadcast(wide), ALU.mult)
                ins.then_inc(sem("wv_spread"), 1)

        def sp_va(sp, E):
            for c in range(NCH):
                sp.wait_ge(sem("va_ev"), c + 1)
                sp.dma_start(va_tab[cols(c), :].rearrange("(i p) f -> p i f", p=NP_),
                             tabn[:, c % 2, 0:chunk(c) * 2 * HEADS].rearrange("p (a b) -> p a b", b=2 * HEADS))\
                    .then_inc(sem(f"table_out{c % 2}"), 16)

        def pool_va(pool, E):
            pool.wait_ge(sem("table_out0"), 16 * table_parts(2, NCH + NCH % 2))
            pool.wait_ge(sem("table_out1"), 16 * table_parts(2, NCH + 1 - NCH % 2))
            pool.wait_ge(sem("va_tail"), 16)
            for c in range(E.nc):
                nc.gpsimd.indirect_dma_start(
                    out=winv[0:E.ch, c, :], out_offset=None, in_=va_tab,
                    in_offset=bass.IndirectOffsetOnAxis(ap=base_i[0:E.ch, c:c + 1], axis=0))\
                    .then_inc(sem("wv_in"), 16)

        def ring_loop(eng, count, body):
            with eng.Fori(0, count // 4) as j:
                body(j, range(4))
            if count % 4:
                body(count // 4, range(count % 4))

        def ring_tiles(j, s, k=0, n=HALF):
            return bass.ds(j * (4 * HALF) + (s * HALF + k), n)

        def ring_round(j, s, k=0, n=BODY):
            return bass.ds(j * (4 * BODY) + (s * BODY + k), n)

        def sp_soft(sp, E):
            for h in range(2):
                sp.wait_ge(sem(f"stashed{h}"), 16 * E.rounds)
                sp.wait_ge(sem(f"oh_stashed{h}"), 16 * E.rounds + 16)
            sp.wait_ge(sem("wv_spread"), E.nc)

            def fetch_onehots(j, places):
                for s in places:
                    sp.wait_ge(sem("oh_used"), j * 4 + (s + 1))
                    sp.dma_start(ohT4[:, s], oh_stash[bass.ds(j * (8 * TILE) + s * (2 * TILE), 2 * TILE), :]
                                 .rearrange("(h p) n -> p h n", p=TILE)).then_inc(sem(f"oh_in{s}"), 16)
            ring_loop(sp, E.rounds, fetch_onehots)

            def fetch(j, places):
                for s in places:
                    sp.wait_ge(sem(f"msg_ready{s}"), j + 1)
                    sp.dma_start(packed[:, s], stash[bass.ds(j * (4 * TILE) + s * TILE, TILE), :, :])\
                        .then_inc(sem(f"fetched{s}"), 16)
            ring_loop(sp, 2 * E.rounds, fetch)

        def pe_soft(pe, E):
            pe.wait_ge(sem("wv_ev"), 2 * E.nc)
            pe.wait_ge(sem("va_ev"), NCH)
            for s in range(4):
                pe.sem_inc(sem(f"msg_ready{s}"), 1)

            pe.sem_inc(sem("oh_used"), 4)
            pe.sem_inc(sem("va_taken"), 4)

            def destinations(j, places):
                for s in places:
                    pe.wait_ge(sem(f"oh_in{s}"), j * 16 + 16)
                    pe.wait_ge(sem("va_taken"), j * 4 + (s + 1))
                    for q in range(4):
                        ins = M(bank(4 + s, 32, 32 * q), ohT4[:, s, q // 2, (q % 2) * TILE:(q % 2 + 1) * TILE],
                                wtv[:, ring_round(j, s, 4 * q, 4), :].rearrange("p a b -> p (a b)"),
                                start=True, stop=True, skip_group_check=True)
                    ins.then_inc(sem("va_edge"), 1)
            ring_loop(pe, E.rounds, destinations)
            pe.wait_ge(sem("va_taken"), E.rounds + 4)
            pe_clear(C + HEADS)
            pe.sem_inc(sem("scattered_soft"), 2)

            def scatter(j, places):
                for s in places:
                    half = onehot[:, ring_tiles(j, s), :]
                    pe.reg_load(pe_regs, off_row[:, ring_tiles(j, s)])
                    at = [pe.snap(r, min_val=0, max_val=NB * BANK - WIN) for r in pe_regs]
                    pe.wait_ge(sem(f"msg_ready{s}"), j + 2)
                    pe.wait_ge(sem("w_copied"), j * 4 + (s + 1))
                    for k in range(HALF):
                        ins = pe_scatter(at[k], C + HEADS, work[:, s % 2, k, 0:C + HEADS], half[:, k, :])
                    ins.then_inc(sem("scattered_soft"), 1)
            ring_loop(pe, 2 * E.rounds, scatter)
            M(bank(7, 8)[0:1, :], zeros[:, 0:1], zeros[:, 0:8], start=True, stop=True)\
                .then_inc(sem("summed"), 1)
            pe.wait_ge(sem("sums_ready"), 5 * NB)
            for c in range(NCH):
                if c >= 2:
                    pe.wait_ge(sem("o_ev"), c - 1)
                for j, t in enumerate(tiles(c)):
                    ins = nc.tensor.transpose(bank(c % 2, C + HEADS, j * (C + HEADS))[0:NP_, :],
                                              agg[0:C + HEADS, t * NP_:(t + 1) * NP_],
                                              ident[0:C + HEADS, 0:C + HEADS])
                ins.then_inc(sem("o_tr"), 1)

        def act_soft(act, E):
            def exponentials(j, places):
                for s in places:
                    act.wait_ge(sem("d_ready"), j * 4 + (s + 1))
                    A(wtv[:, ring_round(j, s), 0:HEADS], su[:, ring_round(j, s), :], ACT.Exp)\
                        .then_inc(sem("w_ready"), 1)
            ring_loop(act, E.rounds, exponentials)
            act.wait_ge(sem("w_ready"), E.rounds)

            def copy_weights(j, places):
                for s in places:
                    act.wait_ge(sem("scattered_soft"), j * 4 + (s + 1))
                    A(work[:, s % 2, :, C:C + HEADS], wtv[:, ring_tiles(j, s), 0:HEADS], ACT.Copy)\
                        .then_inc(sem("w_copied"), 1)
            ring_loop(act, 2 * E.rounds, copy_weights)

        def dve_soft(dve, chain, E):
            def exponents(j, places):
                for pair in (places[0:2], places[2:4]):
                    tiles_of = {s: su[:, ring_round(j, s), :] for s in pair}
                    va = {s: bank(4 + s, BODY * 2 * HEADS).rearrange("p (t f) -> p t f", f=2 * HEADS) for s in pair}
                    for s in pair:
                        dve.wait_ge(sem("va_edge"), j * 4 + (s + 1))
                        dve.sem_inc(sem("oh_used"), 1)
                        V.tensor_tensor(tiles_of[s], tiles_of[s], va[s][:, :, 0:HEADS], ALU.add)\
                            .then_inc(sem("alpha_sum"), 1)
                    for s in pair:
                        dve.wait_ge(sem("alpha_sum"), j * 4 + (s + 1))
                        V.scalar_tensor_tensor(out=tiles_of[s], in0=tiles_of[s], scalar=NEG_SLOPE, in1=tiles_of[s],
                                               op0=ALU.mult, op1=ALU.max).then_inc(sem("alpha"), 1)
                    for s in pair:
                        dve.wait_ge(sem("alpha"), j * 4 + (s + 1))
                        V.tensor_tensor(tiles_of[s], tiles_of[s], va[s][:, :, HEADS:2 * HEADS], ALU.subtract)\
                            .then_inc(sem("va_taken"), 1)
                    for s in pair:
                        dve.wait_ge(sem("va_taken"), j * 4 + (s + 5))
                        V.tensor_scalar(tiles_of[s], tiles_of[s], 0.0, None, ALU.min).then_inc(sem("d_ready"), 1)
            ring_loop(dve, E.rounds, exponents)
            dve.wait_ge(sem("w_ready"), E.rounds)

            def weigh(j, places):
                for s in places:
                    dve.wait_ge(sem(f"fetched{s}"), j * 16 + 16)
                    dve.wait_ge(sem("scattered_soft"), j * 4 + (s + 1))
                    V.tensor_tensor(signed_w[:, s % 2], wtv[:, ring_tiles(j, s), 0:HEADS],
                                    sg[:, ring_tiles(j, s)].unsqueeze(2).to_broadcast([TILE, HALF, HEADS]),
                                    ALU.mult).then_inc(sem("signed"), 1)
                    dve.wait_ge(sem("signed"), j * 4 + (s + 1))
                    V.tensor_tensor(
                        work[:, s % 2, :, 0:C].rearrange("p a (k d) -> p a k d", d=HD),
                        packed[:, s].rearrange("p a (k d) -> p a k d", d=HD),
                        signed_w[:, s % 2].unsqueeze(3).to_broadcast([TILE, HALF, HEADS, HD]),
                        ALU.mult).then_inc(sem(f"msg_ready{s}"), 1)
            ring_loop(dve, 2 * E.rounds, weigh)
            dve_sums(dve, chain, 4, C + HEADS)
            for c in range(NCH):
                n = chunk(c)
                dve.wait_ge(sem("o_tr"), c + 1)
                got = bank(c % 2, n * (C + HEADS))[0:NP_, :].rearrange("p (a b) -> p a b", b=C + HEADS)
                den = tabn[:, 0, 0:n * HEADS].rearrange("p (a b) -> p a b", b=HEADS)
                y = yn[:, c * CH:c * CH + n, :]
                chain(V.tensor_scalar(den, got[:, :, C:C + HEADS], 1e-16, None, ALU.max))
                chain(V.reciprocal(den, den))
                V.tensor_tensor(y.rearrange("p a (k d) -> p a k d", d=HD),
                                got[:, :, 0:C].rearrange("p a (k d) -> p a k d", d=HD),
                                den.unsqueeze(3).to_broadcast([NP_, n, HEADS, HD]), ALU.mult)\
                    .then_inc(sem("o_ev"), 1)
                dve.wait_ge(sem("o_ev"), c + 1)
                chain(V.tensor_tensor(y, y, xn[:, c * CH:c * CH + n, :], ALU.add))
            dve_norm(dve, chain, 2)

        PAIRS = [(c, j) for c in range(NCH) for j in range(0, chunk(c), 2)]

        def pe_rel(pe, E):
            for step in range(NCH + 1):
                if step < NCH:
                    pe_back(pe, 2, step)
                if step >= 1:
                    c = step - 1
                    pe.wait_ge(sem("back_ev"), 2 * NCH + c + 1)
                    for n, (cc, j) in enumerate(PAIRS):
                        if cc != c:
                            continue
                        if n >= 4:
                            pe.wait_ge(sem("rel_ev"), n - 3)
                        for k in range(min(2, chunk(c) - j)):
                            t = c * CH + j + k
                            ins = M(bank(2 + n % 4, RELS * C, k * RELS * C)[0:NP_, :],
                                    xt[:, t * NP_:(t + 1) * NP_], wrel[:, :, :].rearrange("p r c -> p (r c)"),
                                    start=True, stop=True, skip_group_check=True)
                        ins.then_inc(sem("rel_mm"), 1)
            pe.wait_ge(sem("rel_ev"), len(PAIRS))
            pe_clear(C)
            for h in range(2):
                pe.sem_inc(sem(f"scattered5{h}"), 1)
            with pe.Fori(0, E.rounds) as i:
                for h in range(2):
                    at = pe_windows(pe, i, h)
                    pe.wait_ge(sem("weighted"), i * 2 + (h + 1))
                    pe.wait_ge(sem(f"landed{h}"), E.landed(5, i))
                    for k in range(HALF):
                        ins = pe_scatter(at[k], C, rows[:, h, k, 0:C], msk[:, h, k, :])
                    ins.then_inc(sem(f"scattered5{h}"), 1)
            M(bank(7, 8)[0:1, :], zeros[:, 0:1], zeros[:, 0:8], start=True, stop=True)\
                .then_inc(sem("summed"), 1)
            pe.wait_ge(sem("sums_ready"), 6 * NB)
            for c in range(NCH):
                pe.wait_ge(sem("y_ready"), c + 1)
                if c >= 2:
                    pe.wait_ge(sem("y_ev"), c - 1)
                for j, t in enumerate(tiles(c)):
                    ins = nc.tensor.transpose(bank(c % 2, C, j * C)[0:NP_, :], y1[0:C, t * NP_:(t + 1) * NP_],
                                              ident[0:C, 0:C])
                ins.then_inc(sem("y_tr"), 1)

        def act_rel(act, E):
            act_norm(act, 2)
            for step in range(NCH + 1):
                if step < NCH:
                    act_back(act, 2, step)
                if step >= 1:
                    c = step - 1
                    if c >= 2:
                        act.wait_ge(sem(f"table_out{c % 2}"), 16 * table_parts(3, c))
                    for n, (cc, j) in enumerate(PAIRS):
                        if cc == c:
                            m = min(2, chunk(c) - j) * RELS * C
                            act.wait_ge(sem("rel_mm"), n + 1)
                            A(tabn[:, c % 2, j * RELS * C:j * RELS * C + m], bank(2 + n % 4, m)[0:NP_, :],
                              ACT.Copy).then_inc(sem("rel_ev"), 1)
            stage_first(act, E, 5, rel_i)
            act.wait_ge(sem("bn_mean"), 1)
            A(y1[0:C, 0:N], xt[:, :], ACT.Square, bias=bnst[:, 1:2], accum_out=bnst[:, 2:3])\
                .then_inc(sem("bn_square"), 1)
            act.wait_ge(sem("bn_var"), 1)
            A(bnst[:, 4:5], bnst[:, 3:4], ACT.Sqrt).then_inc(sem("bn_sd"), 1)
            with act.Fori(0, E.rounds) as i:
                for h in range(2):
                    act.wait_ge(sem(f"scattered5{h}"), i + 2)
                    stage_next(5, rel_i, i, h)
            for step in range(NCH + 2):
                if step < NCH:
                    c = step
                    act.wait_ge(sem("hbn"), c + 1)
                    A(y1[0:C, cols(c)], y1[0:C, cols(c)], ACT.Relu, bias=bnst[:, 7:8])\
                        .then_inc(sem("relu_out"), 1)
                if step >= 2:
                    c = step - 2
                    act.wait_ge(sem("y_tr"), c + 1)
                    A(yn[:, c * CH:c * CH + chunk(c), :].rearrange("p a b -> p (a b)"),
                      bank(c % 2, chunk(c) * C)[0:NP_, :], ACT.Copy).then_inc(sem("y_ev"), 1)
            act_norm(act, 3)

        def dve_rel(dve, chain, E):
            dve.wait_ge(sem("back_ev"), 3 * NCH)
            chain(V.tensor_reduce(bnst[:, 0:1], xt[:, :], AX, ALU.add))
            V.tensor_scalar(bnst[:, 1:2], bnst[:, 0:1], -1.0 / N, None, ALU.mult).then_inc(sem("bn_mean"), 1)
            dve.wait_ge(sem("bn_square"), 1)
            V.tensor_scalar(bnst[:, 3:4], bnst[:, 2:3], 1.0 / N, 1e-05, ALU.mult, ALU.add)\
                .then_inc(sem("bn_var"), 1)
            dve.wait_ge(sem("bn_sd"), 1)
            chain(V.reciprocal(bnst[:, 5:6], bnst[:, 4:5]))
            chain(V.tensor_tensor(bnst[:, 6:7], bnst[:, 5:6], prm[0:C, P_GAMMA:P_GAMMA + 1], ALU.mult))
            V.scalar_tensor_tensor(out=bnst[:, 7:8], in0=bnst[:, 1:2], scalar=bnst[:, 6:7],
                                   in1=prm[0:C, P_BETA:P_BETA + 1], op0=ALU.mult, op1=ALU.add)\
                .then_inc(sem("bn_ready"), 1)
            with dve.Fori(0, E.rounds) as i:
                for h in range(2):
                    dve.wait_ge(sem(f"scattered5{h}"), i + 1)
                    V.tensor_tensor(msk[:, h], onehot[:, half_tiles(i, h), :],
                                    wgt[:, half_tiles(i, h)].unsqueeze(2).to_broadcast([TILE, HALF, WIN]),
                                    ALU.mult).then_inc(sem("weighted"), 1)
            dve_sums(dve, chain, 5, C)
            dve.wait_ge(sem("bn_ready"), 1)
            dve.wait_ge(sem("sums_ready"), 6 * NB)
            for step in range(NCH + 1):
                if step < NCH:
                    c = step
                    V.scalar_tensor_tensor(out=y1[0:C, cols(c)], in0=xt[:, cols(c)], scalar=bnst[:, 6:7],
                                           in1=agg[0:C, cols(c)], op0=ALU.mult, op1=ALU.add)\
                        .then_inc(sem("hbn"), 1)
                if step >= 1:
                    c = step - 1
                    dve.wait_ge(sem("relu_out"), c + 1)
                    V.tensor_tensor(y1[0:C, cols(c)], y1[0:C, cols(c)], xt[:, cols(c)], ALU.add)\
                        .then_inc(sem("y_ready"), 1)
            dve_norm(dve, chain, 3, lambda part: (sem("y_ev"), (4, NCH)[part]))

        def sp_rel(sp, E):
            for c in range(NCH):
                sp.wait_ge(sem("rel_ev"), sum(1 for cc, _ in PAIRS if cc <= c))
                for r in range(RELS):
                    sp.dma_start(
                        rel_tab[r * N + cols(c).start:r * N + cols(c).stop, :].rearrange("(i p) f -> p i f", p=NP_),
                        tabn[:, c % 2, 0:chunk(c) * RELS * C].rearrange("p (a b) -> p a b", b=RELS * C)
                        [:, :, r * C:(r + 1) * C]).then_inc(sem(f"table_out{c % 2}"), 16)

        def pool_rel(pool, E):
            pool.wait_ge(sem("table_out0"), 16 * table_parts(3, NCH + NCH % 2))
            pool.wait_ge(sem("table_out1"), 16 * table_parts(3, NCH + 1 - NCH % 2))
            pool_gather(pool, E, 5, rel_tab, C)

        def sp_out(sp):
            for part, (a, b) in enumerate(PARTS):
                sp.wait_ge(sem("xn_ready"), 7 + part)
                sp.dma_start(out[a * NP_:b * NP_, :].rearrange("(i p) f -> p i f", p=NP_), xn[:, a:b, :])\
                    .then_inc(sem("out_done"), 16)
            sp.wait_ge(sem("out_done"), 32)

        scratch = onehot[:, :, :].rearrange("p t j -> p (t j)")
        TG = T_GIVEN
        blk, member, rank, place = (scratch[:, k * TG:(k + 1) * TG] for k in range(4))
        blk_i = scratch[:, 4 * TG:5 * TG].bitcast(I32)
        place_i = scratch[:, 5 * TG:6 * TG].bitcast(I32)
        rest = scratch[:, 6 * TG:]
        RECORD = 4 + FE
        rec = rest[:, 0:HALF * RECORD].rearrange("p (k f) -> p k f", f=RECORD)
        rec_i = rest[:, 0:HALF * RECORD].bitcast(I32).rearrange("p (k f) -> p k f", f=RECORD)
        empty = rest[:, 320:320 + HALF * RECORD].rearrange("p (k f) -> p k f", f=RECORD)
        empty_i = rest[:, 320:320 + HALF * RECORD].bitcast(I32).rearrange("p (k f) -> p k f", f=RECORD)
        place_st = rest[:, 640:640 + HALF].bitcast(I32)
        lower = rest[:, 704:704 + 128]
        at_blk, first, held, before, full = (rest[:, 840 + k:841 + k] for k in range(5))
        full_i = rest[:, 848:849].bitcast(I32)
        spare = rest[:, 849:850]
        attr_s = rest[0:FE, 1024:1024 + HALF * TILE]
        dst_f = rest[:, 2048:2048 + T_SORTED]

        def dve_sort(dve, chain):
            dve.wait_ge(sem("edges_in"), 64)
            chain(V.memset(empty, 0.0))
            V.memset(empty_i[:, :, 1:2], FAR).then_inc(sem("empty_ready"), 1)
            chain(V.tensor_scalar(lower, iota_f[:, :], pidx_f[:, 0:1], None, ALU.is_gt))
            chain(V.tensor_scalar(blk_i, dst_i[:, 0:TG], WIN.bit_length() - 1, None, ALU.logical_shift_right))
            chain(V.tensor_copy(blk, blk_i))
            chain(V.memset(place, 0.0))
            chain(V.memset(rest[:, 840:850], 0.0))
            with chain.loop(BLOCKS, 13) as i:
                chain(V.tensor_scalar(member, blk, at_blk, None, ALU.is_equal))
                chain(V.tensor_tensor_scan(rank, member, member, 0.0, ALU.add, ALU.bypass))
                V.tensor_copy(held, rank[:, TG - 1:TG]).then_inc(sem("held"), 1)
                dve.wait_ge(sem("held_sums"), i + 1)
                chain(V.tensor_scalar(before, bank(0, 1), first, -1.0, ALU.add, ALU.add))
                chain(V.tensor_scalar(full, bank(0, 1, 1), float(TILE - 1), None, ALU.add))
                chain(V.tensor_scalar(rank, rank, before, None, ALU.add))
                chain(V.tensor_tensor(rank, rank, member, ALU.mult))
                chain(V.tensor_tensor(place, place, rank, ALU.add))
                chain(V.tensor_copy(full_i, full))
                chain(V.tensor_scalar(full_i, full_i, 7, None, ALU.logical_shift_right))
                chain(V.tensor_scalar(full_i, full_i, 7, None, ALU.logical_shift_left))
                chain(V.tensor_copy(full, full_i))
                chain(V.tensor_tensor(first, first, full, ALU.add))
                chain(V.tensor_scalar(at_blk, at_blk, 1.0, None, ALU.add))
            chain(V.tensor_scalar(spare, pidx_f[:, 0:1], float(T_SORTED * TILE), None, ALU.add))
            chain(V.tensor_scalar(member, blk, float(FAR // WIN), spare, ALU.is_equal, ALU.mult))
            chain(V.tensor_tensor(place, place, member, ALU.add))
            V.tensor_copy(place_i, place).then_inc(sem("places"), 1)
            E = ordered
            for c in range(E.nc):
                dve.wait_ge(sem("dst_tr"), c + 1)
                V.tensor_copy(dst_tm[0:E.ch, c, :], bank(3 + c % 2, TILE)[0:E.ch, :])\
                    .then_inc(sem("dst_tr_ev"), 1)
            dve.wait_ge(sem("dst_tr_ev"), E.nc)
            dve_min_max(dve, chain, E)

        def pe_sort(pe):
            pe.wait_ge(sem("empty_ready"), 1)
            with pe.Fori(0, BLOCKS) as i:
                pe.wait_ge(sem("held"), i + 1)
                M(bank(0, 1), lower, held, start=True, stop=True, skip_group_check=True)
                M(bank(0, 1, 1), ones[:, :], held, start=True, stop=True, skip_group_check=True)\
                    .then_inc(sem("held_sums"), 1)
            with pe.Fori(0, T_SORTED // HALF) as i:
                pe.wait_ge(sem("rec_back"), i * 16 + 16)
                for k in range(HALF):
                    ins = nc.tensor.transpose(bank(1 + k // 4, TILE, (k % 4) * TILE)[0:FE, :],
                                              rec[:, k, 4:RECORD], ident[:, :])
                ins.then_inc(sem("attr_tr"), 1)
            for c in range(ordered.nc):
                pe.wait_ge(sem("dst_back"), 1)
                if c >= 2:
                    pe.wait_ge(sem("dst_tr_ev"), c - 1)
                nc.tensor.transpose(bank(3 + c % 2, TILE)[0:ordered.ch, :],
                                    dst_f[:, c * ordered.ch:(c + 1) * ordered.ch], ident[:, :])\
                    .then_inc(sem("dst_tr"), 1)

        def act_sort(act):
            act.wait_ge(sem("consts"), 8)
            act.wait_ge(sem("edges_in"), 64)
            act.wait_ge(sem("places"), 1)
            act.sem_inc(sem("rec_free"), 1)
            with act.Fori(0, T_GIVEN // HALF) as i:
                act.wait_ge(sem("rec_free"), i + 1)
                eight = bass.ds(i * HALF, HALF)
                A(place_st, place_i[:, eight], ACT.Copy).then_inc(sem("rec_cols"), 1)
                for f, of in enumerate((src_i, dst_i, rel_i)):
                    A(rec_i[:, :, f], of[:, eight], ACT.Copy).then_inc(sem("rec_cols"), 1)
                A(rec[:, :, 3], wgt[:, eight], ACT.Copy).then_inc(sem("rec_cols"), 1)
            with act.Fori(0, T_SORTED // HALF) as i:
                act.wait_ge(sem("rec_back"), i * 16 + 16)
                eight = bass.ds(i * HALF, HALF)
                for f, to in enumerate((src_i, dst_i, rel_i)):
                    A(to[:, eight], rec_i[:, :, f], ACT.Copy)
                A(dst_f[:, eight], rec_i[:, :, 1], ACT.Copy)
                A(wgt[:, eight], rec[:, :, 3], ACT.Copy)
                act.wait_ge(sem("attr_tr"), i + 1)
                act.wait_ge(sem("attr_stored"), i * 16 + 16)
                A(attr_s, ps[0:FE, BANK:3 * BANK], ACT.Copy).then_inc(sem("attr_back"), 1)
            act.wait_ge(sem("attr_back"), T_SORTED // HALF + 1)
            act.wait_ge(sem("attr_stored"), 16 * (T_SORTED // HALF + 1))
            act.sem_inc(sem("dst_back"), 1)

        def sp_sort(sp):
            sp.wait_ge(sem("empty_ready"), 1)
            with sp.Fori(0, T_SORTED // HALF + 1) as i:
                sp.dma_start(records[bass.ds(i * (HALF * TILE), HALF * TILE), :]
                             .rearrange("(k p) f -> p k f", p=TILE), empty).then_inc(sem("emptied"), 16)
            with sp.Fori(0, T_GIVEN // HALF) as i:
                sp.wait_ge(sem("rec_free"), i + 1)
                sp.dma_start(rec[:, :, 4:RECORD], I["attr_r"][bass.ds(i * (HALF * TILE), HALF * TILE), :]
                             .rearrange("(k p) f -> p k f", p=TILE)).then_inc(sem("rec_attr"), 16)
            sp.wait_ge(sem("rec_free"), T_GIVEN // HALF + 1)
            sp.sem_inc(sem("attr_back"), 1)
            sp.sem_inc(sem("attr_stored"), 16)
            with sp.Fori(0, T_SORTED // HALF) as i:
                at = sp.snap(i * (HALF * TILE), min_val=0, max_val=(T_SORTED - HALF) * TILE)
                sp.wait_ge(sem("attr_back"), i + 1)
                sp.dma_start(rec, records[bass.ds(at, HALF * TILE), :]
                             .rearrange("(k p) f -> p k f", p=TILE)).then_inc(sem("rec_back"), 16)
                sp.wait_ge(sem("attr_back"), i + 2)
                sp.sem_inc(sem("store_started"), 1)
                sp.dma_start(attr_sorted[:, bass.ds(at, HALF * TILE)], attr_s)\
                    .then_inc(sem("attr_stored"), 16)
            sp.wait_ge(sem("attr_stored"), 16 * (T_SORTED // HALF + 1))

        def pool_sort(pool):
            pool.wait_ge(sem("emptied"), 16 * (T_SORTED // HALF + 1))
            with pool.Fori(0, T_GIVEN // HALF) as i:
                pool.wait_ge(sem("rec_attr"), i * 16 + 16)
                pool.wait_ge(sem("rec_cols"), i * 5 + 5)
                pool.sem_inc(sem("gather_started"), 1)
                for k in range(HALF):
                    nc.gpsimd.indirect_dma_start(
                        out=records, out_offset=bass.IndirectOffsetOnAxis(ap=place_st[:, k:k + 1], axis=0),
                        in_=rec[:, k, :], in_offset=None).then_inc(sem("scattered_rec"), 16)
                pool.wait_ge(sem("scattered_rec"), i * (16 * HALF) + 16 * HALF)
                pool.sem_inc(sem("rec_free"), 1)

        def fits(eng):
            eng.wait_ge(sem("flag"), 1)
            return eng.value_load(flag[0:1, 0:1], min_val=0, max_val=1)

        def sp_passes(sp, E):
            sp_gin(sp, E)
            sp_edge(sp, E)
            sp_att_tables(sp, E)
            sp_signs(sp, E)
            sp_va(sp, E)
            sp_soft(sp, E)
            sp_rel(sp, E)
            sp_out(sp)

        def pool_passes(pool, E):
            pool_gin(pool, E)
            pool_edge(pool, E)
            pool_att_tables(pool, E)
            pool_gather(pool, E, 4, att_tab, ROW2)
            pool_va(pool, E)
            pool_rel(pool, E)

        def act_passes(act, E):
            act_gin(act, E)
            act_edge(act, E)
            act_att_tables(act, E)
            act_signs(act, Chain(act, sem("act")), E)
            act_va(act, E)
            act_soft(act, E)
            act_rel(act, E)

        def dve_passes(dve, chain, E):
            dve_edges(dve, chain, E)
            dve_gin(dve, chain, E)
            dve_edge(dve, chain, E)
            dve_att_tables(dve, chain, E)
            dve_signs(dve, chain, E)
            dve_va(dve, chain, E)
            dve_soft(dve, chain, E)
            dve_rel(dve, chain, E)

        def pe_passes(pe, E):
            pe_edges(pe, E)
            pe_gin(pe, E)
            pe_edge(pe, E)
            pe_att_tables(pe, E)
            pe_signs(pe, E)
            pe_va(pe, E)
            pe_soft(pe, E)
            pe_rel(pe, E)

        block = ctx.enter_context(nc.Block())

        @block.sync
        def _(sp):
            sp_start(sp)
            with sp.If(fits(sp)):
                sp_passes(sp, given)
            with sp.Else():
                sp_sort(sp)
                sp_passes(sp, ordered)

        @block.gpsimd
        def _(pool):
            pool_start(pool)
            with pool.If(fits(pool)):
                pool_passes(pool, given)
            with pool.Else():
                pool_sort(pool)
                pool_passes(pool, ordered)

        @block.scalar
        def _(act):
            with act.If(fits(act)):
                act_passes(act, given)
            with act.Else():
                act_sort(act)
                act_passes(act, ordered)

        @block.vector
        def _(dve):
            nonlocal dve_regs
            dve_regs = [dve.alloc_register(f"base{k}") for k in range(HALF)]
            chain = Chain(dve, sem("dve"))
            dve_start(dve, chain)
            steps = chain.n
            with dve.If(fits(dve)):
                dve_passes(dve, chain, given)
            with dve.Else():
                chain.n = steps
                dve_sort(dve, chain)
                dve_passes(dve, chain, ordered)

        @block.tensor
        def _(pe):
            nonlocal pe_regs
            pe_regs = [pe.alloc_register(f"window{k}") for k in range(HALF)]
            pe_start(pe)
            with pe.If(fits(pe)):
                pe_passes(pe, given)
            with pe.Else():
                pe_sort(pe)
                pe_passes(pe, ordered)


def lay_out(inputs):
    import numpy as np

    a = {k: np.asarray(v) for k, v in inputs.items()}
    pad = T_GIVEN * TILE - E_EDGES

    def tiled(v, fill):
        return np.ascontiguousarray(np.pad(v, (0, pad), constant_values=fill).reshape(T_GIVEN, TILE).T)

    dst = np.pad(a["dst"], (0, pad), constant_values=FAR).reshape(4, T_GIVEN // 4, TILE)
    prm = np.zeros((128, P_COLS), np.float32)
    for at, name in ((P_B1, "L0_gnn_b1"), (P_G1, "L0_gnn_g1"), (P_BE1, "L0_gnn_be1"), (P_B2, "L0_gnn_b2"),
                     (P_G2, "L0_gnn_g2"), (P_BE2, "L0_gnn_be2"), (P_BNG, "L0_gnn_bn_g"),
                     (P_BNB, "L0_gnn_bn_be")):
        prm[0:C, at:at + 3] = a[name].T
    prm[0:C, P_EPS:P_EPS + 3] = a["L0_gnn_eps"][None, :]
    prm[:, P_L1B3] = a["L1_gnn_b3"]
    for at, name in ((P_BL, "L2_gnn_bl"), (P_BD, "L2_gnn_bd"),
                     (P_GAMMA, "L3_gnn_gamma"), (P_BETA, "L3_gnn_beta")):
        prm[0:C, at] = a[name]
    prm[:, P_BA], prm[:, P_BF] = a["L2_gnn_ba"][0], a["L2_gnn_bf"][0]
    prm[0:C, P_WF:P_WF + 3] = a["L2_gnn_Wf"].reshape(3, C).T
    for k in range(HEADS):
        prm[k * HD:(k + 1) * HD, P_A1 + k] = a["L2_gnn_Wa"][0:HD, 0]
        prm[k * HD:(k + 1) * HD, P_A2 + k] = a["L2_gnn_Wa"][HD:2 * HD, 0]
    got = {
        "x": a["x"], "x_t": np.ascontiguousarray(a["x"].T), "params": prm,
        "src_e": tiled(a["src"], 0), "dst_e": tiled(a["dst"], FAR), "rel_e": tiled(a["edge_type_3"], 0),
        "wgt_e": tiled(a["edge_weight"], 0), "dst_t": np.ascontiguousarray(dst.transpose(1, 0, 2)),
        "attr_r": np.pad(a["edge_attr_32"], ((0, pad), (0, 0))),
        "attr_t": np.ascontiguousarray(np.pad(a["edge_attr_32"], ((0, pad), (0, 0))).T),
        "b1_row": a["L1_gnn_b1"][None, :],
        "brow": np.concatenate([a["L1_gnn_b2"], a["L1_gnn_b4"]])[None, :],
        "nought": np.zeros((WIN, WIN), np.float32),
    }
    for name in ("L0_gnn_W1", "L0_gnn_W2", "L1_gnn_W1", "L1_gnn_W2", "L1_gnn_W3", "L1_gnn_W4",
                 "L2_gnn_Wl", "L2_gnn_Wd", "L3_gnn_weight"):
        got[name] = a[name]
    return got


def kernel(**inputs):
    import numpy as np
    import concourse.bacc as bacc
    from concourse.bass_utils import run_bass_kernel_spmd

    arrays = {f"in_{k}": v for k, v in lay_out(inputs).items()}
    nc = bacc.Bacc("TRN2", target_bir_lowering=False, num_devices=1)
    args = {k[3:]: nc.dram_tensor(k, v.shape, mybir.dt.from_np(v.dtype), kind="ExternalInput").ap()
            for k, v in arrays.items()}
    out = nc.dram_tensor("out", [N, C], F32, kind="ExternalOutput").ap()
    build(nc, args, out)
    got = run_bass_kernel_spmd(nc, [arrays], core_ids=[0])
    return np.asarray(got.results[0]["out"])
```
